# Optimizing a Trainium2 kernel written in Bass

```python
import numpy as np
import jax
import jax.numpy as jnp

def _softmax(x, axis=-1):
    return jax.nn.softmax(x, axis=axis)

def _gelu(x):
    return jax.nn.gelu(x, approximate=True)

def _silu(x):
    return jax.nn.silu(x)

def _sigmoid(x):
    return jax.nn.sigmoid(x)

def _layernorm(x, axis=-1, eps=1e-05):
    m = jnp.mean(x, axis=axis, keepdims=True)
    v = jnp.var(x, axis=axis, keepdims=True)
    return (x - m) / jnp.sqrt(v + eps)

def _scatter_add(tgt, idx, src, axis=0):
    return tgt.at[idx].add(src)

def _segment_sum(src, seg, n):
    return jax.ops.segment_sum(src, seg, n)
kernel_name = 'mk_gnn_resnorm_d4_gnn_r64_ea1fb9'

def setup_inputs(seed: int=0):
    np.random.seed(seed)
    _w = jnp.asarray

    def _rec_inputs():
        import jax
        import jax.numpy as jnp
        _gk = jax.random.key(seed)
        x = -0.0003713 + 1 * jax.random.normal(jax.random.fold_in(_gk, 1), (100000, 128), jnp.float32)
        src = jax.random.randint(jax.random.fold_in(_gk, 2), (25000,), 0, 100000, jnp.int32)
        dst = jnp.minimum((100000 * jax.random.uniform(jax.random.fold_in(_gk, 3), (25000,)) ** 2.0).astype(jnp.int32), 99999)
        _o = jnp.argsort(dst, stable=True)
        src = src[_o]
        dst = dst[_o]
        edge_attr_128 = -4.21973e-05 + 0.999841 * jax.random.normal(jax.random.fold_in(_gk, 11), (25000, 128), jnp.float32)
        edge_weight = jax.random.uniform(jax.random.fold_in(_gk, 14), (25000,), jnp.float32, 0.0, 0.999998)
        return (x, src, dst, edge_attr_128, edge_weight)
    x, src, dst, edge_attr_128, edge_weight = _rec_inputs()

    def _L0_gnn_setup():
        import jax, jax.numpy as jnp
        import numpy as np
        N_NODES = 100000
        N_EDGES = 9375
        DIM = 128
        N_LAYERS = 2
        LN_EPS = 1e-05

        def _gnn_layer(x, row, col, edge_weight, gamma, beta):
            n = x.shape[0]
            ones_e = jnp.ones(row.shape[0], dtype=x.dtype)
            deg_row = jax.ops.segment_sum(ones_e, row, num_segments=n)
            deg_col = jax.ops.segment_sum(ones_e, col, num_segments=n)
            dri = jnp.where(deg_row > 0, deg_row ** (-0.5), 0.0)
            dci = jnp.where(deg_col > 0, deg_col ** (-0.5), 0.0)
            norm = dri[row] * dci[col] * edge_weight
            msgs = norm[:, None] * x[row]
            agg = jax.ops.segment_sum(msgs, col, num_segments=n)
            h = x + agg
            mean = jnp.mean(h, axis=-1, keepdims=True)
            var = jnp.mean((h - mean) ** 2, axis=-1, keepdims=True)
            h = (h - mean) * jax.lax.rsqrt(var + LN_EPS) * gamma + beta
            return jax.nn.elu(h)
        key = jax.random.key(seed)
        k1, k2, k3 = jax.random.split(key, 3)
        x = jax.random.normal(k1, (N_NODES, DIM), dtype=jnp.float32)
        edge_index = jax.random.randint(k2, (2, N_EDGES), 0, N_NODES, dtype=jnp.int64)
        edge_weight = jax.random.uniform(k3, (N_EDGES,), dtype=jnp.float32)
        ln_gamma = jnp.ones((N_LAYERS, DIM), dtype=jnp.float32)
        ln_beta = jnp.zeros((N_LAYERS, DIM), dtype=jnp.float32)
        return {'x': x, 'edge_index': edge_index, 'edge_weight': edge_weight, 'ln_gamma': ln_gamma, 'ln_beta': ln_beta}
    _L0_gnn_all = _L0_gnn_setup()
    _L0_gnn_in = {k: v for k, v in _L0_gnn_all.items() if k in ('ln_gamma', 'ln_beta')}
    del _L0_gnn_all

    def _L1_gnn_setup():
        import jax, jax.numpy as jnp
        import numpy as np
        N_NODES = 50000
        N_EDGES = 9375
        D_OBJ = 128
        D_REL = 128
        D_OUT = 128
        key = jax.random.key(seed)
        ks = jax.random.split(key, 7)
        s_obj = 1.0 / np.sqrt(D_OBJ)
        s_rel = 1.0 / np.sqrt(D_REL)
        return {'obj_vecs': jax.random.normal(ks[0], (N_NODES, D_OBJ), dtype=jnp.float32), 'rel_vecs': jax.random.normal(ks[1], (N_EDGES, D_REL), dtype=jnp.float32), 'edge_index': jax.random.randint(ks[2], (N_EDGES, 2), 0, N_NODES, dtype=jnp.int64), 'W_obj': jax.random.normal(ks[3], (D_OUT, D_OBJ), dtype=jnp.float32) * s_obj, 'b_obj': jax.random.normal(ks[4], (D_OUT,), dtype=jnp.float32) * s_obj, 'W_rel': jax.random.normal(ks[5], (D_OUT, D_REL), dtype=jnp.float32) * s_rel, 'b_rel': jax.random.normal(ks[6], (D_OUT,), dtype=jnp.float32) * s_rel}
    _L1_gnn_all = _L1_gnn_setup()
    _L1_gnn_in = {k: v for k, v in _L1_gnn_all.items() if k in ('W_obj', 'b_obj', 'W_rel', 'b_rel')}
    del _L1_gnn_all

    def _L2_gnn_setup():
        import jax, jax.numpy as jnp
        import numpy as np
        N_NODES = 10000
        N_EDGES = 10000
        D = 128

        def sage_layer(x, src, dst, W_self, W_neigh, b, num_nodes):
            msgs = x[src]
            agg = jax.ops.segment_sum(msgs, dst, num_segments=num_nodes)
            deg = jax.ops.segment_sum(jnp.ones((src.shape[0],), x.dtype), dst, num_segments=num_nodes)
            agg = agg / jnp.maximum(deg, 1.0)[:, None]
            return x @ W_self.T + agg @ W_neigh.T + b
        key = jax.random.key(seed)
        ks = jax.random.split(key, 8)
        s = 1.0 / np.sqrt(D)
        return {'x': jax.random.normal(ks[0], (N_NODES, D), dtype=jnp.float32), 'edge_index': jax.random.randint(ks[1], (2, N_EDGES), 0, N_NODES, dtype=jnp.int64), 'W1_self': jax.random.normal(ks[2], (D, D), dtype=jnp.float32) * s, 'W1_neigh': jax.random.normal(ks[3], (D, D), dtype=jnp.float32) * s, 'b1': jnp.zeros((D,), dtype=jnp.float32), 'W2_self': jax.random.normal(ks[4], (D, D), dtype=jnp.float32) * s, 'W2_neigh': jax.random.normal(ks[5], (D, D), dtype=jnp.float32) * s, 'b2': jnp.zeros((D,), dtype=jnp.float32)}
    _L2_gnn_all = _L2_gnn_setup()
    _L2_gnn_in = {k: v for k, v in _L2_gnn_all.items() if k in ('W1_self', 'W1_neigh', 'b1', 'W2_self', 'W2_neigh', 'b2')}
    del _L2_gnn_all

    def _L3_gnn_setup():
        import jax, jax.numpy as jnp
        import numpy as np
        NUM_NODES = 100000
        NUM_EDGES = 10000
        D_FEAT = 128
        key = jax.random.key(seed)
        k1, k2 = jax.random.split(key)
        embeddings = jax.random.normal(k1, (NUM_NODES, D_FEAT), dtype=jnp.float32)
        edge_index = jax.random.randint(k2, (2, NUM_EDGES), 0, NUM_NODES, dtype=jnp.int64)
        return {'embeddings': embeddings, 'edge_index': edge_index}
    _L3_gnn_all = _L3_gnn_setup()
    _L3_gnn_in = {k: v for k, v in _L3_gnn_all.items() if k in ()}
    del _L3_gnn_all
    return {'x': x, 'src': src, 'dst': dst, 'edge_attr_128': edge_attr_128, 'edge_weight': edge_weight, 'L0_gnn_ln_gamma': _L0_gnn_in['ln_gamma'], 'L0_gnn_ln_beta': _L0_gnn_in['ln_beta'], 'L1_gnn_W_obj': _L1_gnn_in['W_obj'], 'L1_gnn_b_obj': _L1_gnn_in['b_obj'], 'L1_gnn_W_rel': _L1_gnn_in['W_rel'], 'L1_gnn_b_rel': _L1_gnn_in['b_rel'], 'L2_gnn_W1_self': _L2_gnn_in['W1_self'], 'L2_gnn_W1_neigh': _L2_gnn_in['W1_neigh'], 'L2_gnn_b1': _L2_gnn_in['b1'], 'L2_gnn_W2_self': _L2_gnn_in['W2_self'], 'L2_gnn_W2_neigh': _L2_gnn_in['W2_neigh'], 'L2_gnn_b2': _L2_gnn_in['b2']}

def reference(x, src, dst, edge_attr_128, edge_weight, L0_gnn_ln_gamma, L0_gnn_ln_beta, L1_gnn_W_obj, L1_gnn_b_obj, L1_gnn_W_rel, L1_gnn_b_rel, L2_gnn_W1_self, L2_gnn_W1_neigh, L2_gnn_b1, L2_gnn_W2_self, L2_gnn_W2_neigh, L2_gnn_b2):
    import jax
    import jax.numpy as jnp

    def _L0_gnn_ref(x, edge_index, edge_weight, ln_gamma, ln_beta):
        import jax, jax.numpy as jnp
        import numpy as np
        N_NODES = 100000
        N_EDGES = 9375
        DIM = 128
        N_LAYERS = 2
        LN_EPS = 1e-05

        def _gnn_layer(x, row, col, edge_weight, gamma, beta):
            n = x.shape[0]
            ones_e = jnp.ones(row.shape[0], dtype=x.dtype)
            deg_row = jax.ops.segment_sum(ones_e, row, num_segments=n)
            deg_col = jax.ops.segment_sum(ones_e, col, num_segments=n)
            dri = jnp.where(deg_row > 0, deg_row ** (-0.5), 0.0)
            dci = jnp.where(deg_col > 0, deg_col ** (-0.5), 0.0)
            norm = dri[row] * dci[col] * edge_weight
            msgs = norm[:, None] * x[row]
            agg = jax.ops.segment_sum(msgs, col, num_segments=n)
            h = x + agg
            mean = jnp.mean(h, axis=-1, keepdims=True)
            var = jnp.mean((h - mean) ** 2, axis=-1, keepdims=True)
            h = (h - mean) * jax.lax.rsqrt(var + LN_EPS) * gamma + beta
            return jax.nn.elu(h)
        row, col = (edge_index[0], edge_index[1])
        for l in range(N_LAYERS):
            x = _gnn_layer(x, row, col, edge_weight, ln_gamma[l], ln_beta[l])
        return x

    def _L1_gnn_ref(obj_vecs, rel_vecs, edge_index, W_obj, b_obj, W_rel, b_rel):
        import jax, jax.numpy as jnp
        import numpy as np
        N_NODES = 50000
        N_EDGES = 9375
        D_OBJ = 128
        D_REL = 128
        D_OUT = 128
        obj_lin = obj_vecs @ W_obj.T + b_obj
        rel_lin = rel_vecs @ W_rel.T + b_rel
        src = edge_index[:, 0]
        dst = edge_index[:, 1]
        msg = jax.nn.relu(obj_lin[src] + rel_lin + obj_lin[dst])
        aggr = jax.ops.segment_sum(msg, dst, num_segments=obj_vecs.shape[0])
        return jax.nn.relu(aggr)

    def _L2_gnn_ref(x, edge_index, W1_self, W1_neigh, b1, W2_self, W2_neigh, b2):
        import jax, jax.numpy as jnp
        import numpy as np
        N_NODES = 10000
        N_EDGES = 10000
        D = 128

        def sage_layer(x, src, dst, W_self, W_neigh, b, num_nodes):
            msgs = x[src]
            agg = jax.ops.segment_sum(msgs, dst, num_segments=num_nodes)
            deg = jax.ops.segment_sum(jnp.ones((src.shape[0],), x.dtype), dst, num_segments=num_nodes)
            agg = agg / jnp.maximum(deg, 1.0)[:, None]
            return x @ W_self.T + agg @ W_neigh.T + b
        src, dst = (edge_index[0], edge_index[1])
        n = x.shape[0]
        h = sage_layer(x, src, dst, W1_self, W1_neigh, b1, n)
        h = jax.nn.relu(h)
        out = sage_layer(h, src, dst, W2_self, W2_neigh, b2, n)
        return out

    def _L3_gnn_ref(embeddings, edge_index):
        import jax, jax.numpy as jnp
        import numpy as np
        NUM_NODES = 100000
        NUM_EDGES = 10000
        D_FEAT = 128
        'LightGCN propagation: out[v] = sum_{(u,v) in E} e[u] / (sqrt(deg(u)) * sqrt(deg(v)))\n            where deg is the out-degree computed from the row (source) indices.'
        num_nodes = embeddings.shape[0]
        row, col = (edge_index[0], edge_index[1])
        deg = jax.ops.segment_sum(jnp.ones_like(row, dtype=embeddings.dtype), row, num_segments=num_nodes)
        deg = jnp.maximum(deg, 1.0)
        deg_inv_sqrt = deg ** (-0.5)
        norm = deg_inv_sqrt[row] * deg_inv_sqrt[col]
        msgs = embeddings[row] * norm[:, None]
        out = jax.ops.segment_sum(msgs, col, num_segments=num_nodes)
        return out
    edge_index = jnp.stack([src, dst])
    edge_index_t = jnp.stack([src, dst], axis=1)
    x = _layernorm(x + _L0_gnn_ref(x, edge_index, edge_weight, L0_gnn_ln_gamma, L0_gnn_ln_beta), axis=-1)
    x = _layernorm(x + _L1_gnn_ref(x, edge_attr_128, edge_index_t, L1_gnn_W_obj, L1_gnn_b_obj, L1_gnn_W_rel, L1_gnn_b_rel), axis=-1)
    x = _layernorm(x + _L2_gnn_ref(x, edge_index, L2_gnn_W1_self, L2_gnn_W1_neigh, L2_gnn_b1, L2_gnn_W2_self, L2_gnn_W2_neigh, L2_gnn_b2), axis=-1)
    x = _layernorm(x + _L3_gnn_ref(x, edge_index), axis=-1)
    return x

_drawn_inputs = setup_inputs


def setup_inputs(seed=0):
    import zlib

    import numpy as np

    out = dict(_drawn_inputs(seed))
    spreads = {'L0_gnn_ln_gamma': (1.0, 0.2),
     'L0_gnn_ln_beta': (0.0, 0.1),
     'L2_gnn_b1': (0.0, 0.1),
     'L2_gnn_b2': (0.0, 0.1)}
    factors = {'L1_gnn_b_rel': 4.339}
    for name, (base, spread) in spreads.items():
        noise = np.random.default_rng([zlib.crc32(name.encode()), seed]).standard_normal(out[name].shape)
        drawn = base * np.exp(spread * noise) if base else spread * noise
        out[name] = jnp.asarray(drawn.astype(out[name].dtype))
    for name, factor in factors.items():
        out[name] = (out[name] * factor).astype(out[name].dtype)
    return out
```

```python
from contextlib import ExitStack

import concourse.bass as bass
from concourse import mybir

ALU = mybir.AluOpType
ACT = mybir.ActivationFunctionType
F32 = mybir.dt.float32
F16 = mybir.dt.float16
I32 = mybir.dt.int32
AX_X = mybir.AxisListType.X

P = 128
EPS = 1e-5
DS = 3
DG = 8
DROWS = DS * DG * P
US = 4
G = 7
GW = G * P
LO = 256
NBUF = 6


def phase_semaphores(nc, ctx, suffix):
    used = []

    def sem(name):
        used.append(nc.alloc_semaphore(name + suffix))
        return used[-1]

    def clear():
        nc.clear_and_free_semaphores(used)
        nc.all_engine_barrier()

    ctx.callback(clear)
    return sem


def gnn_kernel(nc, x, src, dst, edge_attr, edge_weight, ln_gamma, ln_beta, W_obj, b_obj, W_rel,
               b_rel, W1_self, W1_neigh, b1, W2_self, W2_neigh, b2, out):
    N = x.shape[0]
    E = src.shape[0]
    ET = -(-E // P)
    EP = ET * P
    HB = ET // 2
    NG = ET // G
    HI = -(-(N + 1) // (LO * 4)) * 4
    HP = HI // 4
    PAD = HI * LO - 1
    TAIL = E - (ET - 1) * P
    assert ET % (2 * G) == 0 and NG % US == 0 and PAD >= N and HP <= P and x.shape[1] == P

    with ExitStack() as root:
        root.enter_context(nc.allow_non_contiguous_dma(reason="small columns and edge id blocks"))

        def sb(name, shape, dt=F32):
            return root.enter_context(nc.sbuf_tensor(name, shape, dt))

        def dram(name, shape, dt=F32):
            return nc.dram_tensor(name, shape, dt).ap()

        level_rows = [None] + [dram(f"level{l}", (2 * EP, P)) for l in range(1, 6)]
        src_x = dram("src_x", (EP, P))
        dst_x = dram("dst_x", (EP, P))
        agg_dram = dram("agg", (EP, P))
        match_dram = dram("match", (NG, P, GW))
        dst_flat = dram("dst_flat", (1, EP))
        ends_dram = dram("ends", (1, 2 * ET))
        ends_mask = dram("ends_mask", (2, EP))
        carry_dram = dram("carry", (2, EP))
        node_dram = dram("node", (HI * LO, 4))

        ident = sb("ident", [P, P])
        center = sb("center", [P, P])
        ones_row = sb("ones_row", [1, P])
        upper = sb("upper", [P, P])
        ones_sq = sb("ones_sq", [P, P])
        eps_t = sb("eps_t", [P, 2])
        w_raw = sb("w_raw", [P, 6, P])
        w_use = sb("w_use", [P, 6, P])
        cols = sb("cols", [P, 8])
        bias_row = sb("bias_row", [1, 3, P])
        edge_bias = sb("edge_bias", [1, P])
        ids_i = sb("ids_i", [HB, 2, 2, P], I32)
        ids_f = sb("ids_f", [HB, 2, 2, P])
        w_tb = sb("w_tb", [HB, 2, P])
        mask_tb = sb("mask_tb", [HB, 2, 2, P])
        ends_b = sb("ends_b", [HB, 2, ET])
        reach = sb("reach", [HB, 2, 2, ET])
        srcP = sb("srcP", [P, ET])
        dstP = sb("dstP", [P, ET])
        wP = sb("wP", [P, ET])
        hilo_i = sb("hilo_i", [P, 4, ET], I32)
        hilo = sb("hilo", [P, 4, ET])
        idx_src = sb("idx_src", [P, ET], I32)
        idx_dst = sb("idx_dst", [P, ET], I32)
        idx_srcn = sb("idx_srcn", [P, ET], I32)
        idx_dstn = sb("idx_dstn", [P, ET], I32)
        idx_lvl = sb("idx_lvl", [P, ET], I32)
        idx_out = sb("idx_out", [P, ET], I32)
        iota_i = sb("iota_i", [P, HI], I32)
        iota_h = sb("iota_h", [P, HI], F16)
        edge_no = sb("edge_no", [P, ET])
        edge_no_i = sb("edge_no_i", [P, ET], I32)
        info = sb("info", [P, 2, ET, 4])
        w_gcn = sb("w_gcn", [P, ET])
        w_mean = sb("w_mean", [P, ET])
        w_light = sb("w_light", [P, ET])
        tmp = sb("tmp", [P, 3, ET])
        small = sb("small", [P, US, 4, DG])
        ring_idx = sb("ring_idx", [P, 2, G], I32)
        buf = [sb(f"buf{j}", [P, NBUF, DG * P]) for j in range(US)]
        extra = sb("extra", [P, 2 * US, GW])
        carry_in = [extra[0:2, 2 * j:2 * j + 2, :] for j in range(US)]
        psum = root.enter_context(nc.psum_tensor("psum", [P, US, DG * P], F32))

        def tiles(ap, g=DG):
            return ap[:, 0:g * P].rearrange("p (k d) -> p k d", d=P)

        def edge_rows(ap, g):
            return ap[bass.ds(g * GW, GW), :].rearrange("(k p) d -> p k d", p=P)

        with ExitStack() as ctx:
            sem = phase_semaphores(nc, ctx, "")

            w_in, col_in, ids_in = sem("w_in"), sem("col_in"), sem("ids_in")
            filled, pool_done = sem("filled"), sem("pool_done")
            pe_done, act_done, dve_done = sem("pe_done"), sem("act_done"), sem("dve_done")
            ends_out, ends_in, tb_out = sem("ends_out"), sem("ends_in"), sem("tb_out")
            FULL = ET - 1 - HB
            block = ctx.enter_context(nc.Block())

            @block.sync
            def _(sp):
                sp.wait_ge(filled, 3)
                for a, s in enumerate((src, dst)):
                    sp.dma_start(ids_i[:, a, 0, :], s[0:HB * P].rearrange("(t p) -> t p", p=P)).then_inc(ids_in, 16)
                    sp.dma_start(ids_i[0:FULL, a, 1, :],
                                 s[HB * P:(ET - 1) * P].rearrange("(t p) -> t p", p=P)).then_inc(ids_in, 16)
                    sp.dma_start(ids_i[FULL:HB, a, 1, 0:TAIL],
                                 s[(ET - 1) * P:E].rearrange("(t p) -> t p", t=1)).then_inc(ids_in, 16)
                ew = edge_weight
                sp.dma_start(w_tb[:, 0, :], ew[0:HB * P].rearrange("(t p) -> t p", p=P)).then_inc(ids_in, 16)
                sp.dma_start(w_tb[0:FULL, 1, :],
                             ew[HB * P:(ET - 1) * P].rearrange("(t p) -> t p", p=P)).then_inc(ids_in, 16)
                sp.dma_start(w_tb[FULL:HB, 1, 0:TAIL],
                             ew[(ET - 1) * P:E].rearrange("(t p) -> t p", t=1)).then_inc(ids_in, 16)
                for k, w in enumerate((W_obj, W_rel, W1_self, W1_neigh, W2_self, W2_neigh)):
                    sp.dma_start(w_raw[:, k, :], w).then_inc(w_in, 16)
                sp.dma_start(cols[:, 0:2], ln_gamma.rearrange("l d -> d l")).then_inc(col_in, 16)
                sp.dma_start(cols[:, 2:4], ln_beta.rearrange("l d -> d l")).then_inc(col_in, 16)
                sp.dma_start(cols[:, 4:5], b1.rearrange("(d a) -> d a", a=1)).then_inc(col_in, 16)
                sp.dma_start(cols[:, 5:6], b2.rearrange("(d a) -> d a", a=1)).then_inc(col_in, 16)
                sp.dma_start(bias_row[:, 0, :], b_obj.rearrange("(a d) -> a d", a=1)).then_inc(col_in, 16)
                sp.dma_start(bias_row[:, 1, :], b_rel.rearrange("(a d) -> a d", a=1)).then_inc(col_in, 16)
                sp.wait_ge(dve_done, 4)
                for b in range(2):
                    sp.dma_start(dst_flat[0:1, b * HB * P:(b + 1) * HB * P].rearrange("a (t p) -> (a t) p", p=P),
                                 ids_f[:, 1, b, :]).then_inc(tb_out, 16)
                    for side, at in enumerate((0, P - 1)):
                        lo = side * ET + b * HB
                        sp.dma_start(ends_dram[0:1, lo:lo + HB].rearrange("a (t o) -> (a t) o", o=1),
                                     ids_f[:, 1, b, at:at + 1]).then_inc(ends_out, 16)
                sp.wait_ge(ends_out, 64)
                sp.dma_start(ends_b.rearrange("t s n -> t (s n)"),
                             ends_dram.to_broadcast([HB, 2 * ET])).then_inc(ends_in, 16)
                sp.wait_ge(dve_done, 8)
                for side in range(2):
                    for b in range(2):
                        sp.dma_start(
                            ends_mask[side:side + 1, b * HB * P:(b + 1) * HB * P].rearrange("a (t p) -> (a t) p", p=P),
                            mask_tb[:, side, b, :]).then_inc(tb_out, 16)
                sp.wait_ge(tb_out, 96)

            @block.gpsimd
            def _(pool):
                pool.iota(ids_i[:, :, :, :], [[0, 2 * 2 * P]], base=PAD, channel_multiplier=0).then_inc(filled, 1)
                pool.memset(w_tb[:, :, :], 0.0).then_inc(filled, 1)
                pool.memset(ones_row[:, :], 1.0).then_inc(filled, 1)
                pool.memset(ones_sq[:, :], 1.0).then_inc(pool_done, 1)
                pool.memset(ident[:, :], 0.0).then_inc(pool_done, 1)
                pool.wait_ge(pool_done, 2)
                pool.affine_select(out=ident[:, :], in_=ident[:, :], compare_op=ALU.not_equal, fill=1.0, base=0,
                                   pattern=[[-1, P]], channel_multiplier=1).then_inc(pool_done, 1)
                pool.affine_select(out=upper[:, :], in_=ones_sq[:, :], compare_op=ALU.is_gt, fill=0.0, base=0,
                                   pattern=[[1, P]], channel_multiplier=-1).then_inc(pool_done, 1)
                pool.iota(iota_i[:, :], [[1, HI]], base=0, channel_multiplier=0).then_inc(pool_done, 1)
                pool.iota(edge_no_i[:, :], [[P, ET]], base=0, channel_multiplier=1).then_inc(pool_done, 1)
                pool.memset(eps_t[:, 0:1], EPS).then_inc(pool_done, 1)
                pool.memset(eps_t[:, 1:2], EPS * EPS).then_inc(pool_done, 1)
                pool.wait_ge(dve_done, 12)
                for b in range(2):
                    pool.affine_select(out=reach[:, 0, b, :], in_=reach[:, 0, b, :], compare_op=ALU.is_gt, fill=0.0,
                                       base=-b * HB, pattern=[[1, ET]], channel_multiplier=-1).then_inc(pool_done, 1)
                    pool.affine_select(out=reach[:, 1, b, :], in_=reach[:, 1, b, :], compare_op=ALU.is_gt, fill=0.0,
                                       base=b * HB, pattern=[[-1, ET]], channel_multiplier=1).then_inc(pool_done, 1)

            @block.tensor
            def _(pe):
                pe.wait_ge(pool_done, 3)
                pe.wait_ge(w_in, 96)
                for k in range(4):
                    pe.transpose(psum[:, 0, k * P:(k + 1) * P], w_raw[:, k, :], ident[:, :])
                pe.wait_ge(dve_done, 5)
                for k in range(4, 6):
                    pe.matmul(psum[:, 0, k * P:(k + 1) * P], w_raw[:, k, :], center[:, :], start=True, stop=True)
                pe.wait_ge(col_in, 96)
                pe.matmul(psum[0:1, 1, 0:P], cols[:, 5:6], center[:, :], start=True, stop=True).then_inc(pe_done, 1)
                for b in range(2):
                    pe.transpose(psum[:, 2, b * HB:(b + 1) * HB], ids_f[:, 0, b, :], ident[0:HB, 0:HB])
                for b in range(2):
                    pe.transpose(psum[:, 2, 512 + b * HB:512 + (b + 1) * HB], ids_f[:, 1, b, :], ident[0:HB, 0:HB])
                for b in range(2):
                    mm = pe.transpose(psum[:, 3, b * HB:(b + 1) * HB], w_tb[:, b, :], ident[0:HB, 0:HB])
                mm.then_inc(pe_done, 1)

            @block.scalar
            def _(act):
                act.wait_ge(pe_done, 1)
                act.copy(w_use.rearrange("p k d -> p (k d)"), psum[:, 0, 0:6 * P]).then_inc(act_done, 1)
                act.copy(bias_row[:, 2, :], psum[0:1, 1, 0:P]).then_inc(act_done, 1)

            @block.vector
            def _(dve):
                dve.wait_ge(ids_in, 144)
                for a in range(2):
                    for b in range(2):
                        dve.tensor_copy(ids_f[:, a, b, :], ids_i[:, a, b, :]).then_inc(dve_done, 1)
                dve.wait_ge(pool_done, 3)
                dve.tensor_scalar(center[:, :], ident[:, :], 1.0 / P, None, ALU.subtract).then_inc(dve_done, 1)
                dve.wait_ge(dve_done, 4)
                for b in range(2):
                    for side, at in enumerate((0, P - 1)):
                        ins = dve.tensor_scalar(mask_tb[:, side, b, :], ids_f[:, 1, b, :],
                                                ids_f[:, 1, b, at:at + 1], None, ALU.is_equal)
                        if (b, side) != (0, 0):
                            ins.then_inc(dve_done, 1)
                dve.wait_ge(ends_in, 16)
                for b in range(2):
                    for side, at in enumerate((P - 1, 0)):
                        dve.tensor_scalar(reach[:, side, b, :], ends_b[:, side, :], ids_f[:, 1, b, at:at + 1],
                                          None, ALU.is_equal).then_inc(dve_done, 1)
                dve.wait_ge(pool_done, 8)
                dve.tensor_copy(iota_h[:, :], iota_i[:, :]).then_inc(dve_done, 1)
                dve.tensor_copy(edge_no[:, :], edge_no_i[:, :]).then_inc(dve_done, 1)
                dve.wait_ge(col_in, 96)
                dve.scalar_tensor_tensor(out=edge_bias[:, :], in0=bias_row[:, 0, :], scalar=2.0, in1=bias_row[:, 1, :],
                                         op0=ALU.mult, op1=ALU.add).then_inc(dve_done, 1)
                dve.wait_ge(pe_done, 2)
                dve.tensor_copy(srcP[:, :], psum[:, 2, 0:ET]).then_inc(dve_done, 1)
                dve.tensor_copy(dstP[:, :], psum[:, 2, 512:512 + ET]).then_inc(dve_done, 1)
                dve.tensor_copy(wP[:, :], psum[:, 3, 0:ET]).then_inc(dve_done, 1)
                dve.wait_ge(dve_done, 18)
                dve.tensor_copy(idx_srcn[:, :], srcP[:, :]).then_inc(dve_done, 1)
                dve.tensor_copy(idx_dstn[:, :], dstP[:, :]).then_inc(dve_done, 1)
                dve.tensor_scalar(idx_src[:, :], srcP[:, :], float(N - 1), None, ALU.min).then_inc(dve_done, 1)
                dve.tensor_scalar(idx_dst[:, :], dstP[:, :], float(N - 1), None, ALU.min).then_inc(dve_done, 1)
                dve.wait_ge(dve_done, 20)
                for a, ids in enumerate((idx_srcn, idx_dstn)):
                    dve.tensor_scalar(hilo_i[:, 2 * a, :], ids[:, :], LO.bit_length() - 1, None,
                                      ALU.logical_shift_right).then_inc(dve_done, 1)
                    dve.tensor_scalar(hilo_i[:, 2 * a + 1, :], ids[:, :], LO - 1, None,
                                      ALU.bitwise_and).then_inc(dve_done, 1)
                dve.wait_ge(dve_done, 26)
                dve.tensor_copy(hilo.rearrange("p a t -> p (a t)"),
                                hilo_i.rearrange("p a t -> p (a t)")).then_inc(dve_done, 1)

        DENSE_IT = -(-N // DROWS)
        SRC_IT = -(-EP // DROWS)
        with ExitStack() as ctx:
            sem = phase_semaphores(nc, ctx, "")

            HR = 4
            onehot = ctx.enter_context(nc.sbuf_tensor("onehot", [P, HR, HI + LO], F16))
            node = buf[3][0:HP, 0:4, :].rearrange("p b (l f) -> p b l f", f=4)
            incl = buf[3][0:HP, 4, :].rearrange("p (b l) -> p b l", b=4)
            tot = ctx.enter_context(nc.sbuf_tensor("tot", [HP, 8], F32))
            ring_info = ctx.enter_context(nc.sbuf_tensor("ring_info", [P, 2, G, 4], F32))
            hot_ready, hot_used = sem("hot_ready"), sem("hot_used")
            counted, tab_dve, tab_pe, node_out = sem("counted"), sem("tab_dve"), sem("tab_pe"), sem("node_out")
            dstrow_in, match_ready = [sem(f"dstrow_in{p}") for p in range(2)], sem("match_ready")
            match_out = [sem(f"match_out{p}") for p in range(2)]
            idx_copied, ring_free = sem("idx_copied"), sem("ring_free")
            rows_in = [sem(f"rows_in{p}") for p in range(2)]
            rows_out = [sem(f"rows_out{p}") for p in range(2)]
            src_all = sem("src_all")
            info_in = [sem(f"info_in{p}") for p in range(2)]
            info_copied = sem("info_copied")
            x_in = [sem(f"x_in{j}") for j in range(DS)]
            pe_step = [sem(f"pe_step{j}") for j in range(DS)]
            act_step = [sem(f"act_step{j}") for j in range(DS)]
            dve_step = [sem(f"dve_step{j}") for j in range(DS)]
            out_stored = [sem(f"out_stored{j}") for j in range(DS)]
            s_in = [sem(f"s_in{j}") for j in range(DS)]
            s_pe = [sem(f"s_pe{j}") for j in range(DS)]
            s_act = [sem(f"s_act{j}") for j in range(DS)]
            s_dve = [sem(f"s_dve{j}") for j in range(DS)]
            y1_out = [sem(f"y1_out{j}") for j in range(DS)]
            x1_out = [sem(f"x1_out{j}") for j in range(DS)]
            x2_out = [sem(f"x2_out{j}") for j in range(DS)]
            h1_out = [sem(f"h1_out{j}") for j in range(DS)]
            x3_out = [sem(f"x3_out{j}") for j in range(DS)]
            block = ctx.enter_context(nc.Block())

            DPE, DACT, DDVE = 9, 19, 12
            SPE, SACT, SDVE = 11, 23, 13
            gamma = lambda l: cols[:, l:l + 1]
            beta = lambda l: cols[:, 2 + l:3 + l]

            def B(j, k):
                return buf[j][:, k, :]

            def ps(j):
                return psum[:, j, :]

            def dense_rows(ap, i, j, base, last, total):
                lo = (total - DROWS + j * DG * P) if last else i * DROWS + j * DG * P + base
                return ap[bass.ds(lo, DG * P), :].rearrange("(p k) d -> p (k d)", p=P)

            def src_rows(l, i, j, last):
                lo = EP + (EP - DROWS + j * DG * P if last else i * DROWS + j * DG * P)
                return level_rows[l][bass.ds(lo, DG * P), :].rearrange("(p k) d -> p (k d)", p=P)

            @block.sync
            def _(sp):
                def load_dst(g, p):
                    sp.dma_start(extra[:, p, :], dst_flat[0:1, bass.ds(g * GW, GW)].to_broadcast([P, GW])
                                 ).then_inc(dstrow_in[p], 16)

                def store_match(g, p):
                    sp.dma_start(match_dram[bass.ds(g, 1)].rearrange("a p w -> (a p) w"), extra[:, 2 + p, :]
                                 ).then_inc(match_out[p], 16)

                for p in range(2):
                    load_dst(p, p)
                with sp.Fori(0, NG // 2 - 1) as i:
                    for p in range(2):
                        sp.wait_ge(match_ready, 2 * i + p + 1)
                        store_match(2 * i + p, p)
                        load_dst(2 * i + 2 + p, p)
                for p in range(2):
                    sp.wait_ge(match_ready, NG - 1 + p)
                    store_match(NG - 2 + p, p)
                sp.wait_ge(tab_dve, 17)
                sp.dma_start(node_dram.rearrange("(b p l) f -> p b (l f)", p=HP, l=LO),
                             node.rearrange("p b l f -> p b (l f)")).then_inc(node_out, 16)

                def load_x(i, j, last):
                    sp.dma_start(B(j, 0), dense_rows(x, i, j, 0, last, N)).then_inc(x_in[j], 16)

                def store_out(i, j, last):
                    sp.wait_ge(dve_step[j], DDVE * i + DDVE)
                    if last:
                        for k in range(DS):
                            sp.wait_ge(out_stored[k], 16 * i)
                    sp.dma_start(dense_rows(out, i, j, 0, last, N), B(j, 5)).then_inc(out_stored[j], 16)

                for j in range(DS):
                    load_x(0, j, False)
                with sp.Fori(0, DENSE_IT - 2) as i:
                    for j in range(DS):
                        sp.wait_ge(pe_step[j], DPE * i + 1)
                        load_x(i + 1, j, False)
                    for j in range(DS):
                        store_out(i, j, False)
                i = DENSE_IT - 2
                for j in range(DS):
                    sp.wait_ge(pe_step[j], DPE * i + 1)
                    load_x(i + 1, j, True)
                for j in range(DS):
                    store_out(i, j, False)
                for j in range(DS):
                    store_out(i + 1, j, True)

                sp.wait_ge(src_all, 1)

                def load_s(i, j, last):
                    sp.dma_start(B(j, 0), dense_rows(src_x, i, j, 0, last, EP)).then_inc(s_in[j], 16)

                def store_s(i, last):
                    if last:
                        for j in range(DS):
                            for s in (y1_out, x1_out, x2_out, h1_out, x3_out):
                                sp.wait_ge(s[j], 16 * i)
                    for j in range(DS):
                        sp.wait_ge(s_act[j], SACT * i + 7)
                        sp.dma_start(src_rows(1, i, j, last), B(j, 5)).then_inc(y1_out[j], 16)
                    for j in range(DS):
                        sp.wait_ge(s_dve[j], SDVE * i + 11)
                        sp.dma_start(src_rows(2, i, j, last), B(j, 2)).then_inc(x1_out[j], 16)
                        sp.dma_start(src_rows(3, i, j, last), B(j, 3)).then_inc(x2_out[j], 16)
                    for j in range(DS):
                        sp.wait_ge(s_act[j], SACT * i + 20)
                        sp.dma_start(src_rows(4, i, j, last), B(j, 5)).then_inc(h1_out[j], 16)
                    for j in range(DS):
                        sp.wait_ge(s_dve[j], SDVE * i + 13)
                        sp.dma_start(src_rows(5, i, j, last), B(j, 4)).then_inc(x3_out[j], 16)

                for j in range(DS):
                    sp.wait_ge(pe_step[j], DPE * DENSE_IT)
                    load_s(0, j, False)
                with sp.Fori(0, SRC_IT - 2) as i:
                    for j in range(DS):
                        sp.wait_ge(s_pe[j], SPE * i + 1)
                        load_s(i + 1, j, False)
                    store_s(i, False)
                i = SRC_IT - 2
                for j in range(DS):
                    sp.wait_ge(s_pe[j], SPE * i + 1)
                    load_s(i + 1, j, True)
                store_s(i, False)
                store_s(i + 1, True)
                for j in range(DS):
                    sp.wait_ge(out_stored[j], 16 * DENSE_IT)
                    for s in (y1_out, x1_out, x2_out, h1_out, x3_out):
                        sp.wait_ge(s[j], 16 * SRC_IT)
                for p in range(2):
                    sp.wait_ge(match_out[p], 8 * NG)

            @block.gpsimd
            def _(pool):
                for a, (ids, table) in enumerate(((idx_src, src_x), (idx_dst, dst_x))):
                    with pool.Fori(0, NG // 2) as i:
                        for p in range(2):
                            n = a * (NG // 2) + i
                            pool.tensor_copy(ring_idx[:, p, :], ids[:, bass.ds((2 * i + p) * G, G)]
                                             ).then_inc(idx_copied, 1)
                            pool.wait_ge(idx_copied, 2 * n + p + 1)
                            pool.wait_ge(rows_out[p], 16 * n)
                            pool.sem_inc(ring_free, 1)
                            for k in range(G):
                                pool.indirect_dma_start(
                                    out=extra[:, 4 + p, k * P:(k + 1) * P], out_offset=None, in_=x,
                                    in_offset=bass.IndirectOffsetOnAxis(ap=ring_idx[:, p, k:k + 1], axis=0),
                                ).then_inc(rows_in[p], 16)
                        for p in range(2):
                            n = a * (NG // 2) + i
                            pool.wait_ge(rows_in[p], 16 * G * n + 16 * G)
                            pool.dma_start(edge_rows(table, 2 * i + p),
                                           extra[:, 4 + p, :].rearrange("p (k d) -> p k d", d=P)
                                           ).then_inc(rows_out[p], 16)
                    for p in range(2):
                        pool.wait_ge(rows_out[p], 8 * NG * (a + 1))
                    if a == 0:
                        pool.engine_nop().then_inc(src_all, 1)
                pool.wait_ge(node_out, 16)
                for a, ids in enumerate((idx_srcn, idx_dstn)):
                    with pool.Fori(0, NG // 2) as i:
                        for p in range(2):
                            n = (2 + a) * (NG // 2) + i
                            pool.tensor_copy(ring_idx[:, p, :], ids[:, bass.ds((2 * i + p) * G, G)]
                                             ).then_inc(idx_copied, 1)
                            pool.wait_ge(idx_copied, 2 * n + p + 1)
                            pool.sem_inc(ring_free, 1)
                            for k in range(G):
                                pool.indirect_dma_start(
                                    out=ring_info[:, p, k, :], out_offset=None, in_=node_dram,
                                    in_offset=bass.IndirectOffsetOnAxis(ap=ring_idx[:, p, k:k + 1], axis=0),
                                ).then_inc(info_in[p], 16)
                        for p in range(2):
                            m = a * (NG // 2) + i
                            pool.wait_ge(info_in[p], 16 * G * m + 16 * G)
                            pool.tensor_copy(info[:, a, bass.ds((2 * i + p) * G, G), :], ring_info[:, p, :, :]
                                             ).then_inc(info_copied, 1)
                            pool.wait_ge(info_copied, 2 * m + p + 1)
                            pool.sem_inc(ring_free, 1)

            @block.tensor
            def _(pe):
                for a in range(2):
                    for q in range(HR):
                        pe.wait_ge(hot_ready, a * ET + q + 1)
                        for b in range(4):
                            mm = pe.matmul(psum[0:HP, 2 * a + b // 2, (b % 2) * 512:(b % 2) * 512 + LO],
                                           onehot[:, q, b * HP:(b + 1) * HP], onehot[:, q, HI:HI + LO],
                                           start=(q == 0), stop=False)
                        mm.then_inc(hot_used, 1)
                    with pe.Fori(1, ET // HR) as i:
                        for q in range(HR):
                            pe.wait_ge(hot_ready, i * HR + (a * ET + q + 1))
                            for b in range(4):
                                mm = pe.matmul(psum[0:HP, 2 * a + b // 2, (b % 2) * 512:(b % 2) * 512 + LO],
                                               onehot[:, q, b * HP:(b + 1) * HP], onehot[:, q, HI:HI + LO],
                                               start=False, stop=False)
                            mm.then_inc(hot_used, 1)
                pe.wait_ge(tab_dve, 1)
                for a in range(2):
                    for b in range(4):
                        mm = pe.matmul(psum[0:HP, 2 * a + b // 2, (b % 2) * 512:(b % 2) * 512 + LO],
                                       onehot[:, 0, b * HP:(b + 1) * HP], onehot[:, 1, HI:HI + LO],
                                       start=False, stop=True)
                mm.then_inc(counted, 1)
                pe.wait_ge(tab_dve, 12)
                pe.matmul(psum[0:HP, 0, 0:4], upper[0:HP, 0:HP], tot[:, 0:4], start=True, stop=False)
                pe.matmul(psum[0:HP, 0, 0:4], ones_sq[0:HP, 0:HP], tot[:, 4:8], start=False,
                          stop=True).then_inc(tab_pe, 1)
                pe.wait_ge(tab_dve, 17)

                def transposed(j, k, step):
                    for t in range(DG):
                        mm = pe.transpose(ps(j)[:, t * P:(t + 1) * P], B(j, k)[:, t * P:(t + 1) * P], ident[:, :])
                    mm.then_inc(step[j], 1)

                def times(j, terms, step):
                    for t in range(DG):
                        o = ps(j)[:, t * P:(t + 1) * P]
                        for n, (k, m) in enumerate(terms):
                            mm = pe.matmul(o, B(j, k)[:, t * P:(t + 1) * P] if k is not None else ones_row[0:1, :],
                                           m, start=(n == 0), stop=(n == len(terms) - 1))
                    mm.then_inc(step[j], 1)

                def hidden(j, step):
                    for h in range(2):
                        mm = pe.matmul(ps(j)[:, h * 512:(h + 1) * 512], w_use[:, 2, :],
                                       B(j, 1)[:, h * 512:(h + 1) * 512], start=True, stop=True)
                    mm.then_inc(step[j], 1)

                C = center[:, :]

                def dense(i):
                    for j in range(DS):
                        pe.wait_ge(x_in[j], 16 * i + 16)
                        pe.wait_ge(dve_step[j], DDVE * i)
                        transposed(j, 0, pe_step)
                    for j in range(DS):
                        pe.wait_ge(act_step[j], DACT * i + 1)
                        times(j, [(1, C)], pe_step)
                    for j in range(DS):
                        pe.wait_ge(dve_step[j], DDVE * i + 2)
                        transposed(j, 3, pe_step)
                    for j in range(DS):
                        pe.wait_ge(dve_step[j], DDVE * i + 4)
                        times(j, [(4, C)], pe_step)
                    for j in range(DS):
                        pe.wait_ge(dve_step[j], DDVE * i + 6)
                        transposed(j, 3, pe_step)
                    for j in range(DS):
                        pe.wait_ge(dve_step[j], DDVE * i + 8)
                        times(j, [(1, C), (4, C)], pe_step)
                    for j in range(DS):
                        pe.wait_ge(dve_step[j], DDVE * i + 10)
                        transposed(j, 3, pe_step)
                    for j in range(DS):
                        pe.wait_ge(act_step[j], DACT * i + 15)
                        hidden(j, pe_step)
                    for j in range(DS):
                        pe.wait_ge(act_step[j], DACT * i + 16)
                        times(j, [(1, C), (4, w_use[:, 4, :]), (None, bias_row[0:1, 2, :])], pe_step)

                with pe.Fori(0, DENSE_IT) as i:
                    dense(i)

                def source(i):
                    for j in range(DS):
                        pe.wait_ge(s_in[j], 16 * i + 16)
                        pe.wait_ge(s_dve[j], SDVE * i)
                        transposed(j, 0, s_pe)
                    for j in range(DS):
                        pe.wait_ge(s_act[j], SACT * i + 1)
                        times(j, [(1, C)], s_pe)
                    for j in range(DS):
                        pe.wait_ge(s_dve[j], SDVE * i + 2)
                        transposed(j, 3, s_pe)
                    for j in range(DS):
                        pe.wait_ge(s_dve[j], SDVE * i + 4)
                        transposed(j, 4, s_pe)
                    for j in range(DS):
                        pe.wait_ge(s_act[j], SACT * i + 7)
                        times(j, [(4, C)], s_pe)
                    for j in range(DS):
                        pe.wait_ge(s_dve[j], SDVE * i + 6)
                        transposed(j, 3, s_pe)
                    for j in range(DS):
                        pe.wait_ge(s_dve[j], SDVE * i + 8)
                        times(j, [(1, C), (4, C)], s_pe)
                    for j in range(DS):
                        pe.wait_ge(s_dve[j], SDVE * i + 11)
                        transposed(j, 3, s_pe)
                    for j in range(DS):
                        pe.wait_ge(s_act[j], SACT * i + 18)
                        hidden(j, s_pe)
                    for j in range(DS):
                        pe.wait_ge(s_act[j], SACT * i + 19)
                        transposed(j, 4, s_pe)
                    for j in range(DS):
                        pe.wait_ge(s_act[j], SACT * i + 20)
                        times(j, [(1, C), (4, w_use[:, 4, :]), (None, bias_row[0:1, 2, :])], s_pe)

                for j in range(DS):
                    pe.wait_ge(dve_step[j], DDVE * DENSE_IT)
                with pe.Fori(0, SRC_IT) as i:
                    source(i)

            @block.scalar
            def _(act):
                act.preload_act_table_set("natural_log_exp_and_others")

                def inv_std(j, i, step, per, k, dve, dper, d, scale, bias, o):
                    return None

                def squares(j):
                    return act.activation(B(j, 2), ps(j), ACT.Square)

                def log_var(j, scale, c):
                    return act.activation(small[:, j, 1, :], small[:, j, 0, :], ACT.Ln, bias=eps_t[:, c:c + 1],
                                          scale=scale)

                def inv_root(j, o=2):
                    return act.activation(small[:, j, o, :], small[:, j, 1, :], ACT.Exp, scale=-0.5)

                def norm_steps(i, k, pe_k, dve_k, S, per, pper, dper, pe_s, dve_s):
                    for j in range(DS):
                        act.wait_ge(pe_s[j], pper * i + pe_k)
                        squares(j).then_inc(S[j], 1)
                    for j in range(DS):
                        act.wait_ge(dve_s[j], dper * i + dve_k)
                        log_var(j, 1.0 / P, 0).then_inc(S[j], 1)
                    for j in range(DS):
                        act.wait_ge(S[j], per * i + k + 1)
                        inv_root(j).then_inc(S[j], 1)

                def affine_exp(i, l, pe_k, S, pper, pe_s):
                    for j in range(DS):
                        act.wait_ge(pe_s[j], pper * i + pe_k)
                        act.activation(B(j, 2), ps(j), ACT.Exp, bias=beta(l), scale=gamma(l)).then_inc(S[j], 1)
                        act.activation(B(j, 3), ps(j), ACT.Identity, bias=beta(l), scale=gamma(l)).then_inc(S[j], 1)

                def dense(i):
                    args = (act_step, DACT, DPE, DDVE, pe_step, dve_step)
                    for j in range(DS):
                        act.wait_ge(pe_step[j], DPE * i + 1)
                        act.copy(B(j, 1), ps(j)).then_inc(act_step[j], 1)
                    norm_steps(i, 2, 2, 1, *args)
                    affine_exp(i, 0, 3, act_step, DPE, pe_step)
                    norm_steps(i, 7, 4, 5, *args)
                    affine_exp(i, 1, 5, act_step, DPE, pe_step)
                    for j in range(DS):
                        act.wait_ge(pe_step[j], DPE * i + 6)
                        squares(j).then_inc(act_step[j], 1)
                    for j in range(DS):
                        act.wait_ge(dve_step[j], DDVE * i + 9)
                        log_var(j, (1.0 + EPS) / P, 1).then_inc(act_step[j], 1)
                    for j in range(DS):
                        act.wait_ge(act_step[j], DACT * i + 13)
                        inv_root(j).then_inc(act_step[j], 1)
                    for j in range(DS):
                        act.wait_ge(pe_step[j], DPE * i + 7)
                        act.copy(B(j, 1), ps(j)).then_inc(act_step[j], 1)
                    for j in range(DS):
                        act.wait_ge(pe_step[j], DPE * i + 8)
                        act.activation(B(j, 4), ps(j), ACT.Relu, bias=cols[:, 4:5]).then_inc(act_step[j], 1)
                    for j in range(DS):
                        act.wait_ge(pe_step[j], DPE * i + 9)
                        squares(j).then_inc(act_step[j], 1)
                    for j in range(DS):
                        act.wait_ge(dve_step[j], DDVE * i + 11)
                        log_var(j, (1.0 + EPS) / P, 1).then_inc(act_step[j], 1)
                    for j in range(DS):
                        act.wait_ge(act_step[j], DACT * i + 18)
                        inv_root(j).then_inc(act_step[j], 1)

                with act.Fori(0, DENSE_IT) as i:
                    dense(i)

                def source(i):
                    args = (s_act, SACT, SPE, SDVE, s_pe, s_dve)
                    for j in range(DS):
                        act.wait_ge(s_pe[j], SPE * i + 1)
                        act.copy(B(j, 1), ps(j)).then_inc(s_act[j], 1)
                    norm_steps(i, 2, 2, 1, *args)
                    affine_exp(i, 0, 3, s_act, SPE, s_pe)
                    for j in range(DS):
                        act.wait_ge(s_pe[j], SPE * i + 4)
                        act.wait_ge(h1_out[j], 16 * i)
                        act.copy(B(j, 5), ps(j)).then_inc(s_act[j], 1)
                    norm_steps(i, 8, 5, 5, *args)
                    affine_exp(i, 1, 6, s_act, SPE, s_pe)
                    norm_steps(i, 13, 7, 9, *args)
                    for j in range(DS):
                        act.activation(small[:, j, 3, :], small[:, j, 0, :], ACT.Ln, bias=eps_t[:, 1:2],
                                       scale=(1.0 + EPS) / P).then_inc(s_act[j], 1)
                    for j in range(DS):
                        act.wait_ge(s_act[j], SACT * i + 16)
                        act.activation(small[:, j, 3, :], small[:, j, 3, :], ACT.Exp, scale=-0.5
                                       ).then_inc(s_act[j], 1)
                    for j in range(DS):
                        act.wait_ge(s_pe[j], SPE * i + 8)
                        act.copy(B(j, 1), ps(j)).then_inc(s_act[j], 1)
                    for j in range(DS):
                        act.wait_ge(s_pe[j], SPE * i + 9)
                        act.activation(B(j, 4), ps(j), ACT.Relu, bias=cols[:, 4:5]).then_inc(s_act[j], 1)
                    for j in range(DS):
                        act.wait_ge(s_pe[j], SPE * i + 10)
                        act.wait_ge(y1_out[j], 16 * i + 16)
                        act.copy(B(j, 5), ps(j)).then_inc(s_act[j], 1)
                    for j in range(DS):
                        act.wait_ge(x1_out[j], 16 * i + 16)
                    norm_steps(i, 21, 11, 12, *args)

                for j in range(DS):
                    act.wait_ge(out_stored[j], 16 * DENSE_IT)
                with act.Fori(0, SRC_IT) as i:
                    source(i)

            @block.vector
            def _(dve):
                for a in range(2):
                    def hot(i, q, wait):
                        t = i * HR + q
                        if wait:
                            dve.wait_ge(hot_used, a * ET + t - HR + 1)
                        dve.tensor_scalar(onehot[:, q, 0:HI], iota_h[:, :], hilo[:, 2 * a, bass.ds(t, 1)], None,
                                          ALU.is_equal)
                        dve.tensor_scalar(onehot[:, q, HI:HI + LO], iota_h[:, 0:LO],
                                          hilo[:, 2 * a + 1, bass.ds(t, 1)], None, ALU.is_equal
                                          ).then_inc(hot_ready, 1)
                    for q in range(HR):
                        hot(0, q, a > 0)
                    with dve.Fori(1, ET // HR) as i:
                        for q in range(HR):
                            hot(i, q, True)
                dve.wait_ge(hot_used, 2 * ET)
                dve.memset(onehot[:, 1, HI:HI + LO], 0.0).then_inc(tab_dve, 1)
                with dve.Fori(0, NG // 2) as i:
                    for p in range(2):
                        dve.wait_ge(dstrow_in[p], 16 * i + 16)
                        dve.wait_ge(match_out[p], 16 * i)
                        dve.tensor_tensor(extra[:, 2 + p, :].rearrange("p (k d) -> p k d", d=P),
                                          extra[:, p, :].rearrange("p (k d) -> p k d", d=P),
                                          dstP[:, bass.ds((2 * i + p) * G, G)].unsqueeze(2).to_broadcast([P, G, P]),
                                          ALU.is_equal).then_inc(match_ready, 1)
                dve.wait_ge(counted, 1)
                for a, f in enumerate((2, 1)):
                    for h in range(2):
                        dve.tensor_copy(node[:, 2 * h:2 * h + 2, :, f],
                                        psum[0:HP, 2 * a + h, :].rearrange("p (b w) -> p b w", b=2)[:, :, 0:LO]
                                        ).then_inc(tab_dve, 1)
                dve.memset(node[:, :, :, 3], 0.0).then_inc(tab_dve, 1)
                dve.wait_ge(tab_dve, 6)
                for b in range(4):
                    dve.tensor_tensor_scan(incl[:, b, :], node[:, b, :, 1], node[:, b, :, 3], 0.0, ALU.add, ALU.add
                                           ).then_inc(tab_dve, 1)
                dve.wait_ge(tab_dve, 10)
                dve.tensor_copy(tot[:, 0:4], incl[:, :, LO - 1])
                dve.memset(tot[:, 4:5], 0.0)
                dve.tensor_copy(tot[:, 5:6], incl[:, 0, LO - 1:LO])
                dve.tensor_tensor(tot[:, 6:7], incl[:, 0, LO - 1:LO], incl[:, 1, LO - 1:LO], ALU.add
                                  ).then_inc(tab_dve, 1)
                dve.wait_ge(tab_dve, 11)
                dve.tensor_tensor(tot[:, 7:8], tot[:, 6:7], incl[:, 2, LO - 1:LO], ALU.add
                                  ).then_inc(tab_dve, 1)
                dve.wait_ge(tab_pe, 1)
                dve.tensor_copy(tot[:, 0:4], psum[0:HP, 0, 0:4]).then_inc(tab_dve, 1)
                dve.wait_ge(tab_dve, 13)
                for b in range(4):
                    dve.scalar_tensor_tensor(out=node[:, b, :, 0], in0=incl[:, b, :], scalar=tot[:, b:b + 1],
                                             in1=node[:, b, :, 1], op0=ALU.add, op1=ALU.subtract
                                             ).then_inc(tab_dve, 1)

                def wide(ap):
                    return ap.rearrange("p (k d) -> p k d", d=P)

                def sum_squares(j):
                    return dve.tensor_reduce(small[:, j, 0, :], wide(B(j, 2)), AX_X, ALU.add)

                def scaled(j, k, r=2):
                    return dve.tensor_tensor(wide(B(j, k)), wide(ps(j)),
                                             small[:, j, r, :].unsqueeze(2).to_broadcast([P, DG, P]), ALU.mult)

                def norm_steps(i, act_k, S, per, aper, act_s, k_out):
                    for j in range(DS):
                        dve.wait_ge(act_s[j], aper * i + act_k)
                        sum_squares(j).then_inc(S[j], 1)
                    for j in range(DS):
                        dve.wait_ge(act_s[j], aper * i + act_k + 2)
                        scaled(j, k_out).then_inc(S[j], 1)

                def elu_steps(i, k, act_k, S, per, aper, act_s):
                    for j in range(DS):
                        dve.wait_ge(act_s[j], aper * i + act_k)
                        dve.tensor_scalar(B(j, 2), B(j, 2), 1.0, -1.0, ALU.min, ALU.add).then_inc(S[j], 1)
                    for j in range(DS):
                        dve.wait_ge(act_s[j], aper * i + act_k + 1)
                        dve.wait_ge(S[j], per * i + k)
                        dve.tensor_tensor(B(j, 4), B(j, 3), B(j, 2), ALU.max).then_inc(S[j], 1)

                with dve.Fori(0, DENSE_IT) as i:
                    args = (dve_step, DDVE, DACT, act_step)
                    norm_steps(i, 2, *args, 3)
                    elu_steps(i, 3, 5, *args)
                    norm_steps(i, 7, *args, 3)
                    elu_steps(i, 7, 10, *args)
                    norm_steps(i, 12, *args, 3)
                    for j in range(DS):
                        dve.wait_ge(act_step[j], DACT * i + 17)
                        sum_squares(j).then_inc(dve_step[j], 1)
                    for j in range(DS):
                        dve.wait_ge(act_step[j], DACT * i + 19)
                        dve.wait_ge(out_stored[j], 16 * i)
                        scaled(j, 5).then_inc(dve_step[j], 1)

                with dve.Fori(0, SRC_IT) as i:
                    args = (s_dve, SDVE, SACT, s_act)
                    for j in range(DS):
                        dve.wait_ge(x2_out[j], 16 * i)
                    norm_steps(i, 2, *args, 3)
                    elu_steps_wait = [dve.wait_ge(x3_out[j], 16 * i) for j in range(DS)]
                    elu_steps(i, 3, 5, *args)
                    norm_steps(i, 8, *args, 3)
                    elu_steps(i, 7, 11, *args)
                    norm_steps(i, 13, *args, 2)
                    for j in range(DS):
                        dve.wait_ge(s_act[j], SACT * i + 17)
                        scaled(j, 3, 3).then_inc(s_dve[j], 1)
                    norm_steps(i, 21, *args, 4)

        with ExitStack() as ctx:
            sem = phase_semaphores(nc, ctx, "")

            v, a = sem("wt_dve"), sem("wt_act")
            block = ctx.enter_context(nc.Block())
            out_src, out_dst, in_dst = info[:, 0, :, 2], info[:, 1, :, 2], info[:, 1, :, 1]
            in_src, first_src, first_dst = info[:, 0, :, 1], info[:, 0, :, 0], info[:, 1, :, 0]

            @block.vector
            def _(dve):
                dve.tensor_tensor(tmp[:, 0, :], out_src, in_dst, ALU.mult).then_inc(v, 1)
                dve.tensor_scalar(w_light[:, :], out_dst, 1.0, None, ALU.max).then_inc(v, 1)
                dve.wait_ge(v, 2)
                dve.tensor_tensor(tmp[:, 1, :], out_src, w_light[:, :], ALU.mult).then_inc(v, 1)
                dve.reciprocal(w_mean[:, :], in_dst).then_inc(v, 1)
                dve.tensor_scalar(tmp[:, 2, :], in_src, 0.5, None, ALU.is_gt).then_inc(v, 1)
                dve.tensor_scalar(edge_no[:, :], edge_no[:, :], float(EP), None, ALU.add).then_inc(v, 1)
                dve.wait_ge(v, 6)
                dve.tensor_tensor(first_src, first_src, edge_no[:, :], ALU.subtract).then_inc(v, 1)
                dve.wait_ge(v, 7)
                dve.tensor_tensor(first_src, first_src, tmp[:, 2, :], ALU.mult).then_inc(v, 1)
                dve.wait_ge(v, 8)
                dve.tensor_tensor(first_src, first_src, edge_no[:, :], ALU.add).then_inc(v, 1)
                dve.wait_ge(v, 9)
                dve.tensor_copy(idx_lvl[:, :], first_src).then_inc(v, 1)
                dve.tensor_scalar(edge_no[:, :], edge_no[:, :], -float(EP), None, ALU.add).then_inc(v, 1)
                dve.wait_ge(v, 11)
                dve.tensor_tensor(tmp[:, 2, :], first_dst, edge_no[:, :], ALU.not_equal).then_inc(v, 1)
                dve.wait_ge(v, 12)
                dve.scalar_tensor_tensor(out=tmp[:, 2, :], in0=tmp[:, 2, :], scalar=float(4 * HI * LO), in1=dstP[:, :],
                                         op0=ALU.mult, op1=ALU.add).then_inc(v, 1)
                dve.wait_ge(v, 13)
                dve.tensor_copy(idx_out[:, :], tmp[:, 2, :]).then_inc(v, 1)
                dve.wait_ge(a, 4)
                dve.tensor_tensor(w_gcn[:, :], tmp[:, 0, :], wP[:, :], ALU.mult).then_inc(v, 1)

            @block.scalar
            def _(act):
                act.wait_ge(v, 3)
                act.activation(tmp[:, 0, :], tmp[:, 0, :], ACT.Ln).then_inc(a, 1)
                act.activation(tmp[:, 1, :], tmp[:, 1, :], ACT.Ln).then_inc(a, 1)
                act.wait_ge(a, 2)
                act.activation(tmp[:, 0, :], tmp[:, 0, :], ACT.Exp, scale=-0.5).then_inc(a, 1)
                act.activation(w_light[:, :], tmp[:, 1, :], ACT.Exp, scale=-0.5).then_inc(a, 1)

        weights = [w_gcn, w_gcn, None, w_mean, w_mean, w_light]
        tables = [src_x] + level_rows[1:6]
        dst_tables = [dst_x] + level_rows[1:6]
        for level in range(6):
            sum_edges(nc, locals(), level, weights[level], tables[level], dst_tables[level])
            carry_sums(nc, locals(), level)
            update_rows(nc, locals(), level, dst_tables)


def sum_edges(nc, env, level, weight, table, dst_table):
    buf, extra, psum, ident, w_use = (env[k] for k in ("buf", "extra", "psum", "ident", "w_use"))
    match_dram, agg_dram, edge_attr = env["match_dram"], env["agg_dram"], env["edge_attr"]
    ring_idx, idx_lvl, ones_row, edge_bias = env["ring_idx"], env["idx_lvl"], env["ones_row"], env["edge_bias"]
    edge_rows, NG, E, TAIL, EP = env["edge_rows"], env["NG"], env["E"], env["TAIL"], env["EP"]
    HALF = NG // 2
    relational = level == 2
    gathers = level > 0

    def wide(ap):
        return ap.rearrange("p (k d) -> p k d", d=P)

    M = [buf[3][:, p, 0:GW] for p in range(2)]
    R = [buf[3][:, 2 + p, 0:GW] for p in range(2)]
    O = [buf[3][:, 4 + p, 0:GW] for p in range(2)]
    XD = [extra[:, p, :] for p in range(2)]
    AT = [extra[:, 2 + p, :] for p in range(2)]
    ZT = [extra[:, 4 + p, :] for p in range(2)]
    AX = [extra[:, 6 + p, :] for p in range(2)]
    with ExitStack() as ctx:
        sem = phase_semaphores(nc, ctx, f"_{level}")

        match_in = [sem(f"match_in{p}") for p in range(2)]
        rows_in = [sem(f"rows_got{p}") for p in range(2)]
        more_in = [sem(f"more_in{p}") for p in range(2)]
        summed_out = [sem(f"summed_out{p}") for p in range(2)]
        idx_copied, ring_free = sem("lvl_idx"), sem("lvl_ring_free")
        scaled, multiplied, copied = sem("scaled"), sem("multiplied"), sem("copied")
        z_ready, zT_ready, a_ready, aT_ready, m_ready, msg_ready = (
            sem(n) for n in ("z_ready", "zT_ready", "a_ready", "aT_ready", "m_ready", "msg_ready"))
        block = ctx.enter_context(nc.Block())
        OUT_PS = [psum[:, 2 * p + 1, 0:GW] for p in range(2)]
        IN_PS = [psum[:, 2 * p, 0:GW] for p in range(2)]

        @block.sync
        def _(sp):
            def loads(i, p, last=False):
                g = 2 * i + p
                sp.dma_start(M[p], match_dram[bass.ds(g, 1)].rearrange("a p w -> (a p) w")).then_inc(match_in[p], 16)
                if not gathers:
                    sp.dma_start(wide(R[p]), edge_rows(table, g)).then_inc(rows_in[p], 16)
                if relational:
                    sp.dma_start(wide(XD[p]), edge_rows(dst_table, g)).then_inc(more_in[p], 16)
                    sp.dma_start(wide(AT[p])[:, 0:G - 1, :],
                                 edge_attr[bass.ds(g * GW, GW - P), :].rearrange("(k p) d -> p k d", p=P)
                                 ).then_inc(more_in[p], 16)
                    rows = TAIL if last else P
                    sp.dma_start(AT[p][0:rows, (G - 1) * P:GW],
                                 edge_attr[bass.ds(g * GW + GW - P, rows), :]).then_inc(more_in[p], 16)

            def store(i, p):
                sp.wait_ge(copied, 2 * i + p + 1)
                sp.dma_start(edge_rows(agg_dram, 2 * i + p), wide(O[p])).then_inc(summed_out[p], 16)

            for p in range(2):
                loads(0, p)
            with sp.Fori(0, HALF - 2) as i:
                for p in range(2):
                    sp.wait_ge(multiplied, 2 * i + p + 1)
                    loads(i + 1, p)
                    store(i, p)
            i = HALF - 2
            for p in range(2):
                sp.wait_ge(multiplied, 2 * i + p + 1)
                loads(i + 1, p, last=(p == 1))
                store(i, p)
            for p in range(2):
                store(HALF - 1, p)
            for p in range(2):
                sp.wait_ge(summed_out[p], 16 * HALF)

        if gathers:
            @block.gpsimd
            def _(pool):
                with pool.Fori(0, HALF) as i:
                    for p in range(2):
                        if relational:
                            pool.wait_ge(z_ready, 2 * i)
                        else:
                            pool.wait_ge(multiplied, 2 * i)
                        pool.sem_inc(ring_free, 1)
                        pool.tensor_copy(ring_idx[:, p, :], idx_lvl[:, bass.ds((2 * i + p) * G, G)]
                                         ).then_inc(idx_copied, 1)
                        pool.wait_ge(idx_copied, 2 * i + p + 1)
                        pool.sem_inc(ring_free, 1)
                        for k in range(G):
                            pool.indirect_dma_start(
                                out=R[p][:, k * P:(k + 1) * P], out_offset=None, in_=table,
                                in_offset=bass.IndirectOffsetOnAxis(ap=ring_idx[:, p, k:k + 1], axis=0),
                            ).then_inc(rows_in[p], 16)

        ROWS = 16 * G if gathers else 16

        @block.tensor
        def _(pe):
            with pe.Fori(0, HALF) as i:
                if relational:
                    for p in range(2):
                        pe.wait_ge(rows_in[p], ROWS * i + ROWS)
                        pe.wait_ge(more_in[p], 48 * i + 48)
                        pe.wait_ge(msg_ready, 2 * i)
                        for k in range(G):
                            o = IN_PS[p][:, k * P:(k + 1) * P]
                            pe.matmul(o, R[p][:, k * P:(k + 1) * P], ident[:, :], start=True, stop=False)
                            mm = pe.matmul(o, XD[p][:, k * P:(k + 1) * P], ident[:, :], start=False, stop=True)
                        mm.then_inc(z_ready, 1)
                    for p in range(2):
                        pe.wait_ge(copied, 2 * i)
                        for k in range(G):
                            mm = pe.transpose(OUT_PS[p][:, k * P:(k + 1) * P], AT[p][:, k * P:(k + 1) * P], ident[:, :])
                        mm.then_inc(a_ready, 1)
                    for p in range(2):
                        pe.wait_ge(zT_ready, 2 * i + p + 1)
                        pe.wait_ge(aT_ready, 2 * i + p + 1)
                        for k in range(G):
                            o = IN_PS[p][:, k * P:(k + 1) * P]
                            pe.matmul(o, ZT[p][:, k * P:(k + 1) * P], w_use[:, 0, :], start=True, stop=False)
                            pe.matmul(o, AX[p][:, k * P:(k + 1) * P], w_use[:, 1, :], start=False, stop=False)
                            mm = pe.matmul(o, ones_row[0:1, :], edge_bias[0:1, :], start=False, stop=True)
                        mm.then_inc(m_ready, 1)
                for p in range(2):
                    pe.wait_ge(match_in[p], 16 * i + 16)
                    if relational:
                        pe.wait_ge(msg_ready, 2 * i + p + 1)
                    else:
                        pe.wait_ge(scaled, 2 * i + p + 1)
                        pe.wait_ge(copied, 2 * i)
                    rows = ZT[p] if relational else R[p]
                    for k in range(G):
                        mm = pe.matmul(OUT_PS[p][:, k * P:(k + 1) * P], M[p][:, k * P:(k + 1) * P],
                                       rows[:, k * P:(k + 1) * P], start=True, stop=True)
                    mm.then_inc(multiplied, 1)

        @block.vector
        def _(dve):
            with dve.Fori(0, HALF) as i:
                for p in range(2):
                    if relational:
                        dve.wait_ge(a_ready, 2 * i + p + 1)
                        dve.tensor_copy(AX[p], OUT_PS[p]).then_inc(aT_ready, 1)
                    else:
                        dve.wait_ge(rows_in[p], ROWS * i + ROWS)
                        w = weight[:, bass.ds((2 * i + p) * G, G)].unsqueeze(2).to_broadcast([P, G, P])
                        dve.tensor_tensor(wide(R[p]), wide(R[p]), w, ALU.mult).then_inc(scaled, 1)

        @block.scalar
        def _(act):
            with act.Fori(0, HALF) as i:
                if relational:
                    for p in range(2):
                        act.wait_ge(z_ready, 2 * i + p + 1)
                        act.copy(ZT[p], IN_PS[p]).then_inc(zT_ready, 1)
                    for p in range(2):
                        act.wait_ge(m_ready, 2 * i + p + 1)
                        act.activation(ZT[p], IN_PS[p], ACT.Relu).then_inc(msg_ready, 1)
                for p in range(2):
                    act.wait_ge(multiplied, 2 * i + p + 1)
                    act.wait_ge(summed_out[p], 16 * i)
                    act.copy(O[p], OUT_PS[p]).then_inc(copied, 1)


def carry_sums(nc, env, level):
    extra, psum, reach = env["extra"], env["psum"], env["reach"]
    agg_dram, carry_dram, HB, ET = env["agg_dram"], env["carry_dram"], env["HB"], env["ET"]
    with ExitStack() as ctx:
        sem = phase_semaphores(nc, ctx, f"_{level}")

        ends_in, carried, copied, carry_out = (sem(n) for n in ("carry_ends", "carried", "carry_copied", "carry_out"))
        block = ctx.enter_context(nc.Block())
        by_tile = agg_dram.rearrange("(b t i) d -> t b i d", b=2, i=P)
        side_rows = [extra[0:HB, s, 0:2 * P].rearrange("t (b d) -> t b d", b=2) for s in range(2)]

        @block.sync
        def _(sp):
            for s, at in enumerate((P - 1, 0)):
                sp.dma_start(side_rows[s], by_tile[:, :, at, :]).then_inc(ends_in, 16)
            sp.wait_ge(copied, 1)
            for s in range(2):
                sp.dma_start(carry_dram[s:s + 1, :].rearrange("a (b t d) -> (a t) b d", b=2, d=P),
                             extra[0:HB, 2 + s, 0:2 * P].rearrange("t (b d) -> t b d", b=2)).then_inc(carry_out, 16)
            sp.wait_ge(carry_out, 32)

        @block.tensor
        def _(pe):
            pe.wait_ge(ends_in, 32)
            for s in range(2):
                for tb in range(2):
                    for b in range(2):
                        mm = pe.matmul(psum[0:HB, s, tb * P:(tb + 1) * P], reach[:, s, b, tb * HB:(tb + 1) * HB],
                                       side_rows[s][:, b, :], start=(b == 0), stop=(b == 1))
            mm.then_inc(carried, 1)

        @block.vector
        def _(dve):
            dve.wait_ge(carried, 1)
            for s in range(2):
                ins = dve.tensor_copy(extra[0:HB, 2 + s, 0:2 * P], psum[0:HB, s, 0:2 * P])
            ins.then_inc(copied, 1)


def update_rows(nc, env, level, dst_tables):
    buf, carry_in, psum, small, cols = (env[k] for k in ("buf", "carry_in", "psum", "small", "cols"))
    ident, center, w_use, eps_t = (env[k] for k in ("ident", "center", "w_use", "eps_t"))
    ones_row, bias_row, agg_dram, carry_dram = (env[k] for k in ("ones_row", "bias_row", "agg_dram", "carry_dram"))
    ends_mask, edge_rows, NG, N = env["ends_mask"], env["edge_rows"], env["NG"], env["N"]
    idx_out, ring_out, out = env["idx_out"], env["ring_idx"], env["out"]
    IT = NG // US
    PE_N = (4, 5, 3, 4, 4, 2)[level]
    ACT_N = (7, 10, 5, 4, 6, 4)[level]
    DVE_N = (4, 6, 2, 1, 2, 2)[level]
    LOADS = (4, 5, 4, 4, 5, 4)[level]
    RESULT = (1, 3, 3, 2, 1, 3)[level]

    def B(j, k):
        return buf[j][:, k, 0:GW]

    def ps(j):
        return psum[:, j, 0:GW]

    def wide(ap):
        return ap.rearrange("p (k d) -> p k d", d=P)

    with ExitStack() as ctx:
        sem = phase_semaphores(nc, ctx, f"_{level}")

        loaded = [sem(f"loaded{j}") for j in range(US)]
        pe_step = [sem(f"upe{j}") for j in range(US)]
        act_step = [sem(f"uact{j}") for j in range(US)]
        dve_step = [sem(f"udve{j}") for j in range(US)]
        stored = [sem(f"stored{j}") for j in range(US)]
        idx_ready, rows_final = sem("idx_ready"), sem("rows_final")
        block = ctx.enter_context(nc.Block())
        done, DONE_N = {1: (act_step, ACT_N), 0: (dve_step, DVE_N)}[int(level in (0, 3))]
        STORES = 16 * G if level == 5 else 16

        @block.sync
        def _(sp):
            def loads(i, j):
                g = US * i + j
                sp.dma_start(wide(B(j, 5)), edge_rows(agg_dram, g)).then_inc(loaded[j], 16)
                sp.dma_start(carry_in[j][:, 0, :], carry_dram[:, bass.ds(g * GW, GW)]).then_inc(loaded[j], 16)
                sp.dma_start(carry_in[j][:, 1, :], ends_mask[:, bass.ds(g * GW, GW)]).then_inc(loaded[j], 16)
                state = dst_tables[3 if level == 4 else level]
                sp.dma_start(wide(B(j, 0)), edge_rows(state, g)).then_inc(loaded[j], 16)
                if level == 1:
                    sp.dma_start(wide(B(j, 4)), edge_rows(dst_tables[0], g)).then_inc(loaded[j], 16)
                if level == 4:
                    sp.dma_start(wide(B(j, 3)), edge_rows(dst_tables[4], g)).then_inc(loaded[j], 16)

            def store(i, j):
                if level < 5:
                    sp.wait_ge(done[j], DONE_N * i + DONE_N)
                    sp.dma_start(edge_rows(dst_tables[level + 1], US * i + j), wide(B(j, RESULT))
                                 ).then_inc(stored[j], 16)

            for j in range(US):
                loads(0, j)
            with sp.Fori(0, IT - 1) as i:
                for j in range(US):
                    sp.wait_ge(pe_step[j], PE_N * i + PE_N)
                    loads(i + 1, j)
                for j in range(US):
                    store(i, j)
            for j in range(US):
                store(IT - 1, j)
            for j in range(US):
                if level < 5:
                    sp.wait_ge(stored[j], 16 * IT)

        if level == 5:
            @block.gpsimd
            def _(pool):
                with pool.Fori(0, IT) as i:
                    for j in range(US):
                        n = j % 2
                        if j < 2:
                            pool.wait_ge(stored[j + 2], STORES * i)
                        else:
                            pool.wait_ge(stored[j - 2], STORES * i + STORES)
                        pool.tensor_copy(ring_out[:, n, :], idx_out[:, bass.ds((US * i + j) * G, G)]
                                         ).then_inc(idx_ready, 1)
                        pool.wait_ge(idx_ready, US * i + j + 1)
                        pool.wait_ge(dve_step[j], DVE_N * i + DVE_N)
                        pool.sem_inc(rows_final, 1)
                        for k in range(G):
                            pool.indirect_dma_start(
                                out=out, out_offset=bass.IndirectOffsetOnAxis(ap=ring_out[:, n, k:k + 1], axis=0),
                                in_=B(j, 3)[:, k * P:(k + 1) * P], in_offset=None,
                                bounds_check=N - 1, oob_is_err=False).then_inc(stored[j], 16)
                for j in range(US):
                    pool.wait_ge(stored[j], STORES * IT)

        @block.tensor
        def _(pe):
            I, C = ident[:, :], center[:, :]

            def step(j, terms, tr=False):
                for t in range(G):
                    o = ps(j)[:, t * P:(t + 1) * P]
                    sl = slice(t * P, (t + 1) * P)
                    for n, (a, b) in enumerate(terms):
                        lhs = a if a.shape[-1] == P else a[:, sl]
                        rhs = b if b.shape[-1] == P else b[:, sl]
                        mm = pe.matmul(o, lhs, rhs, start=(n == 0), stop=(n == len(terms) - 1))
                mm.then_inc(pe_step[j], 1)

            def turn(j, k):
                for t in range(G):
                    mm = pe.transpose(ps(j)[:, t * P:(t + 1) * P], B(j, k)[:, t * P:(t + 1) * P], I)
                mm.then_inc(pe_step[j], 1)

            def after(s, per, i, k):
                def wait(j):
                    pe.wait_ge(s[j], per * i + k)
                return wait

            with pe.Fori(0, IT) as i:
                A = lambda k: after(act_step, ACT_N, i, k)
                V = lambda k: after(dve_step, DVE_N, i, k)
                sums = lambda j: [(B(j, 5), I), (carry_in[j][:, 0, :], carry_in[j][:, 1, :])]
                for j in range(US):
                    pe.wait_ge(loaded[j], 16 * LOADS * i + 16 * LOADS)
                    pe.wait_ge(done[j], DONE_N * i)
                    if level in (0, 1, 5):
                        step(j, [(B(j, 0), I)] + sums(j))
                    elif level == 2:
                        step(j, [(I, B(j, 5)), (carry_in[j][:, 1, :], carry_in[j][:, 0, :])])
                    else:
                        step(j, sums(j))
                if level == 1:
                    for j in range(US):
                        A(1)(j)
                        turn(j, 4)
                if level == 2:
                    for j in range(US):
                        A(1)(j)
                        step(j, [(B(j, 0), I), (B(j, 4), I)])
                if level in (3, 4):
                    for j in range(US):
                        A(1)(j)
                        turn(j, 0)
                if level in (0, 1, 2, 5):
                    k = 3 if level in (1, 2) else 2
                    for j in range(US):
                        A(k - 1)(j)
                        step(j, [(B(j, 1), C)])
                if level in (0, 1):
                    for j in range(US):
                        V(2)(j)
                        turn(j, 3)
                if level == 0:
                    for j in range(US):
                        V(4)(j)
                        turn(j, 4)
                if level == 1:
                    for j in range(US):
                        V(4)(j)
                        step(j, [(B(j, 0), C), (B(j, 4), C)])
                if level == 3:
                    for j in range(US):
                        A(2)(j)
                        for lo, hi in ((0, 512), (512, GW)):
                            pe.matmul(ps(j)[:, lo:hi], w_use[:, 2, :], B(j, 1)[:, lo:hi], start=True, stop=False)
                            mm = pe.matmul(ps(j)[:, lo:hi], w_use[:, 3, :], B(j, 4)[:, lo:hi], start=False, stop=True)
                        mm.then_inc(pe_step[j], 1)
                    for j in range(US):
                        A(3)(j)
                        turn(j, 3)
                if level == 4:
                    for j in range(US):
                        A(2)(j)
                        turn(j, 3)
                    for j in range(US):
                        A(3)(j)
                        step(j, [(B(j, 1), C), (B(j, 2), w_use[:, 4, :]), (B(j, 4), w_use[:, 5, :]),
                                 (ones_row[0:1, :], bias_row[0:1, 2, :])])

        @block.scalar
        def _(act):
            with act.Fori(0, IT) as i:
                def P_(j, k):
                    act.wait_ge(pe_step[j], PE_N * i + k)

                def put(k, b, func=ACT.Copy, **kw):
                    for j in range(US):
                        P_(j, k)
                        act.activation(B(j, b), ps(j), func, **kw).then_inc(act_step[j], 1)

                def norm_steps(pe_k, dve_k, act_k):
                    put(pe_k, 2, ACT.Square)
                    for j in range(US):
                        act.wait_ge(dve_step[j], DVE_N * i + dve_k)
                        act.activation(small[:, j, 1, 0:G], small[:, j, 0, 0:G], ACT.Ln, bias=eps_t[:, 0:1],
                                       scale=1.0 / P).then_inc(act_step[j], 1)
                    for j in range(US):
                        act.wait_ge(act_step[j], ACT_N * i + act_k + 1)
                        act.activation(small[:, j, 2, 0:G], small[:, j, 1, 0:G], ACT.Exp, scale=-0.5
                                       ).then_inc(act_step[j], 1)

                def affine(pe_k, l):
                    for j in range(US):
                        P_(j, pe_k)
                        act.activation(B(j, 2), ps(j), ACT.Exp, bias=cols[:, 2 + l:3 + l], scale=cols[:, l:l + 1]
                                       ).then_inc(act_step[j], 1)
                        act.activation(B(j, 3), ps(j), ACT.Identity, bias=cols[:, 2 + l:3 + l],
                                       scale=cols[:, l:l + 1]).then_inc(act_step[j], 1)

                def result_free():
                    for j in range(US):
                        act.wait_ge(stored[j], 16 * i)

                if level == 0:
                    result_free()
                    put(1, 1)
                    norm_steps(2, 1, 2)
                    affine(3, 0)
                    put(4, 1)
                if level == 1:
                    put(1, 1)
                    put(2, 0)
                    norm_steps(3, 1, 3)
                    affine(4, 1)
                    norm_steps(5, 5, 8)
                if level == 2:
                    put(1, 4, ACT.Relu)
                    put(2, 1)
                    norm_steps(3, 1, 3)
                if level == 3:
                    put(1, 4)
                    put(2, 1)
                    put(3, 3, ACT.Relu, bias=cols[:, 4:5])
                    result_free()
                    put(4, 2)
                if level == 4:
                    put(1, 4)
                    result_free()
                    put(2, 1)
                    put(3, 2)
                    norm_steps(4, 1, 4)
                if level == 5:
                    put(1, 1)
                    norm_steps(2, 1, 2)

        @block.vector
        def _(dve):
            if level == 3:
                return
            with dve.Fori(0, IT) as i:
                def norm_steps(act_k, k_out):
                    for j in range(US):
                        dve.wait_ge(act_step[j], ACT_N * i + act_k)
                        dve.tensor_reduce(small[:, j, 0, 0:G], wide(B(j, 2)), AX_X, ALU.add).then_inc(dve_step[j], 1)
                    for j in range(US):
                        dve.wait_ge(act_step[j], ACT_N * i + act_k + 2)
                        dve.tensor_tensor(wide(B(j, k_out)), wide(ps(j)),
                                          small[:, j, 2, 0:G].unsqueeze(2).to_broadcast([P, G, P]), ALU.mult
                                          ).then_inc(dve_step[j], 1)

                def elu_steps(act_k, k):
                    for j in range(US):
                        dve.wait_ge(act_step[j], ACT_N * i + act_k)
                        dve.tensor_scalar(B(j, 2), B(j, 2), 1.0, -1.0, ALU.min, ALU.add).then_inc(dve_step[j], 1)
                    for j in range(US):
                        dve.wait_ge(act_step[j], ACT_N * i + act_k + 1)
                        dve.wait_ge(dve_step[j], DVE_N * i + k)
                        dve.tensor_tensor(B(j, 4), B(j, 3), B(j, 2), ALU.max).then_inc(dve_step[j], 1)

                if level in (1, 2, 5):
                    for j in range(US):
                        dve.wait_ge(stored[j], STORES * i)
                if level == 0:
                    norm_steps(2, 3)
                    elu_steps(5, 3)
                if level == 1:
                    norm_steps(3, 3)
                    elu_steps(6, 3)
                    norm_steps(8, 3)
                if level == 2:
                    norm_steps(3, 3)
                if level == 4:
                    norm_steps(4, 1)
                if level == 5:
                    norm_steps(2, 3)


_INS = ["x", "src", "dst", "edge_attr_128", "edge_weight", "L0_gnn_ln_gamma", "L0_gnn_ln_beta", "L1_gnn_W_obj",
        "L1_gnn_b_obj", "L1_gnn_W_rel", "L1_gnn_b_rel", "L2_gnn_W1_self", "L2_gnn_W1_neigh", "L2_gnn_b1",
        "L2_gnn_W2_self", "L2_gnn_W2_neigh", "L2_gnn_b2"]


def build(nc, shapes):
    args = [nc.dram_tensor(f"in_{n}_dram", s, d, kind="ExternalInput").ap() for n, s, d in shapes]
    out = nc.dram_tensor("out_0_dram", shapes[0][1], F32, kind="ExternalOutput").ap()
    gnn_kernel(nc, *args, out)


def kernel(**inputs):
    import numpy as _np
    import concourse.bacc as _bacc
    from concourse.bass_utils import run_bass_kernel_spmd as _run

    nc = _bacc.Bacc("TRN2", target_bir_lowering=False, num_devices=1)
    arrays, shapes = {}, []
    for name in _INS:
        a = _np.ascontiguousarray(inputs[name])
        arrays[f"in_{name}_dram"] = a
        shapes.append((name, a.shape, mybir.dt.from_np(a.dtype)))
    build(nc, shapes)
    r = _run(nc, [arrays], core_ids=[0])
    return r.results[0]["out_0_dram"]
```

```python
from contextlib import ExitStack

import concourse.bass as bass
from concourse import mybir

ALU = mybir.AluOpType
ACT = mybir.ActivationFunctionType
F32 = mybir.dt.float32
F16 = mybir.dt.float16
BF16 = mybir.dt.bfloat16
I32 = mybir.dt.int32
AX_X = mybir.AxisListType.X

P = 128
EPS = 1e-5
US = 4
G = 7
GW = G * P
ROWS = US * GW
LO = 256
NBUF = 6


class Steps:

    def __init__(self, names):
        self.names = names.split()
        self.n = len(self.names)

    def at(self, it, name):
        return it * self.n + (self.names.index(name) + 1)


def wait(engine, sem, count):
    if not (isinstance(count, int) and count == 0):
        engine.wait_ge(sem, count)


def staggered(engine, n, stages, lag, body, tail=1):
    assert lag * (US - 1) < stages

    def ticks(i):
        for k in range(stages):
            for j in range(US):
                late = k < lag * j
                if isinstance(i, int) and ((late and i == 0) or (not late and i == n)):
                    continue
                body((k - lag * j) % stages, i - 1 if late else i, j)

    ticks(0)
    if n > 1 + tail:
        with engine.Fori(1, n - tail) as i:
            ticks(i)
    for i in range(max(1, n - tail), n + 1):
        ticks(i)


def phase_semaphores(nc, ctx, suffix):
    used = []

    def sem(name):
        used.append(nc.alloc_semaphore(name + suffix))
        return used[-1]

    def clear():
        nc.clear_and_free_semaphores(used)
        nc.all_engine_barrier()

    ctx.callback(clear)
    return sem


def gnn_kernel(nc, x, src, dst, edge_attr, edge_weight, ln_gamma, ln_beta, W_obj, b_obj, W_rel,
               b_rel, W1_self, W1_neigh, b1, W2_self, W2_neigh, b2, out):
    N = x.shape[0]
    E = src.shape[0]
    ET = -(-E // P)
    EP = ET * P
    HB = ET // 2
    NG = ET // G
    HI = -(-(N + 1) // (LO * 4)) * 4
    HP = HI // 4
    PAD = HI * LO - 1
    TAIL = E - (ET - 1) * P
    assert ET % (US * G) == 0 and PAD >= N and HP <= P and x.shape[1] == P

    with ExitStack() as root:
        root.enter_context(nc.allow_non_contiguous_dma(reason="small columns and edge id blocks"))

        def sb(name, shape, dt=F32):
            return root.enter_context(nc.sbuf_tensor(name, shape, dt))

        def dram(name, shape, dt=F32):
            return nc.dram_tensor(name, shape, dt).ap()

        level_rows = [None] + [dram(f"level{l}", (2 * EP, P)) for l in range(1, 6)]
        src_x = dram("src_x", (EP, P))
        dst_x = dram("dst_x", (EP, P))
        sums_dram = dram("sums", (NG, P, GW))
        match_dram = dram("match", (NG, P, GW))
        dst_flat = dram("dst_flat", (1, EP))
        ends_dram = dram("ends", (1, 2 * ET))
        ends_mask = dram("ends_mask", (6, EP), BF16)
        carry_dram = dram("carry", (6, EP), BF16)
        bias_dram = dram("bias", (3, 2 * P), BF16)
        node_dram = dram("node", (HI * LO, 4))

        ident = sb("ident", [P, P])
        center = sb("center", [P, P])
        ones3 = sb("ones3", [3, P], BF16)
        upper = sb("upper", [P, P])
        ones_sq = sb("ones_sq", [P, P])
        eps_t = sb("eps_t", [P, 2])
        w_raw = sb("w_raw", [P, 6, P])
        w_use = sb("w_use", [P, 6, P])
        cols = sb("cols", [P, 8])
        bias_row = sb("bias_row", [1, 2, P])
        bias_f = sb("bias_f", [1, 2, P])
        bias_parts = sb("bias_parts", [1, 3, 2, P], BF16)
        bias3 = sb("bias3", [3, 2, P], BF16)
        ids_i = sb("ids_i", [HB, 2, 2, P], I32)
        ids_f = sb("ids_f", [HB, 2, 2, P])
        w_tb = sb("w_tb", [HB, 2, P])
        mask_tb = sb("mask_tb", [HB, 2, 2, P], BF16)
        ends_b = sb("ends_b", [HB, 2, ET])
        reach = sb("reach", [HB, 2, 2, ET])
        srcP = sb("srcP", [P, ET])
        dstP = sb("dstP", [P, ET])
        wP = sb("wP", [P, ET])
        hilo_i = sb("hilo_i", [P, 4, ET], I32)
        hilo = sb("hilo", [P, 4, ET])
        idx_src = sb("idx_src", [P, ET], I32)
        idx_dst = sb("idx_dst", [P, ET], I32)
        idx_srcn = sb("idx_srcn", [P, ET], I32)
        idx_dstn = sb("idx_dstn", [P, ET], I32)
        idx_lvl = sb("idx_lvl", [P, ET], I32)
        idx_out = sb("idx_out", [P, ET], I32)
        iota_i = sb("iota_i", [P, HI], I32)
        iota_h = sb("iota_h", [P, HI], F16)
        edge_no = sb("edge_no", [P, ET])
        edge_no_i = sb("edge_no_i", [P, ET], I32)
        info = sb("info", [P, 2, ET, 4])
        w_gcn = sb("w_gcn", [P, ET])
        w_mean = sb("w_mean", [P, ET])
        w_light = sb("w_light", [P, ET])
        tmp = sb("tmp", [P, 3, ET])
        small = sb("small", [P, US, 4, G])
        ring_idx = sb("ring_idx", [P, US, G], I32)
        ends = sb("ends_sb", [P, ET, 2])
        buf = [sb(f"buf{j}", [P, NBUF, GW]) for j in range(US)]
        extra = sb("extra", [P, 6, GW])
        carry_in = [sb(f"carry_in{j}", [6, 2, GW], BF16) for j in range(US)]
        psum = root.enter_context(nc.psum_tensor("psum", [P, US, 1024], F32))

        def edge_rows(ap, g):
            return ap[bass.ds(g * GW, GW), :].rearrange("(k p) d -> p k d", p=P)

        with ExitStack() as ctx:
            sem = phase_semaphores(nc, ctx, "")

            w_in, col_in, ids_in = sem("w_in"), sem("col_in"), sem("ids_in")
            filled, pool_done = sem("filled"), sem("pool_done")
            pe_done, act_done, dve_done = sem("pe_done"), sem("act_done"), sem("dve_done")
            ends_out, ends_in, tb_out = sem("ends_out"), sem("ends_in"), sem("tb_out")
            split, split_out, split_in = sem("split"), sem("split_out"), sem("split_in")
            FULL = ET - 1 - HB
            block = ctx.enter_context(nc.Block())

            @block.sync
            def _(sp):
                sp.wait_ge(filled, 3)
                for a, s in enumerate((src, dst)):
                    sp.dma_start(ids_i[:, a, 0, :], s[0:HB * P].rearrange("(t p) -> t p", p=P)).then_inc(ids_in, 16)
                    sp.dma_start(ids_i[0:FULL, a, 1, :],
                                 s[HB * P:(ET - 1) * P].rearrange("(t p) -> t p", p=P)).then_inc(ids_in, 16)
                    sp.dma_start(ids_i[FULL:HB, a, 1, 0:TAIL],
                                 s[(ET - 1) * P:E].rearrange("(t p) -> t p", t=1)).then_inc(ids_in, 16)
                ew = edge_weight
                sp.dma_start(w_tb[:, 0, :], ew[0:HB * P].rearrange("(t p) -> t p", p=P)).then_inc(ids_in, 16)
                sp.dma_start(w_tb[0:FULL, 1, :],
                             ew[HB * P:(ET - 1) * P].rearrange("(t p) -> t p", p=P)).then_inc(ids_in, 16)
                sp.dma_start(w_tb[FULL:HB, 1, 0:TAIL],
                             ew[(ET - 1) * P:E].rearrange("(t p) -> t p", t=1)).then_inc(ids_in, 16)
                for k, w in enumerate((W_obj, W_rel, W1_self, W1_neigh, W2_self, W2_neigh)):
                    sp.dma_start(w_raw[:, k, :], w).then_inc(w_in, 16)
                sp.dma_start(cols[:, 0:2], ln_gamma.rearrange("l d -> d l")).then_inc(col_in, 16)
                sp.dma_start(cols[:, 2:4], ln_beta.rearrange("l d -> d l")).then_inc(col_in, 16)
                sp.dma_start(cols[:, 4:5], b1.rearrange("(d a) -> d a", a=1)).then_inc(col_in, 16)
                sp.dma_start(cols[:, 5:6], b2.rearrange("(d a) -> d a", a=1)).then_inc(col_in, 16)
                sp.dma_start(bias_row[:, 0, :], b_obj.rearrange("(a d) -> a d", a=1)).then_inc(col_in, 16)
                sp.dma_start(bias_row[:, 1, :], b_rel.rearrange("(a d) -> a d", a=1)).then_inc(col_in, 16)
                sp.wait_ge(dve_done, 4)
                for b in range(2):
                    sp.dma_start(dst_flat[0:1, b * HB * P:(b + 1) * HB * P].rearrange("a (t p) -> (a t) p", p=P),
                                 ids_f[:, 1, b, :]).then_inc(tb_out, 16)
                    for side, at in enumerate((0, P - 1)):
                        lo = side * ET + b * HB
                        sp.dma_start(ends_dram[0:1, lo:lo + HB].rearrange("a (t o) -> (a t) o", o=1),
                                     ids_f[:, 1, b, at:at + 1]).then_inc(ends_out, 16)
                sp.wait_ge(ends_out, 64)
                sp.dma_start(ends_b.rearrange("t s n -> t (s n)"),
                             ends_dram.to_broadcast([HB, 2 * ET])).then_inc(ends_in, 16)
                sp.wait_ge(dve_done, 8)
                for row in range(6):
                    for b in range(2):
                        sp.dma_start(
                            ends_mask[row:row + 1, b * HB * P:(b + 1) * HB * P].rearrange("a (t p) -> (a t) p", p=P),
                            mask_tb[:, row // 3, b, :]).then_inc(tb_out, 16)
                sp.wait_ge(split, 6)
                sp.dma_start(bias_dram.rearrange("k (b d) -> (k b) d", d=P).unsqueeze(0),
                             bias_parts.rearrange("a k b d -> a (k b) d")).then_inc(split_out, 16)
                sp.wait_ge(split_out, 16)
                sp.dma_start(bias3.rearrange("k b d -> k (b d)"), bias_dram).then_inc(split_in, 16)
                sp.wait_ge(split_in, 16)
                sp.wait_ge(tb_out, 32 + 192)

            @block.gpsimd
            def _(pool):
                pool.iota(ids_i[:, :, :, :], [[0, 2 * 2 * P]], base=PAD, channel_multiplier=0).then_inc(filled, 1)
                pool.memset(w_tb[:, :, :], 0.0).then_inc(filled, 1)
                pool.memset(ones3[:, :], 1.0).then_inc(filled, 1)
                pool.memset(ones_sq[:, :], 1.0).then_inc(pool_done, 1)
                pool.memset(ident[:, :], 0.0).then_inc(pool_done, 1)
                pool.wait_ge(pool_done, 2)
                pool.affine_select(out=ident[:, :], in_=ident[:, :], compare_op=ALU.not_equal, fill=1.0, base=0,
                                   pattern=[[-1, P]], channel_multiplier=1).then_inc(pool_done, 1)
                pool.affine_select(out=upper[:, :], in_=ones_sq[:, :], compare_op=ALU.is_gt, fill=0.0, base=0,
                                   pattern=[[1, P]], channel_multiplier=-1).then_inc(pool_done, 1)
                pool.iota(iota_i[:, :], [[1, HI]], base=0, channel_multiplier=0).then_inc(pool_done, 1)
                pool.iota(edge_no_i[:, :], [[P, ET]], base=0, channel_multiplier=1).then_inc(pool_done, 1)
                pool.memset(eps_t[:, 0:1], EPS).then_inc(pool_done, 1)
                pool.memset(eps_t[:, 1:2], EPS * EPS).then_inc(pool_done, 1)
                pool.wait_ge(dve_done, 12)
                for b in range(2):
                    pool.affine_select(out=reach[:, 0, b, :], in_=reach[:, 0, b, :], compare_op=ALU.is_gt, fill=0.0,
                                       base=-b * HB, pattern=[[1, ET]], channel_multiplier=-1).then_inc(pool_done, 1)
                    pool.affine_select(out=reach[:, 1, b, :], in_=reach[:, 1, b, :], compare_op=ALU.is_gt, fill=0.0,
                                       base=b * HB, pattern=[[-1, ET]], channel_multiplier=1).then_inc(pool_done, 1)

            @block.tensor
            def _(pe):
                pe.wait_ge(pool_done, 3)
                pe.wait_ge(w_in, 96)
                for k in range(4):
                    pe.transpose(psum[:, 0, k * P:(k + 1) * P], w_raw[:, k, :], ident[:, :])
                pe.wait_ge(dve_done, 5)
                for k in range(4, 6):
                    pe.matmul(psum[:, 0, k * P:(k + 1) * P], w_raw[:, k, :], center[:, :], start=True, stop=True)
                pe.wait_ge(col_in, 96)
                pe.matmul(psum[0:1, 1, 0:P], cols[:, 5:6], center[:, :], start=True, stop=True).then_inc(pe_done, 1)
                for b in range(2):
                    pe.transpose(psum[:, 2, b * HB:(b + 1) * HB], ids_f[:, 0, b, :], ident[0:HB, 0:HB])
                for b in range(2):
                    pe.transpose(psum[:, 2, 512 + b * HB:512 + (b + 1) * HB], ids_f[:, 1, b, :], ident[0:HB, 0:HB])
                for b in range(2):
                    mm = pe.transpose(psum[:, 3, b * HB:(b + 1) * HB], w_tb[:, b, :], ident[0:HB, 0:HB])
                mm.then_inc(pe_done, 1)

            @block.scalar
            def _(act):
                act.wait_ge(pe_done, 1)
                act.copy(w_use.rearrange("p k d -> p (k d)"), psum[:, 0, 0:6 * P]).then_inc(act_done, 1)
                act.copy(bias_f[:, 1, :], psum[0:1, 1, 0:P]).then_inc(act_done, 1)

            @block.vector
            def _(dve):
                dve.wait_ge(ids_in, 144)
                for a in range(2):
                    for b in range(2):
                        dve.tensor_copy(ids_f[:, a, b, :], ids_i[:, a, b, :]).then_inc(dve_done, 1)
                dve.wait_ge(pool_done, 3)
                dve.tensor_scalar(center[:, :], ident[:, :], 1.0 / P, None, ALU.subtract).then_inc(dve_done, 1)
                dve.wait_ge(dve_done, 4)
                for b in range(2):
                    for side, at in enumerate((0, P - 1)):
                        ins = dve.tensor_scalar(mask_tb[:, side, b, :], ids_f[:, 1, b, :],
                                                ids_f[:, 1, b, at:at + 1], None, ALU.is_equal)
                        if (b, side) != (0, 0):
                            ins.then_inc(dve_done, 1)
                dve.wait_ge(ends_in, 16)
                for b in range(2):
                    for side, at in enumerate((P - 1, 0)):
                        dve.tensor_scalar(reach[:, side, b, :], ends_b[:, side, :], ids_f[:, 1, b, at:at + 1],
                                          None, ALU.is_equal).then_inc(dve_done, 1)
                dve.wait_ge(pool_done, 8)
                dve.tensor_copy(iota_h[:, :], iota_i[:, :]).then_inc(dve_done, 1)
                dve.tensor_copy(edge_no[:, :], edge_no_i[:, :]).then_inc(dve_done, 1)
                dve.wait_ge(col_in, 96)
                dve.scalar_tensor_tensor(out=bias_f[:, 0, :], in0=bias_row[:, 0, :], scalar=2.0, in1=bias_row[:, 1, :],
                                         op0=ALU.mult, op1=ALU.add).then_inc(dve_done, 1)
                dve.wait_ge(pe_done, 2)
                dve.tensor_copy(srcP[:, :], psum[:, 2, 0:ET]).then_inc(dve_done, 1)
                dve.tensor_copy(dstP[:, :], psum[:, 2, 512:512 + ET]).then_inc(dve_done, 1)
                dve.tensor_copy(wP[:, :], psum[:, 3, 0:ET]).then_inc(dve_done, 1)
                dve.wait_ge(dve_done, 18)
                dve.tensor_copy(idx_srcn[:, :], srcP[:, :]).then_inc(dve_done, 1)
                dve.tensor_copy(idx_dstn[:, :], dstP[:, :]).then_inc(dve_done, 1)
                dve.tensor_scalar(idx_src[:, :], srcP[:, :], float(N - 1), None, ALU.min).then_inc(dve_done, 1)
                dve.tensor_scalar(idx_dst[:, :], dstP[:, :], float(N - 1), None, ALU.min).then_inc(dve_done, 1)
                dve.wait_ge(dve_done, 20)
                for a, ids in enumerate((idx_srcn, idx_dstn)):
                    dve.tensor_scalar(hilo_i[:, 2 * a, :], ids[:, :], LO.bit_length() - 1, None,
                                      ALU.logical_shift_right).then_inc(dve_done, 1)
                    dve.tensor_scalar(hilo_i[:, 2 * a + 1, :], ids[:, :], LO - 1, None,
                                      ALU.bitwise_and).then_inc(dve_done, 1)
                dve.wait_ge(dve_done, 26)
                dve.tensor_copy(hilo.rearrange("p a t -> p (a t)"),
                                hilo_i.rearrange("p a t -> p (a t)")).then_inc(dve_done, 1)
                dve.wait_ge(act_done, 2)
                dve.wait_ge(dve_done, 15)
                for k in range(3):
                    if k:
                        dve.wait_ge(split, 2 * k)
                    dve.tensor_copy(bias_parts[:, k, :, :], bias_f[:, :, :]).then_inc(split, 1)
                    dve.wait_ge(split, 2 * k + 1)
                    dve.tensor_tensor(bias_f[:, :, :], bias_f[:, :, :], bias_parts[:, k, :, :], ALU.subtract
                                      ).then_inc(split, 1)

        DENSE_IT = -(-N // ROWS)
        SRC_IT = EP // ROWS
        assert SRC_IT * ROWS == EP
        with ExitStack() as ctx:
            sem = phase_semaphores(nc, ctx, "")

            HR = 4
            onehot = ctx.enter_context(nc.sbuf_tensor("onehot", [P, HR, HI + LO], F16))
            flat3 = buf[3].rearrange("p b w -> p (b w)")
            node = flat3[0:HP, 0:16 * LO].rearrange("p (b l f) -> p b l f", b=4, f=4)
            incl = flat3[0:HP, 16 * LO:20 * LO].rearrange("p (b l) -> p b l", b=4)
            tot = ctx.enter_context(nc.sbuf_tensor("tot", [HP, 8], F32))
            ring_info = ctx.enter_context(nc.sbuf_tensor("ring_info", [P, 2, G, 4], F32))
            hot_ready, hot_used = sem("hot_ready"), sem("hot_used")
            counted, tab_dve, tab_pe, node_out = sem("counted"), sem("tab_dve"), sem("tab_pe"), sem("node_out")
            dstrow_in, match_ready = [sem(f"dstrow_in{p}") for p in range(2)], sem("match_ready")
            match_out = [sem(f"match_out{p}") for p in range(2)]
            idx_copied, ring_free = sem("idx_copied"), sem("ring_free")
            rows_in = [sem(f"rows_in{p}") for p in range(2)]
            rows_out = [sem(f"rows_out{p}") for p in range(2)]
            src_all = sem("src_all")
            info_in = [sem(f"info_in{p}") for p in range(2)]
            info_copied = sem("info_copied")

            def slots(name):
                return [sem(f"{name}{j}") for j in range(US)]

            D_STAGES = ("turn_x copy_x centre1 square1 sum1 root1 norm1 turn1 exp1 fold1 elu1 "
                        "centre2 square2 sum2 root2 norm2 turn2 exp2 fold2 elu2 "
                        "centre3 square3 sum3 root3 norm3 turn3 copy3 hidden relu sage add square4 sum4 root4 norm4"
                        ).split()
            D_PE = Steps("turn_x centre1 turn1 centre2 turn2 centre3 turn3 hidden sage")
            D_ACT = Steps("copy_x square1 log1 root1 exp1 affine1 fold1 square2 log2 root2 exp2 affine2 fold2 "
                          "square3 log3 root3 copy3 relu square4 log4 root4")
            D_DVE = Steps("sum1 norm1 elu1 sum2 norm2 elu2 sum3 norm3 add sum4 norm4")
            d_pe, d_act, d_dve, x_in, out_stored = (slots(n) for n in ("d_pe", "d_act", "d_dve", "x_in", "out_stored"))
            S_STAGES = ("turn_x copy_x centre1 square1 sum1 root1 norm1 turn1 exp1 fold1 elu1 turn_y rows_y "
                        "centre2 square2 sum2 root2 norm2 turn2 exp2 fold2 elu2 "
                        "centre3 square3 sum3 root3 norm_x1 norm3 turn3 copy3 hidden relu turn_h rows_h sage add "
                        "square4 sum4 root4 norm4").split()
            S_PE = Steps("turn_x centre1 turn1 turn_y centre2 turn2 centre3 turn3 hidden turn_h sage")
            S_ACT = Steps("copy_x square1 log1 root1 exp1 affine1 fold1 rows_y square2 log2 root2 exp2 affine2 fold2 "
                          "square3 log3 log_x1 root3 root_x1 copy3 relu rows_h square4 log4 root4")
            S_DVE = Steps("sum1 norm1 elu1 sum2 norm2 elu2 sum3 norm_x1 norm3 add sum4 norm4")
            s_pe, s_act, s_dve, s_in = (slots(n) for n in ("s_pe", "s_act", "s_dve", "s_in"))
            y1_out, x1_out, x2_out, h1_out, x3_out = (slots(n) for n in ("y1_out", "x1_out", "x2_out", "h1_out", "x3_out"))
            D_LAG, S_LAG = len(D_STAGES) // US, len(S_STAGES) // US
            block = ctx.enter_context(nc.Block())

            def B(j, k):
                return buf[j][:, k, :]

            def ps(j):
                return psum[:, j, 0:GW]

            def wide(ap):
                return ap.rearrange("p (k d) -> p k d", d=P)

            def flat_rows(ap, lo):
                return ap[bass.ds(lo, GW), :].rearrange("(p k) d -> p (k d)", p=P)

            def node_rows(ap, it, j):
                last = isinstance(it, int) and it == DENSE_IT - 1
                return flat_rows(ap, (N - ROWS if last else it * ROWS) + j * GW)

            def dense_loop(engine, body):
                staggered(engine, DENSE_IT, len(D_STAGES), D_LAG, body, tail=2)

            @block.sync
            def _(sp):
                def load_dst(g, p):
                    sp.dma_start(extra[:, p, :], dst_flat[0:1, bass.ds(g * GW, GW)].to_broadcast([P, GW])
                                 ).then_inc(dstrow_in[p], 16)

                def store_match(g, p):
                    sp.dma_start(match_dram[bass.ds(g, 1)].rearrange("a p w -> (a p) w"), extra[:, 2 + p, :]
                                 ).then_inc(match_out[p], 16)

                for p in range(2):
                    load_dst(p, p)
                with sp.Fori(0, NG // 2 - 1) as i:
                    for p in range(2):
                        sp.wait_ge(match_ready, 2 * i + p + 1)
                        store_match(2 * i + p, p)
                        load_dst(2 * i + 2 + p, p)
                for p in range(2):
                    sp.wait_ge(match_ready, NG - 1 + p)
                    store_match(NG - 2 + p, p)
                sp.wait_ge(tab_dve, 17)
                sp.dma_start(node_dram.rearrange("(b p l) f -> p b (l f)", p=HP, l=LO),
                             node.rearrange("p b l f -> p b (l f)")).then_inc(node_out, 16)

                def load_x(it, j):
                    sp.dma_start(B(j, 0), node_rows(x, it, j)).then_inc(x_in[j], 16)

                for j in range(US):
                    if j == 3:
                        sp.wait_ge(node_out, 16)
                    load_x(0, j)

                def dense(stage, it, j):
                    last = isinstance(it, int) and it == DENSE_IT - 1
                    if stage == D_STAGES.index("copy_x") and not last:
                        sp.wait_ge(d_pe[j], D_PE.at(it, "turn_x"))
                        load_x(it + 1, j)
                    if stage == D_STAGES.index("norm4"):
                        sp.wait_ge(d_dve[j], D_DVE.at(it, "norm4"))
                        if last:
                            for k in range(US):
                                sp.wait_ge(out_stored[k], 16 * it)
                        sp.dma_start(node_rows(out, it, j), B(j, 5)).then_inc(out_stored[j], 16)

                dense_loop(sp, dense)

                sp.wait_ge(src_all, 1)

                def load_s(it, j):
                    sp.dma_start(B(j, 0), flat_rows(src_x, it * ROWS + j * GW)).then_inc(s_in[j], 16)

                def store_s(l, it, j, k, done):
                    sp.dma_start(flat_rows(level_rows[l], EP + (it * ROWS + j * GW)), B(j, k)).then_inc(done[j], 16)

                for j in range(US):
                    load_s(0, j)

                def source(stage, it, j):
                    name = S_STAGES[stage]
                    if name == "copy_x" and not (isinstance(it, int) and it == SRC_IT - 1):
                        sp.wait_ge(s_pe[j], S_PE.at(it, "turn_x"))
                        load_s(it + 1, j)
                    if name == "rows_y":
                        sp.wait_ge(s_act[j], S_ACT.at(it, "rows_y"))
                        store_s(1, it, j, 5, y1_out)
                    if name == "norm3":
                        sp.wait_ge(s_dve[j], S_DVE.at(it, "norm3"))
                        store_s(2, it, j, 2, x1_out)
                        store_s(3, it, j, 3, x2_out)
                    if name == "rows_h":
                        sp.wait_ge(s_act[j], S_ACT.at(it, "rows_h"))
                        store_s(4, it, j, 5, h1_out)
                    if name == "norm4":
                        sp.wait_ge(s_dve[j], S_DVE.at(it, "norm4"))
                        store_s(5, it, j, 4, x3_out)

                staggered(sp, SRC_IT, len(S_STAGES), S_LAG, source)
                for j in range(US):
                    sp.wait_ge(out_stored[j], 16 * DENSE_IT)
                    for s in (y1_out, x1_out, x2_out, h1_out, x3_out):
                        sp.wait_ge(s[j], 16 * SRC_IT)
                for p in range(2):
                    sp.wait_ge(match_out[p], 8 * NG)

            @block.gpsimd
            def _(pool):
                for a, (ids, table) in enumerate(((idx_src, src_x), (idx_dst, dst_x))):
                    def pair(i):
                        n = a * (NG // 2) + i
                        for p in range(2):
                            pool.tensor_copy(ring_idx[:, p, :], ids[:, bass.ds((2 * i + p) * G, G)]
                                             ).then_inc(idx_copied, 1)
                            pool.wait_ge(idx_copied, 2 * n + p + 1)
                            wait(pool, rows_out[p], 16 * n)
                            pool.sem_inc(ring_free, 1)
                            for k in range(G):
                                pool.indirect_dma_start(
                                    out=extra[:, 4 + p, k * P:(k + 1) * P], out_offset=None, in_=x,
                                    in_offset=bass.IndirectOffsetOnAxis(ap=ring_idx[:, p, k:k + 1], axis=0),
                                ).then_inc(rows_in[p], 16)
                        for p in range(2):
                            pool.wait_ge(rows_in[p], 16 * G * n + 16 * G)
                            pool.dma_start(edge_rows(table, 2 * i + p), wide(extra[:, 4 + p, :])
                                           ).then_inc(rows_out[p], 16)
                    pair(0)
                    with pool.Fori(1, NG // 2) as i:
                        pair(i)
                    for p in range(2):
                        pool.wait_ge(rows_out[p], 8 * NG * (a + 1))
                    if a == 0:
                        pool.engine_nop().then_inc(src_all, 1)
                pool.wait_ge(node_out, 16)
                for a, ids in enumerate((idx_srcn, idx_dstn)):
                    with pool.Fori(0, NG // 2) as i:
                        for p in range(2):
                            n = (2 + a) * (NG // 2) + i
                            pool.tensor_copy(ring_idx[:, p, :], ids[:, bass.ds((2 * i + p) * G, G)]
                                             ).then_inc(idx_copied, 1)
                            pool.wait_ge(idx_copied, 2 * n + p + 1)
                            pool.sem_inc(ring_free, 1)
                            for k in range(G):
                                pool.indirect_dma_start(
                                    out=ring_info[:, p, k, :], out_offset=None, in_=node_dram,
                                    in_offset=bass.IndirectOffsetOnAxis(ap=ring_idx[:, p, k:k + 1], axis=0),
                                ).then_inc(info_in[p], 16)
                        for p in range(2):
                            m = a * (NG // 2) + i
                            pool.wait_ge(info_in[p], 16 * G * m + 16 * G)
                            pool.tensor_copy(info[:, a, bass.ds((2 * i + p) * G, G), :], ring_info[:, p, :, :]
                                             ).then_inc(info_copied, 1)
                            pool.wait_ge(info_copied, 2 * m + p + 1)
                            pool.sem_inc(ring_free, 1)

            @block.tensor
            def _(pe):
                def bank(a, b):
                    return psum[0:HP, 2 * a + b // 2, (b % 2) * 512:(b % 2) * 512 + LO]

                for a in range(2):
                    def count(i, q, first):
                        pe.wait_ge(hot_ready, i * HR + (a * ET + q + 1))
                        for b in range(4):
                            mm = pe.matmul(bank(a, b), onehot[:, q, b * HP:(b + 1) * HP], onehot[:, q, HI:HI + LO],
                                           start=first, stop=False)
                        mm.then_inc(hot_used, 1)
                    for q in range(HR):
                        count(0, q, q == 0)
                    with pe.Fori(1, ET // HR) as i:
                        for q in range(HR):
                            count(i, q, False)
                pe.wait_ge(tab_dve, 1)
                for a in range(2):
                    for b in range(4):
                        mm = pe.matmul(bank(a, b), onehot[:, 0, b * HP:(b + 1) * HP], onehot[:, 1, HI:HI + LO],
                                       start=False, stop=True)
                mm.then_inc(counted, 1)
                pe.wait_ge(tab_dve, 12)
                pe.matmul(psum[0:HP, 0, 0:4], upper[0:HP, 0:HP], tot[:, 0:4], start=True, stop=False)
                pe.matmul(psum[0:HP, 0, 0:4], ones_sq[0:HP, 0:HP], tot[:, 4:8], start=False,
                          stop=True).then_inc(tab_pe, 1)
                pe.wait_ge(tab_dve, 17)

                I, C = ident[:, :], center[:, :]

                def turn(j, k):
                    for t in range(G):
                        mm = pe.transpose(ps(j)[:, t * P:(t + 1) * P], B(j, k)[:, t * P:(t + 1) * P], I)
                    return mm

                def times(j, terms, bias=False):
                    for t in range(G):
                        o = ps(j)[:, t * P:(t + 1) * P]
                        for n, (k, m) in enumerate(terms):
                            mm = pe.matmul(o, B(j, k)[:, t * P:(t + 1) * P], m, start=(n == 0),
                                           stop=(n == len(terms) - 1 and not bias))
                        if bias:
                            mm = pe.matmul(o, ones3[:, :], bias3[:, 1, :], start=False, stop=True)
                    return mm

                def hidden(j):
                    for lo, hi in ((0, 512), (512, GW)):
                        mm = pe.matmul(ps(j)[:, lo:hi], w_use[:, 2, :], B(j, 1)[:, lo:hi], start=True, stop=True)
                    return mm

                def chain(stage, it, j, PE_, ACT_, DVE_, pe_s, act_s, dve_s, arrived):
                    mm = None
                    if stage == "turn_x":
                        pe.wait_ge(arrived[j], 16 * it + 16)
                        wait(pe, dve_s[j], it * DVE_.n)
                        mm = turn(j, 0)
                    elif stage == "centre1":
                        pe.wait_ge(act_s[j], ACT_.at(it, "copy_x"))
                        mm = times(j, [(1, C)])
                    elif stage in ("turn1", "turn2", "turn3"):
                        pe.wait_ge(dve_s[j], DVE_.at(it, "norm" + stage[4]))
                        mm = turn(j, 3)
                    elif stage == "turn_y":
                        pe.wait_ge(dve_s[j], DVE_.at(it, "elu1"))
                        mm = turn(j, 4)
                    elif stage == "centre2":
                        pe.wait_ge(dve_s[j], DVE_.at(it, "elu1"))
                        if "rows_y" in ACT_.names:
                            pe.wait_ge(act_s[j], ACT_.at(it, "rows_y"))
                        mm = times(j, [(4, C)])
                    elif stage == "centre3":
                        pe.wait_ge(dve_s[j], DVE_.at(it, "elu2"))
                        mm = times(j, [(1, C), (4, C)])
                    elif stage == "hidden":
                        pe.wait_ge(act_s[j], ACT_.at(it, "copy3"))
                        mm = hidden(j)
                    elif stage == "turn_h":
                        pe.wait_ge(act_s[j], ACT_.at(it, "relu"))
                        mm = turn(j, 4)
                    elif stage == "sage":
                        pe.wait_ge(act_s[j], ACT_.at(it, "rows_h" if "rows_h" in ACT_.names else "relu"))
                        mm = times(j, [(4, w_use[:, 4, :])], bias=True)
                    if mm is not None:
                        mm.then_inc(pe_s[j], 1)

                dense_loop(pe, lambda s, it, j: chain(D_STAGES[s], it, j, D_PE, D_ACT, D_DVE, d_pe, d_act, d_dve, x_in))
                for j in range(US):
                    pe.wait_ge(d_dve[j], D_DVE.n * DENSE_IT)
                staggered(pe, SRC_IT, len(S_STAGES), S_LAG, lambda s, it, j: chain(
                    S_STAGES[s], it, j, S_PE, S_ACT, S_DVE, s_pe, s_act, s_dve, s_in))

            @block.scalar
            def _(act):
                act.preload_act_table_set("natural_log_exp_and_others")

                def chain(stage, it, j, PE_, ACT_, DVE_, pe_s, act_s, dve_s):
                    source = "turn_y" in PE_.names
                    k = stage[-1]

                    def step(ins):
                        ins.then_inc(act_s[j], 1)

                    if stage == "copy_x":
                        act.wait_ge(pe_s[j], PE_.at(it, "turn_x"))
                        if source:
                            wait(act, h1_out[j], 16 * it)
                        step(act.copy(B(j, 1), ps(j)))
                    elif stage in ("square1", "square2", "square3"):
                        act.wait_ge(pe_s[j], PE_.at(it, "centre" + k))
                        step(act.activation(B(j, 2), ps(j), ACT.Square))
                    elif stage == "square4":
                        act.wait_ge(dve_s[j], DVE_.at(it, "add"))
                        if source:
                            act.wait_ge(x1_out[j], 16 * it + 16)
                        step(act.activation(B(j, 2), B(j, 4), ACT.Square))
                    elif stage.startswith("root"):
                        twice = k == "3" or (k == "4" and not source)
                        act.wait_ge(dve_s[j], DVE_.at(it, "sum" + k))
                        step(act.activation(small[:, j, 1, :], small[:, j, 0, :], ACT.Ln,
                                            bias=eps_t[:, 1:2] if twice else eps_t[:, 0:1],
                                            scale=(1.0 + EPS if twice else 1.0) / P))
                        if source and k == "3":
                            step(act.activation(small[:, j, 3, :], small[:, j, 0, :], ACT.Ln, bias=eps_t[:, 0:1],
                                                scale=1.0 / P))
                        act.wait_ge(act_s[j], ACT_.at(it, "log" + k))
                        step(act.activation(small[:, j, 2, :], small[:, j, 1, :], ACT.Exp, scale=-0.5))
                        if source and k == "3":
                            act.wait_ge(act_s[j], ACT_.at(it, "log_x1"))
                            step(act.activation(small[:, j, 3, :], small[:, j, 3, :], ACT.Exp, scale=-0.5))
                    elif stage in ("exp1", "exp2"):
                        l = int(k) - 1
                        act.wait_ge(pe_s[j], PE_.at(it, "turn" + k))
                        affine = dict(bias=cols[:, 2 + l:3 + l], scale=cols[:, l:l + 1])
                        step(act.activation(B(j, 2), ps(j), ACT.Exp, **affine))
                        step(act.activation(B(j, 3), ps(j), ACT.Identity, **affine))
                    elif stage in ("fold1", "fold2"):
                        act.wait_ge(act_s[j], ACT_.at(it, "exp" + k))
                        step(act.activation(B(j, 2), B(j, 2), ACT.Relu, bias=1.0, scale=-1.0))
                    elif stage == "rows_y":
                        act.wait_ge(pe_s[j], PE_.at(it, "turn_y"))
                        step(act.copy(B(j, 5), ps(j)))
                    elif stage == "copy3":
                        act.wait_ge(pe_s[j], PE_.at(it, "turn3"))
                        step(act.copy(B(j, 1), ps(j)))
                    elif stage == "relu":
                        act.wait_ge(pe_s[j], PE_.at(it, "hidden"))
                        step(act.activation(B(j, 4), ps(j), ACT.Relu, bias=cols[:, 4:5]))
                    elif stage == "rows_h":
                        act.wait_ge(pe_s[j], PE_.at(it, "turn_h"))
                        act.wait_ge(y1_out[j], 16 * it + 16)
                        step(act.copy(B(j, 5), ps(j)))

                dense_loop(act, lambda s, it, j: chain(D_STAGES[s], it, j, D_PE, D_ACT, D_DVE, d_pe, d_act, d_dve))
                for j in range(US):
                    act.wait_ge(out_stored[j], 16 * DENSE_IT)
                staggered(act, SRC_IT, len(S_STAGES), S_LAG, lambda s, it, j: chain(
                    S_STAGES[s], it, j, S_PE, S_ACT, S_DVE, s_pe, s_act, s_dve))

            @block.vector
            def _(dve):
                for a in range(2):
                    def hot(i, q, wait):
                        t = i * HR + q
                        if wait:
                            dve.wait_ge(hot_used, a * ET + t - HR + 1)
                        dve.tensor_scalar(onehot[:, q, 0:HI], iota_h[:, :], hilo[:, 2 * a, bass.ds(t, 1)], None,
                                          ALU.is_equal)
                        dve.tensor_scalar(onehot[:, q, HI:HI + LO], iota_h[:, 0:LO],
                                          hilo[:, 2 * a + 1, bass.ds(t, 1)], None, ALU.is_equal
                                          ).then_inc(hot_ready, 1)
                    for q in range(HR):
                        hot(0, q, a > 0)
                    with dve.Fori(1, ET // HR) as i:
                        for q in range(HR):
                            hot(i, q, True)
                dve.wait_ge(hot_used, 2 * ET)
                dve.memset(onehot[:, 1, HI:HI + LO], 0.0).then_inc(tab_dve, 1)

                def matching(i):
                    for p in range(2):
                        dve.wait_ge(dstrow_in[p], 16 * i + 16)
                        wait(dve, match_out[p], 16 * i)
                        dve.tensor_tensor(wide(extra[:, 2 + p, :]), wide(extra[:, p, :]),
                                          dstP[:, bass.ds((2 * i + p) * G, G)].unsqueeze(2).to_broadcast([P, G, P]),
                                          ALU.is_equal).then_inc(match_ready, 1)

                matching(0)
                with dve.Fori(1, NG // 2) as i:
                    matching(i)
                dve.wait_ge(counted, 1)
                for a, f in enumerate((2, 1)):
                    for h in range(2):
                        dve.tensor_copy(node[:, 2 * h:2 * h + 2, :, f],
                                        psum[0:HP, 2 * a + h, :].rearrange("p (b w) -> p b w", b=2)[:, :, 0:LO]
                                        ).then_inc(tab_dve, 1)
                dve.memset(node[:, :, :, 3], 0.0).then_inc(tab_dve, 1)
                dve.wait_ge(tab_dve, 6)
                for b in range(4):
                    dve.tensor_tensor_scan(incl[:, b, :], node[:, b, :, 1], node[:, b, :, 3], 0.0, ALU.add, ALU.add
                                           ).then_inc(tab_dve, 1)
                dve.wait_ge(tab_dve, 10)
                dve.tensor_copy(tot[:, 0:4], incl[:, :, LO - 1])
                dve.memset(tot[:, 4:5], 0.0)
                dve.tensor_copy(tot[:, 5:6], incl[:, 0, LO - 1:LO])
                dve.tensor_tensor(tot[:, 6:7], incl[:, 0, LO - 1:LO], incl[:, 1, LO - 1:LO], ALU.add
                                  ).then_inc(tab_dve, 1)
                dve.wait_ge(tab_dve, 11)
                dve.tensor_tensor(tot[:, 7:8], tot[:, 6:7], incl[:, 2, LO - 1:LO], ALU.add
                                  ).then_inc(tab_dve, 1)
                dve.wait_ge(tab_pe, 1)
                dve.tensor_copy(tot[:, 0:4], psum[0:HP, 0, 0:4]).then_inc(tab_dve, 1)
                dve.wait_ge(tab_dve, 13)
                for b in range(4):
                    dve.scalar_tensor_tensor(out=node[:, b, :, 0], in0=incl[:, b, :], scalar=tot[:, b:b + 1],
                                             in1=node[:, b, :, 1], op0=ALU.add, op1=ALU.subtract
                                             ).then_inc(tab_dve, 1)

                def chain(stage, it, j, PE_, ACT_, DVE_, pe_s, act_s, dve_s):
                    source = "turn_y" in PE_.names
                    k = stage[-1]

                    def step(ins):
                        ins.then_inc(dve_s[j], 1)

                    def scaled(o, rows, r):
                        return dve.tensor_tensor(wide(o), wide(rows),
                                                 small[:, j, r, :].unsqueeze(2).to_broadcast([P, G, P]), ALU.mult)

                    if stage.startswith("sum"):
                        if stage == "sum1":
                            for s in ((x2_out, x3_out) if source else (out_stored,)):
                                wait(dve, s[j], 16 * it)
                        dve.wait_ge(act_s[j], ACT_.at(it, "square" + k))
                        step(dve.tensor_reduce(small[:, j, 0, :], wide(B(j, 2)), AX_X, ALU.add))
                    elif stage in ("norm1", "norm2", "norm3"):
                        dve.wait_ge(act_s[j], ACT_.at(it, "root" + k))
                        step(scaled(B(j, 3), ps(j), 2))
                    elif stage == "norm_x1":
                        dve.wait_ge(act_s[j], ACT_.at(it, "root_x1"))
                        step(scaled(B(j, 2), ps(j), 3))
                    elif stage == "norm4":
                        dve.wait_ge(act_s[j], ACT_.at(it, "root4"))
                        step(scaled(B(j, 4 if source else 5), B(j, 4), 2))
                    elif stage in ("elu1", "elu2"):
                        dve.wait_ge(act_s[j], ACT_.at(it, "fold" + k))
                        step(dve.scalar_tensor_tensor(out=B(j, 4), in0=B(j, 2), scalar=-1.0, in1=B(j, 3),
                                                      op0=ALU.mult, op1=ALU.max))
                    elif stage == "add":
                        dve.wait_ge(pe_s[j], PE_.at(it, "sage"))
                        step(dve.tensor_tensor(B(j, 4), ps(j), B(j, 3), ALU.add))

                dense_loop(dve, lambda s, it, j: chain(D_STAGES[s], it, j, D_PE, D_ACT, D_DVE, d_pe, d_act, d_dve))
                staggered(dve, SRC_IT, len(S_STAGES), S_LAG, lambda s, it, j: chain(
                    S_STAGES[s], it, j, S_PE, S_ACT, S_DVE, s_pe, s_act, s_dve))

        with ExitStack() as ctx:
            sem = phase_semaphores(nc, ctx, "")

            v, a = sem("wt_dve"), sem("wt_act")
            block = ctx.enter_context(nc.Block())
            out_src, out_dst, in_dst = info[:, 0, :, 2], info[:, 1, :, 2], info[:, 1, :, 1]
            in_src, first_src, first_dst = info[:, 0, :, 1], info[:, 0, :, 0], info[:, 1, :, 0]

            @block.vector
            def _(dve):
                dve.tensor_tensor(tmp[:, 0, :], out_src, in_dst, ALU.mult).then_inc(v, 1)
                dve.tensor_scalar(w_light[:, :], out_dst, 1.0, None, ALU.max).then_inc(v, 1)
                dve.wait_ge(v, 2)
                dve.tensor_tensor(tmp[:, 1, :], out_src, w_light[:, :], ALU.mult).then_inc(v, 1)
                dve.reciprocal(w_mean[:, :], in_dst).then_inc(v, 1)
                dve.tensor_scalar(tmp[:, 2, :], in_src, 0.5, None, ALU.is_gt).then_inc(v, 1)
                dve.tensor_scalar(edge_no[:, :], edge_no[:, :], float(EP), None, ALU.add).then_inc(v, 1)
                dve.wait_ge(v, 6)
                dve.tensor_tensor(first_src, first_src, edge_no[:, :], ALU.subtract).then_inc(v, 1)
                dve.wait_ge(v, 7)
                dve.tensor_tensor(first_src, first_src, tmp[:, 2, :], ALU.mult).then_inc(v, 1)
                dve.wait_ge(v, 8)
                dve.tensor_tensor(first_src, first_src, edge_no[:, :], ALU.add).then_inc(v, 1)
                dve.wait_ge(v, 9)
                dve.tensor_copy(idx_lvl[:, :], first_src).then_inc(v, 1)
                dve.tensor_scalar(edge_no[:, :], edge_no[:, :], -float(EP), None, ALU.add).then_inc(v, 1)
                dve.wait_ge(v, 11)
                dve.tensor_tensor(tmp[:, 2, :], first_dst, edge_no[:, :], ALU.not_equal).then_inc(v, 1)
                dve.wait_ge(v, 12)
                dve.scalar_tensor_tensor(out=tmp[:, 2, :], in0=tmp[:, 2, :], scalar=float(4 * HI * LO), in1=dstP[:, :],
                                         op0=ALU.mult, op1=ALU.add).then_inc(v, 1)
                dve.wait_ge(v, 13)
                dve.tensor_copy(idx_out[:, :], tmp[:, 2, :]).then_inc(v, 1)
                dve.wait_ge(a, 4)
                dve.tensor_tensor(w_gcn[:, :], tmp[:, 0, :], wP[:, :], ALU.mult).then_inc(v, 1)

            @block.scalar
            def _(act):
                act.wait_ge(v, 3)
                act.activation(tmp[:, 0, :], tmp[:, 0, :], ACT.Ln).then_inc(a, 1)
                act.activation(tmp[:, 1, :], tmp[:, 1, :], ACT.Ln).then_inc(a, 1)
                act.wait_ge(a, 2)
                act.activation(tmp[:, 0, :], tmp[:, 0, :], ACT.Exp, scale=-0.5).then_inc(a, 1)
                act.activation(w_light[:, :], tmp[:, 1, :], ACT.Exp, scale=-0.5).then_inc(a, 1)

        weights = [w_gcn, w_gcn, None, w_mean, w_mean, w_light]
        tables = [src_x] + level_rows[1:6]
        dst_tables = [dst_x] + level_rows[1:6]
        for level in range(6):
            sum_edges(nc, locals(), level, weights[level], tables[level], dst_tables[level])
            carry_sums(nc, locals(), level)
            update_rows(nc, locals(), level, dst_tables)


def sum_edges(nc, env, level, weight, table, dst_table):
    buf, extra, psum, ident, w_use = (env[k] for k in ("buf", "extra", "psum", "ident", "w_use"))
    match_dram, sums_dram, edge_attr, ends = (env[k] for k in ("match_dram", "sums_dram", "edge_attr", "ends"))
    ring_idx, idx_lvl, ones3, bias3 = env["ring_idx"], env["idx_lvl"], env["ones3"], env["bias3"]
    edge_rows, NG, E, TAIL, EP = env["edge_rows"], env["NG"], env["E"], env["TAIL"], env["EP"]
    IT = NG // US
    relational = level == 2
    gathers = level > 0
    if relational:
        STAGES = "join turn_z copy_z turn_a copy_a message relu sum copy ends".split()
        PE_, ACT_, DVE_ = Steps("turn_z turn_a message sum"), Steps("copy_z relu copy"), Steps("join copy_a ends")
        used = ("turn_z", "sum")
    else:
        STAGES = "weigh sum copy ends".split()
        PE_, ACT_, DVE_ = Steps("sum"), Steps("copy"), Steps("weigh ends")
        used = ("sum", "sum")
    LAG = len(STAGES) // US

    def wide(ap):
        return ap.rearrange("p (k d) -> p k d", d=P)

    def B(j, k):
        return buf[j][:, k, :]

    def ps(j):
        return psum[:, j, 0:GW]

    with ExitStack() as ctx:
        sem = phase_semaphores(nc, ctx, f"_{level}")

        def slots(name):
            return [sem(f"{name}{j}") for j in range(US)]

        match_in, rows_in, more_in, sums_out = (slots(n) for n in ("match_in", "edge_rows_in", "more_in", "sums_out"))
        pe_s, act_s, dve_s = (slots(n) for n in ("g_pe", "g_act", "g_dve"))
        idx_copied, ring_free = sem("lvl_idx"), sem("lvl_ring_free")
        ARRIVE = 16 * G if gathers else 16
        block = ctx.enter_context(nc.Block())

        @block.sync
        def _(sp):
            def loads(it, j):
                g = US * it + j
                last = isinstance(it, int) and it == IT - 1 and j == US - 1
                sp.dma_start(B(j, 0), match_dram[bass.ds(g, 1)].rearrange("a p w -> (a p) w")).then_inc(match_in[j], 16)
                if not gathers:
                    sp.dma_start(wide(B(j, 1)), edge_rows(table, g)).then_inc(rows_in[j], 16)
                if relational:
                    sp.dma_start(wide(B(j, 3)), edge_rows(dst_table, g)).then_inc(more_in[j], 16)
                    sp.dma_start(wide(B(j, 4))[:, 0:G - 1, :],
                                 edge_attr[bass.ds(g * GW, GW - P), :].rearrange("(k p) d -> p k d", p=P)
                                 ).then_inc(more_in[j], 16)
                    rows = TAIL if last else P
                    sp.dma_start(B(j, 4)[0:rows, (G - 1) * P:GW],
                                 edge_attr[bass.ds(g * GW + GW - P, rows), :]).then_inc(more_in[j], 16)

            for j in range(US):
                loads(0, j)

            def body(stage, it, j):
                if STAGES[stage] == "copy" and not (isinstance(it, int) and it == IT - 1):
                    sp.wait_ge(pe_s[j], PE_.at(it, used[1]))
                    loads(it + 1, j)
                if STAGES[stage] == "ends":
                    sp.wait_ge(act_s[j], ACT_.at(it, "copy"))
                    sp.dma_start(sums_dram[bass.ds(US * it + j, 1)].rearrange("a p w -> (a p) w"), B(j, 2)
                                 ).then_inc(sums_out[j], 16)

            staggered(sp, IT, len(STAGES), LAG, body)
            for j in range(US):
                sp.wait_ge(sums_out[j], 16 * IT)

        if gathers:
            @block.gpsimd
            def _(pool):
                def body(it):
                    for j in range(US):
                        if not (isinstance(it, int) and it == 0):
                            pool.wait_ge(pe_s[j], PE_.at(it - 1, used[0]))
                            pool.sem_inc(ring_free, 1)
                        pool.tensor_copy(ring_idx[:, j, :], idx_lvl[:, bass.ds((US * it + j) * G, G)]
                                         ).then_inc(idx_copied, 1)
                        pool.wait_ge(idx_copied, US * it + j + 1)
                        pool.sem_inc(ring_free, 1)
                        for k in range(G):
                            pool.indirect_dma_start(
                                out=B(j, 1)[:, k * P:(k + 1) * P], out_offset=None, in_=table,
                                in_offset=bass.IndirectOffsetOnAxis(ap=ring_idx[:, j, k:k + 1], axis=0),
                            ).then_inc(rows_in[j], 16)

                body(0)
                with pool.Fori(1, IT) as it:
                    body(it)

        @block.tensor
        def _(pe):
            def body(stage, it, j):
                name, mm = STAGES[stage], None
                if name == "turn_z":
                    pe.wait_ge(dve_s[j], DVE_.at(it, "join"))
                    wait(pe, act_s[j], it * ACT_.n)
                    for k in range(G):
                        mm = pe.transpose(ps(j)[:, k * P:(k + 1) * P], B(j, 1)[:, k * P:(k + 1) * P], ident[:, :])
                elif name == "turn_a":
                    pe.wait_ge(act_s[j], ACT_.at(it, "copy_z"))
                    for k in range(G):
                        mm = pe.transpose(ps(j)[:, k * P:(k + 1) * P], B(j, 4)[:, k * P:(k + 1) * P], ident[:, :])
                elif name == "message":
                    pe.wait_ge(dve_s[j], DVE_.at(it, "copy_a"))
                    for k in range(G):
                        o, at = ps(j)[:, k * P:(k + 1) * P], slice(k * P, (k + 1) * P)
                        pe.matmul(o, B(j, 5)[:, at], w_use[:, 0, :], start=True, stop=False)
                        pe.matmul(o, extra[:, j, at], w_use[:, 1, :], start=False, stop=False)
                        mm = pe.matmul(o, ones3[:, :], bias3[:, 0, :], start=False, stop=True)
                elif name == "sum":
                    pe.wait_ge(match_in[j], 16 * it + 16)
                    if relational:
                        pe.wait_ge(act_s[j], ACT_.at(it, "relu"))
                    else:
                        pe.wait_ge(dve_s[j], DVE_.at(it, "weigh"))
                        wait(pe, act_s[j], it * ACT_.n)
                    rows = B(j, 5) if relational else B(j, 1)
                    for k in range(G):
                        at = slice(k * P, (k + 1) * P)
                        mm = pe.matmul(ps(j)[:, at], rows[:, at], B(j, 0)[:, at], start=True, stop=True)
                if mm is not None:
                    mm.then_inc(pe_s[j], 1)

            staggered(pe, IT, len(STAGES), LAG, body)

        @block.vector
        def _(dve):
            def body(stage, it, j):
                name = STAGES[stage]
                if name == "join":
                    dve.wait_ge(rows_in[j], ARRIVE * it + ARRIVE)
                    dve.wait_ge(more_in[j], 48 * it + 48)
                    dve.tensor_tensor(B(j, 1), B(j, 1), B(j, 3), ALU.add).then_inc(dve_s[j], 1)
                elif name == "copy_a":
                    dve.wait_ge(pe_s[j], PE_.at(it, "turn_a"))
                    dve.tensor_copy(extra[:, j, :], ps(j)).then_inc(dve_s[j], 1)
                elif name == "weigh":
                    dve.wait_ge(rows_in[j], ARRIVE * it + ARRIVE)
                    w = weight[:, bass.ds((US * it + j) * G, G)].unsqueeze(2).to_broadcast([P, G, P])
                    dve.tensor_tensor(wide(B(j, 1)), wide(B(j, 1)), w, ALU.mult).then_inc(dve_s[j], 1)
                elif name == "ends":
                    dve.wait_ge(act_s[j], ACT_.at(it, "copy"))
                    dve.tensor_copy(ends[:, bass.ds((US * it + j) * G, G), :], wide(B(j, 2))[:, :, 0:P:P - 1]
                                    ).then_inc(dve_s[j], 1)

            staggered(dve, IT, len(STAGES), LAG, body)

        @block.scalar
        def _(act):
            def body(stage, it, j):
                name = STAGES[stage]
                if name == "copy_z":
                    act.wait_ge(pe_s[j], PE_.at(it, "turn_z"))
                    act.copy(B(j, 5), ps(j)).then_inc(act_s[j], 1)
                elif name == "relu":
                    act.wait_ge(pe_s[j], PE_.at(it, "message"))
                    act.activation(B(j, 5), ps(j), ACT.Relu).then_inc(act_s[j], 1)
                elif name == "copy":
                    act.wait_ge(pe_s[j], PE_.at(it, "sum"))
                    wait(act, sums_out[j], 16 * it)
                    wait(act, dve_s[j], it * DVE_.n)
                    act.copy(B(j, 2), ps(j)).then_inc(act_s[j], 1)

            staggered(act, IT, len(STAGES), LAG, body)


def carry_sums(nc, env, level):
    extra, psum, reach, ends, ident = (env[k] for k in ("extra", "psum", "reach", "ends", "ident"))
    carry_dram, HB, ET = env["carry_dram"], env["HB"], env["ET"]
    with ExitStack() as ctx:
        sem = phase_semaphores(nc, ctx, f"_{level}")
        by_tile, turned, carried, split, carry_out = (
            sem(n) for n in ("by_tile", "ends_turned", "carried", "carry_split", "carry_out"))
        parts = ctx.enter_context(nc.sbuf_tensor(f"parts_{level}", [HB, 3, 4 * P], BF16))
        block = ctx.enter_context(nc.Block())
        rows = extra[0:HB, 0, 0:4 * P]
        rest = extra[0:HB, 1, 0:4 * P]

        @block.sync
        def _(sp):
            sp.wait_ge(split, 6)
            for k in range(3):
                for s in range(2):
                    sp.dma_start(carry_dram[3 * s + k:3 * s + k + 1, :].rearrange("a (b t d) -> (a t) b d", b=2, d=P),
                                 parts[:, k, s * 2 * P:(s + 1) * 2 * P].rearrange("t (b d) -> t b d", b=2)
                                 ).then_inc(carry_out, 16)
            sp.wait_ge(carry_out, 96)

        @block.tensor
        def _(pe):
            for s in range(2):
                for b in range(2):
                    mm = pe.transpose(psum[0:HB, 0, (2 * s + b) * P:(2 * s + b + 1) * P],
                                      ends[:, b * HB:(b + 1) * HB, 1 - s], ident[:, :])
            mm.then_inc(turned, 1)
            pe.wait_ge(by_tile, 1)
            for s in range(2):
                for tb in range(2):
                    for b in range(2):
                        mm = pe.matmul(psum[0:HB, 1, (2 * s + tb) * P:(2 * s + tb + 1) * P],
                                       reach[:, s, b, tb * HB:(tb + 1) * HB],
                                       rows[:, (2 * s + b) * P:(2 * s + b + 1) * P], start=(b == 0), stop=(b == 1))
            mm.then_inc(carried, 1)

        @block.vector
        def _(dve):
            dve.wait_ge(turned, 1)
            dve.tensor_copy(rows, psum[0:HB, 0, 0:4 * P]).then_inc(by_tile, 1)
            dve.wait_ge(carried, 1)
            for k in range(3):
                left = psum[0:HB, 1, 0:4 * P] if k == 0 else rest
                if k:
                    dve.wait_ge(split, 2 * k)
                dve.tensor_copy(parts[:, k, :], left).then_inc(split, 1)
                dve.wait_ge(split, 2 * k + 1)
                dve.tensor_tensor(rest, left, parts[:, k, :], ALU.subtract).then_inc(split, 1)


def update_rows(nc, env, level, dst_tables):
    buf, carry_in, psum, small, cols = (env[k] for k in ("buf", "carry_in", "psum", "small", "cols"))
    ident, center, w_use, eps_t, extra = (env[k] for k in ("ident", "center", "w_use", "eps_t", "extra"))
    ones3, bias3, sums_dram, carry_dram = (env[k] for k in ("ones3", "bias3", "sums_dram", "carry_dram"))
    ends_mask, edge_rows, NG, N = env["ends_mask"], env["edge_rows"], env["NG"], env["N"]
    idx_out, ring_out, out = env["idx_out"], env["ring_idx"], env["out"]
    IT = NG // US
    LN = lambda k: f"square{k} sum{k} root{k} norm{k}"
    LNA = lambda k: f"square{k} log{k} root{k}"
    STAGES, PE_, ACT_, DVE_, RESULT = [
        (f"carry gather centre1 {LN(1)} turn1 exp1 fold1 elu1 turn_y rows_y", "carry centre1 turn1 turn_y",
         f"{LNA(1)} exp1 affine1 fold1 rows_y", "gather sum1 norm1 elu1", 5),
        (f"carry gather turn_x copy_x centre1 {LN(1)} turn1 exp1 fold1 elu1 centre3 {LN(3)}",
         "carry turn_x centre1 turn1 centre3", f"copy_x {LNA(1)} exp1 affine1 fold1 {LNA(3)}",
         "gather sum1 norm1 elu1 sum3 norm3", 3),
        (f"carry gather turn_x join centre1 {LN(1)}", "carry turn_x centre1", LNA(1), "gather join sum1 norm1", 3),
        ("carry gather turn_x copy_x hidden relu turn_h rows_h", "carry turn_x hidden turn_h",
         "copy_x relu rows_h", "gather", 5),
        (f"carry gather turn_x copy_x sage add {LN(4)}", "carry turn_x sage", f"copy_x {LNA(4)}",
         "gather add sum4 norm4", 5),
        (f"carry gather centre1 {LN(1)}", "carry centre1", LNA(1), "gather sum1 norm1", 3),
    ][level]
    STAGES, PE_, ACT_, DVE_ = STAGES.split(), Steps(PE_), Steps(ACT_), Steps(DVE_)
    LAG = len(STAGES) // US
    joined = level in (0, 1, 5)
    by_act = level in (0, 3)

    def B(j, k):
        return buf[j][:, k, :]

    def sums_in(j):
        return extra[:, j, :]

    def ps(j):
        return psum[:, j, 0:GW]

    def wide(ap):
        return ap.rearrange("p (k d) -> p k d", d=P)

    with ExitStack() as ctx:
        sem = phase_semaphores(nc, ctx, f"_{level}")

        def slots(name):
            return [sem(f"{name}{j}") for j in range(US)]

        sums_got, rows_got, second_got, stored = (slots(n) for n in ("sums_got", "rows_got", "second_got", "stored"))
        pe_s, act_s, dve_s = (slots(n) for n in ("u_pe", "u_act", "u_dve"))
        idx_ready, rows_final = sem("idx_ready"), sem("rows_final")
        STORES = 16 * G if level == 5 else 16
        second = [ctx.enter_context(nc.sbuf_tensor(f"second{level}_{j}", [P, GW], F32)) for j in range(US)] \
            if level in (1, 4) else None
        block = ctx.enter_context(nc.Block())

        @block.sync
        def _(sp):
            def load_sums(it, j):
                g = US * it + j
                sp.dma_start(sums_in(j), sums_dram[bass.ds(g, 1)].rearrange("a p w -> (a p) w")).then_inc(sums_got[j], 16)
                sp.dma_start(carry_in[j][:, 0, :], carry_dram[:, bass.ds(g * GW, GW)]).then_inc(sums_got[j], 16)
                sp.dma_start(carry_in[j][:, 1, :], ends_mask[:, bass.ds(g * GW, GW)]).then_inc(sums_got[j], 16)

            def load_rows(it, j):
                sp.dma_start(wide(B(j, 0)), edge_rows(dst_tables[3 if level == 4 else level], US * it + j)
                             ).then_inc(rows_got[j], 16)

            def load_second(it, j):
                if second:
                    sp.dma_start(wide(second[j][:, :]), edge_rows(dst_tables[0 if level == 1 else 4], US * it + j)
                                 ).then_inc(second_got[j], 16)

            for j in range(US):
                load_sums(0, j)
                load_rows(0, j)
                load_second(0, j)

            rows_used = "add" if level == 4 else "gather" if joined else "join" if level == 2 else None

            def body(stage, it, j):
                name = STAGES[stage]
                last = isinstance(it, int) and it == IT - 1
                if not last:
                    if name == "gather":
                        sp.wait_ge(dve_s[j], DVE_.at(it, "gather"))
                        load_sums(it + 1, j)
                        if joined:
                            load_rows(it + 1, j)
                    if name == "join":
                        sp.wait_ge(dve_s[j], DVE_.at(it, "join"))
                        load_rows(it + 1, j)
                    if name == "copy_x":
                        sp.wait_ge(act_s[j], ACT_.at(it, "copy_x"))
                        load_second(it + 1, j)
                        if level == 3:
                            load_rows(it + 1, j)
                    if name == "add":
                        sp.wait_ge(dve_s[j], DVE_.at(it, "add"))
                        load_rows(it + 1, j)
                if level < 5 and stage == len(STAGES) - 1:
                    if by_act:
                        sp.wait_ge(act_s[j], it * ACT_.n + ACT_.n)
                    else:
                        sp.wait_ge(dve_s[j], it * DVE_.n + DVE_.n)
                    sp.dma_start(edge_rows(dst_tables[level + 1], US * it + j), wide(B(j, RESULT))
                                 ).then_inc(stored[j], 16)

            staggered(sp, IT, len(STAGES), LAG, body)
            if level < 5:
                for j in range(US):
                    sp.wait_ge(stored[j], 16 * IT)

        if level == 5:
            @block.gpsimd
            def _(pool):
                def body(it):
                    for j in range(US):
                        if not (isinstance(it, int) and it == 0):
                            pool.wait_ge(stored[j], STORES * it)
                            pool.sem_inc(rows_final, 1)
                        pool.tensor_copy(ring_out[:, j, :], idx_out[:, bass.ds((US * it + j) * G, G)]
                                         ).then_inc(idx_ready, 1)
                        pool.wait_ge(idx_ready, US * it + j + 1)
                        pool.wait_ge(dve_s[j], it * DVE_.n + DVE_.n)
                        pool.sem_inc(rows_final, 1)
                        for k in range(G):
                            pool.indirect_dma_start(
                                out=out, out_offset=bass.IndirectOffsetOnAxis(ap=ring_out[:, j, k:k + 1], axis=0),
                                in_=B(j, 3)[:, k * P:(k + 1) * P], in_offset=None,
                                bounds_check=N - 1, oob_is_err=False).then_inc(stored[j], 16)

                body(0)
                with pool.Fori(1, IT) as it:
                    body(it)
                for j in range(US):
                    pool.wait_ge(stored[j], STORES * IT)

        @block.tensor
        def _(pe):
            I, C = ident[:, :], center[:, :]

            def each_tile(j, terms, bias=False):
                for t in range(G):
                    at = slice(t * P, (t + 1) * P)
                    for n, (a, b) in enumerate(terms):
                        mm = pe.matmul(ps(j)[:, at], a[:, at], b if b.shape[-1] == P else b[:, at], start=(n == 0),
                                       stop=(n == len(terms) - 1 and not bias))
                    if bias:
                        mm = pe.matmul(ps(j)[:, at], ones3[:, :], bias3[:, 1, :], start=False, stop=True)
                return mm

            def turn(j, rows, carried=False):
                for t in range(G):
                    at = slice(t * P, (t + 1) * P)
                    mm = pe.matmul(ps(j)[:, at], rows[:, at], I, is_transpose=not carried, start=True,
                                   stop=not carried)
                    if carried:
                        mm = pe.matmul(ps(j)[:, at], carry_in[j][:, 0, at], carry_in[j][:, 1, at], start=False,
                                       stop=True)
                return mm

            def body(stage, it, j):
                name, mm = STAGES[stage], None
                if name == "carry":
                    pe.wait_ge(sums_got[j], 48 * it + 48)
                    if by_act:
                        wait(pe, act_s[j], it * ACT_.n)
                    else:
                        wait(pe, dve_s[j], it * DVE_.n)
                    if joined:
                        pe.wait_ge(rows_got[j], 16 * it + 16)
                        mm = turn(j, B(j, 0), carried=True)
                    else:
                        mm = each_tile(j, [(carry_in[j][:, 0, :], carry_in[j][:, 1, :])])
                elif name == "turn_x":
                    pe.wait_ge(dve_s[j], DVE_.at(it, "gather"))
                    pe.wait_ge((second_got if second else rows_got)[j], 16 * it + 16)
                    mm = turn(j, second[j][:, :] if second else B(j, 0))
                elif name == "centre1":
                    if level == 1:
                        pe.wait_ge(act_s[j], ACT_.at(it, "copy_x"))
                    else:
                        pe.wait_ge(dve_s[j], DVE_.at(it, "join" if level == 2 else "gather"))
                    mm = each_tile(j, [(B(j, 1), C)])
                elif name == "turn1":
                    pe.wait_ge(dve_s[j], DVE_.at(it, "norm1"))
                    mm = turn(j, B(j, 3))
                elif name == "turn_y":
                    pe.wait_ge(dve_s[j], DVE_.at(it, "elu1"))
                    mm = turn(j, B(j, 4))
                elif name == "centre3":
                    pe.wait_ge(dve_s[j], DVE_.at(it, "elu1"))
                    mm = each_tile(j, [(B(j, 5), C), (B(j, 4), C)])
                elif name == "hidden":
                    pe.wait_ge(act_s[j], ACT_.at(it, "copy_x"))
                    for lo, hi in ((0, 512), (512, GW)):
                        pe.matmul(ps(j)[:, lo:hi], w_use[:, 2, :], B(j, 1)[:, lo:hi], start=True, stop=False)
                        mm = pe.matmul(ps(j)[:, lo:hi], w_use[:, 3, :], B(j, 4)[:, lo:hi], start=False, stop=True)
                elif name == "turn_h":
                    pe.wait_ge(act_s[j], ACT_.at(it, "relu"))
                    mm = turn(j, B(j, 3))
                elif name == "sage":
                    pe.wait_ge(act_s[j], ACT_.at(it, "copy_x"))
                    mm = each_tile(j, [(B(j, 1), w_use[:, 4, :]), (B(j, 4), w_use[:, 5, :])], bias=True)
                if mm is not None:
                    mm.then_inc(pe_s[j], 1)

            staggered(pe, IT, len(STAGES), LAG, body)

        @block.scalar
        def _(act):
            def body(stage, it, j):
                name = STAGES[stage]
                k = name[-1]

                def step(ins):
                    ins.then_inc(act_s[j], 1)

                if name == "copy_x":
                    act.wait_ge(pe_s[j], PE_.at(it, "turn_x"))
                    step(act.copy(B(j, 5 if level == 1 else 1), ps(j)))
                elif name in ("square1", "square3"):
                    act.wait_ge(pe_s[j], PE_.at(it, "centre" + k))
                    step(act.activation(B(j, 2), ps(j), ACT.Square))
                elif name == "square4":
                    act.wait_ge(dve_s[j], DVE_.at(it, "add"))
                    step(act.activation(B(j, 2), B(j, 4), ACT.Square))
                elif name.startswith("root"):
                    act.wait_ge(dve_s[j], DVE_.at(it, "sum" + k))
                    step(act.activation(small[:, j, 1, :], small[:, j, 0, :], ACT.Ln, bias=eps_t[:, 0:1],
                                        scale=1.0 / P))
                    act.wait_ge(act_s[j], ACT_.at(it, "log" + k))
                    step(act.activation(small[:, j, 2, :], small[:, j, 1, :], ACT.Exp, scale=-0.5))
                elif name == "exp1":
                    l = level
                    affine = dict(bias=cols[:, 2 + l:3 + l], scale=cols[:, l:l + 1])
                    act.wait_ge(pe_s[j], PE_.at(it, "turn1"))
                    step(act.activation(B(j, 2), ps(j), ACT.Exp, **affine))
                    step(act.activation(B(j, 3), ps(j), ACT.Identity, **affine))
                elif name == "fold1":
                    act.wait_ge(act_s[j], ACT_.at(it, "exp1"))
                    step(act.activation(B(j, 2), B(j, 2), ACT.Relu, bias=1.0, scale=-1.0))
                elif name == "relu":
                    act.wait_ge(pe_s[j], PE_.at(it, "hidden"))
                    step(act.activation(B(j, 3), ps(j), ACT.Relu, bias=cols[:, 4:5]))
                elif name in ("rows_y", "rows_h"):
                    act.wait_ge(pe_s[j], PE_.at(it, "turn_" + name[-1]))
                    step(act.copy(B(j, 5), ps(j)))

            staggered(act, IT, len(STAGES), LAG, body)

        @block.vector
        def _(dve):
            def body(stage, it, j):
                name = STAGES[stage]
                k = name[-1]

                def step(ins):
                    ins.then_inc(dve_s[j], 1)

                if name == "gather":
                    wait(dve, stored[j], STORES * it)
                    dve.wait_ge(pe_s[j], PE_.at(it, "carry"))
                    step(dve.tensor_tensor(B(j, 1 if joined else 4), ps(j), sums_in(j), ALU.add))
                elif name == "join":
                    dve.wait_ge(pe_s[j], PE_.at(it, "turn_x"))
                    step(dve.scalar_tensor_tensor(out=B(j, 1), in0=B(j, 4), scalar=0.0, in1=ps(j), op0=ALU.max,
                                                  op1=ALU.add))
                elif name.startswith("sum"):
                    dve.wait_ge(act_s[j], ACT_.at(it, "square" + k))
                    step(dve.tensor_reduce(small[:, j, 0, :], wide(B(j, 2)), AX_X, ALU.add))
                elif name.startswith("norm"):
                    dve.wait_ge(act_s[j], ACT_.at(it, "root" + k))
                    rows, o = (B(j, 4), 5) if k == "4" else (ps(j), 3)
                    step(dve.tensor_tensor(wide(B(j, o)), wide(rows),
                                           small[:, j, 2, :].unsqueeze(2).to_broadcast([P, G, P]), ALU.mult))
                elif name == "elu1":
                    dve.wait_ge(act_s[j], ACT_.at(it, "fold1"))
                    step(dve.scalar_tensor_tensor(out=B(j, 4), in0=B(j, 2), scalar=-1.0, in1=B(j, 3),
                                                  op0=ALU.mult, op1=ALU.max))
                elif name == "add":
                    dve.wait_ge(pe_s[j], PE_.at(it, "sage"))
                    dve.wait_ge(rows_got[j], 16 * it + 16)
                    step(dve.tensor_tensor(B(j, 4), ps(j), B(j, 0), ALU.add))

            staggered(dve, IT, len(STAGES), LAG, body)


_INS = ["x", "src", "dst", "edge_attr_128", "edge_weight", "L0_gnn_ln_gamma", "L0_gnn_ln_beta", "L1_gnn_W_obj",
        "L1_gnn_b_obj", "L1_gnn_W_rel", "L1_gnn_b_rel", "L2_gnn_W1_self", "L2_gnn_W1_neigh", "L2_gnn_b1",
        "L2_gnn_W2_self", "L2_gnn_W2_neigh", "L2_gnn_b2"]


def build(nc, shapes):
    args = [nc.dram_tensor(f"in_{n}_dram", s, d, kind="ExternalInput").ap() for n, s, d in shapes]
    out = nc.dram_tensor("out_0_dram", shapes[0][1], F32, kind="ExternalOutput").ap()
    gnn_kernel(nc, *args, out)


def kernel(**inputs):
    import numpy as _np
    import concourse.bacc as _bacc
    from concourse.bass_utils import run_bass_kernel_spmd as _run

    nc = _bacc.Bacc("TRN2", target_bir_lowering=False, num_devices=1)
    arrays, shapes = {}, []
    for name in _INS:
        a = _np.ascontiguousarray(inputs[name])
        arrays[f"in_{name}_dram"] = a
        shapes.append((name, a.shape, mybir.dt.from_np(a.dtype)))
    build(nc, shapes)
    r = _run(nc, [arrays], core_ids=[0])
    return r.results[0]["out_0_dram"]
```

```python
from contextlib import ExitStack

import concourse.bass as bass
from concourse import mybir

ALU = mybir.AluOpType
ACT = mybir.ActivationFunctionType
F32 = mybir.dt.float32
F16 = mybir.dt.float16
BF16 = mybir.dt.bfloat16
I32 = mybir.dt.int32
AX_X = mybir.AxisListType.X

P = 128
EPS = 1e-5
US = 4
G = 7
GW = G * P
ROWS = US * GW
LO = 256
NBUF = 6
JOINED = (0, 1, 5)
BESIDE = (0, 1, 3, 4, 5)
BESIDE_IT = 4
BESIDE_SLOTS = 3
BESIDE_EDGES = 7


class Steps:

    def __init__(self, names):
        self.names = names.split()
        self.n = len(self.names)

    def at(self, it, name):
        return it * self.n + (self.names.index(name) + 1)


class Plan:

    def __init__(self, text, copies=US, others=None, shift=0):
        words = text.split()
        self.names = words[::2]
        events = []
        for name, due in zip(self.names, map(int, words[1::2])):
            c = (others or {}).get(name, copies)
            events += [(due + shift + j * 1000 // c, name, j) for j in range(c)]
        self.events = [(t % 1000, name, j, t // 1000) for t, name, j in sorted(events, key=lambda e: e[0] % 1000)]
        assert all(late < 2 for _, _, _, late in self.events)


def wait(engine, sem, count):
    if not (isinstance(count, int) and count <= 0):
        engine.wait_ge(sem, count)


def first(it):
    return isinstance(it, int) and it == 0


def is_last(it, n):
    return isinstance(it, int) and it == n - 1


def staggered(engine, n, plan, body, tail=1, before=None, drain=True):

    def tick(i):
        for _, name, j, late in plan.events:
            it = i - 1 if late else i
            if not (isinstance(it, int) and not 0 <= it < n):
                body(name, it, j)

    events = [(t, name, 0, j, body) for t, name, j, late in plan.events if not late]
    if before:
        n0, plan0, body0 = before
        events += [(t, name, n0 - 1, j, body0) for t, name, j, late in plan0.events if late]
    for _, name, it, j, b in sorted(events, key=lambda e: e[0]):
        b(name, it, j)
    head = min(2, n)
    for i in range(1, head):
        tick(i)
    if n - tail > head + 1:
        with engine.Fori(head, n - tail) as i:
            tick(i)
        head = n - tail
    for i in range(head, n + drain):
        tick(i)


def phase_semaphores(nc, ctx, suffix):
    used = []

    def sem(name):
        used.append(nc.alloc_semaphore(name + suffix))
        return used[-1]

    def clear():
        nc.clear_and_free_semaphores(used)
        nc.all_engine_barrier()

    ctx.callback(clear)
    return sem


class Chain:

    def __init__(self, env, sem, tag, source=False, dve_joins=False, slots=US, after=None):
        self.after = after
        self.source, self.dve_joins = source, dve_joins
        self.buf, self.psum, self.small, self.cols, self.ones3, self.bias3, self.w_use, self.eps_t = (
            env[k] for k in ("buf", "psum", "small", "cols", "ones3", "bias3", "w_use", "eps_t"))
        self.ident, self.center = env["ident"][:, :], env["center"][:, :]
        self.pe_s, self.act_s, self.dve_s, self.pool_s, self.arrived = (
            [sem(f"{tag}_{n}{j}") for j in range(slots)] for n in ("pe", "act", "dve", "pool", "in"))
        self.stored = {n: [sem(f"{tag}_{n}_out{j}") for j in range(slots)]
                       for n in (("y1", "x1", "x2", "h1", "x3") if source else ("out",))}
        y, h, x1 = ("turn_y", "turn_h", "norm_x1") if source else ("", "", "")
        self.PE = Steps(f"turn_x centre1 turn1 {y} centre2 turn2 centre3 turn3 hidden {h} sage")
        y, h, l, r = ("rows_y", "rows_h", "log_x1", "root_x1") if source else ("", "", "", "")
        self.ACT = Steps(f"copy_x square1 log1 root1 exp1 affine1 {y} square2 log2 root2 exp2 affine2 "
                         f"square3 log3 {l} root3 {r} copy3 relu {h} square4 log4 root4")
        self.DVE = Steps(f"sum1 norm1 {'fold1' if source else 'shifted_elu1'} sum2 norm2 elu2 {'join' if dve_joins else ''} "
                         f"sum3 {x1} norm3 add sum4 norm4")
        self.POOL = Steps("elu1 join" if source else "join")

    def B(self, j, k):
        return self.buf[j][:, k, :]

    def ps(self, j):
        return self.psum[:, j, 0:GW]

    def wide(self, ap):
        return ap.rearrange("p (k d) -> p k d", d=P)

    def wait_y1(self, engine, it, j):
        if self.source:
            engine.wait_ge(self.pool_s[j], self.POOL.at(it, "elu1"))
        else:
            engine.wait_ge(self.dve_s[j], self.DVE.at(it, "shifted_elu1"))

    def pe(self, pe, stage, it, j):
        B, ps, mm = self.B, self.ps, None

        def turn(k):
            for t in range(G):
                mm = pe.transpose(ps(j)[:, t * P:(t + 1) * P], B(j, k)[:, t * P:(t + 1) * P], self.ident)
            return mm

        def times(k, m, bias=False):
            for t in range(G):
                at = slice(t * P, (t + 1) * P)
                mm = pe.matmul(ps(j)[:, at], B(j, k)[:, at], m, start=True, stop=not bias)
                if bias:
                    mm = pe.matmul(ps(j)[:, at], self.ones3[:, :], self.bias3[:, 1, :], start=False, stop=True)
            return mm

        if stage == "turn_x":
            pe.wait_ge(self.arrived[j], 16 * it + 16)
            if not first(it):
                pe.wait_ge(self.dve_s[j], self.DVE.at(it - 1, "add"))
            elif self.after:
                other, n = self.after
                pe.wait_ge(other.dve_s[j], other.DVE.at(n - 1, "add"))
            mm = turn(0)
        elif stage == "centre1":
            pe.wait_ge(self.act_s[j], self.ACT.at(it, "copy_x"))
            mm = times(1, self.center)
        elif stage in ("turn1", "turn2", "turn3"):
            pe.wait_ge(self.dve_s[j], self.DVE.at(it, "norm" + stage[4]))
            mm = turn(3)
        elif stage == "turn_y":
            self.wait_y1(pe, it, j)
            mm = turn(4)
        elif stage == "centre2":
            self.wait_y1(pe, it, j)
            if self.source:
                pe.wait_ge(self.act_s[j], self.ACT.at(it, "rows_y"))
            mm = times(4, self.center)
        elif stage == "centre3":
            if self.dve_joins:
                pe.wait_ge(self.dve_s[j], self.DVE.at(it, "join"))
            else:
                pe.wait_ge(self.pool_s[j], self.POOL.at(it, "join"))
            mm = times(4, self.center)
        elif stage == "hidden":
            pe.wait_ge(self.act_s[j], self.ACT.at(it, "copy3"))
            for lo, hi in ((0, 512), (512, GW)):
                mm = pe.matmul(ps(j)[:, lo:hi], self.w_use[:, 2, :], B(j, 1)[:, lo:hi], start=True, stop=True)
        elif stage == "turn_h":
            pe.wait_ge(self.act_s[j], self.ACT.at(it, "relu"))
            mm = turn(4)
        elif stage == "sage":
            pe.wait_ge(self.act_s[j], self.ACT.at(it, "rows_h" if self.source else "relu"))
            mm = times(4, self.w_use[:, 4, :], bias=True)
        if mm is not None:
            mm.then_inc(self.pe_s[j], 1)

    def act(self, act, stage, it, j):
        B, ps, small, eps_t, source = self.B, self.ps, self.small, self.eps_t, self.source
        k = stage[-1]

        def step(ins):
            ins.then_inc(self.act_s[j], 1)

        def after_pe(name):
            act.wait_ge(self.pe_s[j], self.PE.at(it, name))

        def after_dve(name):
            act.wait_ge(self.dve_s[j], self.DVE.at(it, name))

        if stage == "copy_x":
            after_pe("turn_x")
            step(act.copy(B(j, 1), ps(j)))
        elif stage in ("square1", "square2", "square3"):
            if k == "1":
                wait(act, self.dve_s[j], it * self.DVE.n)
                if first(it) and self.after:
                    other, n = self.after
                    act.wait_ge(other.dve_s[j], n * other.DVE.n)
            after_pe("centre" + k)
            step(act.activation(B(j, 2), ps(j), ACT.Square))
        elif stage == "square4":
            after_dve("add")
            if source:
                act.wait_ge(self.stored["x1"][j], 16 * it + 16)
            step(act.activation(B(j, 2), B(j, 4), ACT.Square))
        elif stage.startswith("root"):
            twice = k == "3" or (k == "4" and not source)
            after_dve("sum" + k)
            step(act.activation(small[:, j, 1, :], small[:, j, 0, :], ACT.Ln,
                                bias=eps_t[:, 1:2] if twice else eps_t[:, 0:1],
                                scale=(1.0 + EPS if twice else 1.0) / P))
            if source and k == "3":
                step(act.activation(small[:, j, 3, :], small[:, j, 0, :], ACT.Ln, bias=eps_t[:, 0:1],
                                    scale=1.0 / P))
            act.wait_ge(self.act_s[j], self.ACT.at(it, "log" + k))
            step(act.activation(small[:, j, 2, :], small[:, j, 1, :], ACT.Exp, scale=-0.5))
            if source and k == "3":
                act.wait_ge(self.act_s[j], self.ACT.at(it, "log_x1"))
                step(act.activation(small[:, j, 3, :], small[:, j, 3, :], ACT.Exp, scale=-0.5))
        elif stage in ("exp1", "exp2", "affine1", "affine2"):
            l = int(k) - 1
            after_pe("turn" + k)
            o, func = (2, ACT.Exp) if stage.startswith("exp") else (3, ACT.Relu)
            step(act.activation(B(j, o), ps(j), func, bias=self.cols[:, 2 + l:3 + l], scale=self.cols[:, l:l + 1]))
        elif stage == "rows_y":
            after_pe("turn_y")
            wait(act, self.stored["h1"][j], 16 * it)
            if first(it) and self.after:
                other, n = self.after
                act.wait_ge(other.stored["out"][j], 16 * n)
            step(act.copy(B(j, 5), ps(j)))
        elif stage == "copy3":
            after_pe("turn3")
            step(act.copy(B(j, 1), ps(j)))
        elif stage == "relu":
            after_pe("hidden")
            step(act.activation(B(j, 4), ps(j), ACT.Relu, bias=self.cols[:, 4:5]))
        elif stage == "rows_h":
            after_pe("turn_h")
            act.wait_ge(self.stored["y1"][j], 16 * it + 16)
            step(act.copy(B(j, 5), ps(j)))

    def dve(self, dve, stage, it, j):
        B, ps, wide, small, source = self.B, self.ps, self.wide, self.small, self.source
        k = stage[-1]

        def step(ins):
            ins.then_inc(self.dve_s[j], 1)

        def after_act(name):
            dve.wait_ge(self.act_s[j], self.ACT.at(it, name))

        def scaled(o, rows, r):
            return dve.tensor_tensor(wide(o), wide(rows), small[:, j, r, :].unsqueeze(2).to_broadcast([P, G, P]),
                                     ALU.mult)

        if stage.startswith("sum"):
            after_act("square" + k)
            step(dve.tensor_reduce(small[:, j, 0, :], wide(B(j, 2)), AX_X, ALU.add))
        elif stage in ("norm1", "norm2", "norm3"):
            if source and k == "1":
                wait(dve, self.stored["x2"][j], 16 * it)
            after_act("root" + k)
            step(scaled(B(j, 3), ps(j), 2))
        elif stage == "norm_x1":
            after_act("root_x1")
            step(scaled(B(j, 2), ps(j), 3))
        elif stage == "norm4":
            if not source:
                wait(dve, self.stored["out"][j], 16 * it)
            after_act("root4")
            step(scaled(B(j, 4 if source else 5), B(j, 4), 2))
        elif stage == "fold1":
            after_act("exp1")
            step(dve.tensor_scalar(B(j, 2), B(j, 2), -1.0, 0.0, ALU.add, ALU.min))
        elif stage == "elu2" or (stage == "shifted_elu1" and not source):
            after_act("affine" + k)
            step(dve.scalar_tensor_tensor(out=B(j, 4), in0=B(j, 2), scalar=1.0, in1=B(j, 3), op0=ALU.min,
                                          op1=ALU.add))
        elif stage == "join" and self.dve_joins:
            dve.wait_ge(self.dve_s[j], self.DVE.at(it, "elu2"))
            step(dve.tensor_tensor(B(j, 4), B(j, 4), B(j, 1), ALU.add))
        elif stage == "add":
            dve.wait_ge(self.pe_s[j], self.PE.at(it, "sage"))
            step(dve.tensor_tensor(B(j, 4), ps(j), B(j, 3), ALU.add))

    def pool(self, pool, stage, it, j, passed):
        if stage == "elu1" and self.source:
            wait(pool, self.stored["x3"][j], 16 * it)
            pool.wait_ge(self.act_s[j], self.ACT.at(it, "affine1"))
            pool.wait_ge(self.dve_s[j], self.DVE.at(it, "fold1"))
            pool.sem_inc(passed, 1)
            pool.tensor_tensor(self.B(j, 4), self.B(j, 2), self.B(j, 3), ALU.add).then_inc(self.pool_s[j], 1)
        elif stage == "join" and not self.dve_joins:
            pool.wait_ge(self.dve_s[j], self.DVE.at(it, "elu2"))
            pool.sem_inc(passed, 1)
            pool.tensor_tensor(self.B(j, 4), self.B(j, 4), self.B(j, 1), ALU.add).then_inc(self.pool_s[j], 1)


def node_traffic(sp, chain, x, out, node_rows, iterations, slots, base):

    def load(it, j):
        if not first(it):
            sp.wait_ge(chain.pe_s[j], chain.PE.at(it - 1, "turn_x"))
        sp.dma_start(chain.B(j, 0), node_rows(x, base + (it * slots + j))).then_inc(chain.arrived[j], 16)

    def store(it, j):
        sp.wait_ge(chain.dve_s[j], chain.DVE.at(it, "norm4"))
        if j and is_last(it, iterations):
            sp.wait_ge(chain.stored["out"][j - 1], 16 * iterations)
        sp.dma_start(node_rows(out, base + (it * slots + j)), chain.B(j, 5)).then_inc(chain.stored["out"][j], 16)

    return load, store


def gnn_kernel(nc, x, src, dst, edge_attr, edge_weight, ln_gamma, ln_beta, W_obj, b_obj, W_rel,
               b_rel, W1_self, W1_neigh, b1, W2_self, W2_neigh, b2, out):
    N = x.shape[0]
    E = src.shape[0]
    ET = -(-E // P)
    EP = ET * P
    HB = ET // 2
    NG = ET // G
    HI = -(-(N + 1) // (LO * 4)) * 4
    HP = HI // 4
    PAD = HI * LO - 1
    TAIL = E - (ET - 1) * P
    assert ET % (US * G) == 0 and PAD >= N and HP <= P and x.shape[1] == P

    with ExitStack() as root:
        root.enter_context(nc.allow_non_contiguous_dma(reason="small columns and edge id blocks"))

        def sb(name, shape, dt=F32):
            return root.enter_context(nc.sbuf_tensor(name, shape, dt))

        def dram(name, shape, dt=F32):
            return nc.dram_tensor(name, shape, dt).ap()

        level_rows = [None] + [dram(f"level{l}", (2 * EP, P)) for l in range(1, 6)]
        src_x = dram("src_x", (EP, P))
        dst_x = dram("dst_x", (EP, P))
        sums_dram = dram("sums", (NG, P, GW))
        match_dram = dram("match", (NG, P, GW))
        dst_flat = dram("dst_flat", (1, EP))
        ends_dram = dram("ends", (1, 2 * ET))
        ends_mask = dram("ends_mask", (6, EP), BF16)
        carry_dram = dram("carry", (6, EP), BF16)
        bias_dram = dram("bias", (3, 2 * P), BF16)
        node_dram = dram("node", (HI * LO, 4))

        ident = sb("ident", [P, P])
        center = sb("center", [P, P])
        ones3 = sb("ones3", [3, P], BF16)
        upper = sb("upper", [P, P])
        ones_sq = sb("ones_sq", [P, P])
        eps_t = sb("eps_t", [P, 2])
        w_raw = sb("w_raw", [P, 6, P])
        w_use = sb("w_use", [P, 6, P])
        cols = sb("cols", [P, 8])
        bias_row = sb("bias_row", [1, 2, P])
        bias_f = sb("bias_f", [1, 2, P])
        bias_parts = sb("bias_parts", [1, 3, 2, P], BF16)
        bias3 = sb("bias3", [3, 2, P], BF16)
        ids_i = sb("ids_i", [HB, 2, 2, P], I32)
        ids_f = sb("ids_f", [HB, 2, 2, P])
        w_tb = sb("w_tb", [HB, 2, P])
        mask_tb = sb("mask_tb", [HB, 2, 2, P], BF16)
        ends_b = sb("ends_b", [HB, 2, ET])
        reach = sb("reach", [HB, 2, 2, ET])
        srcP = sb("srcP", [P, ET])
        dstP = sb("dstP", [P, ET])
        wP = sb("wP", [P, ET])
        hilo_i = sb("hilo_i", [P, 4, ET], I32)
        hilo = sb("hilo", [P, 4, ET])
        idx_src = sb("idx_src", [P, ET], I32)
        idx_dst = sb("idx_dst", [P, ET], I32)
        idx_node = sb("idx_node", [P, 2 * ET], I32)
        idx_srcn, idx_dstn = idx_node[:, 0:ET], idx_node[:, ET:2 * ET]
        idx_lvl = sb("idx_lvl", [P, ET], I32)
        idx_out = sb("idx_out", [P, ET], I32)
        iota_i = sb("iota_i", [P, HI], I32)
        iota_h = sb("iota_h", [P, HI], F16)
        edge_no = sb("edge_no", [P, ET])
        edge_no_i = sb("edge_no_i", [P, ET], I32)
        info = sb("info", [P, 2, ET, 4])
        info_flat = info.rearrange("p a t f -> p (a t) f")
        w_gcn = sb("w_gcn", [P, ET])
        w_mean = sb("w_mean", [P, ET])
        w_light = sb("w_light", [P, ET])
        tmp = sb("tmp", [P, 3, ET])
        small = sb("small", [P, US, 4, G])
        ring_idx = sb("ring_idx", [P, US, G], I32)
        ends = sb("ends_sb", [P, ET, 2])
        buf = [sb(f"buf{j}", [P, NBUF, GW]) for j in range(US)]
        extra = sb("extra", [P, 6, GW])
        carry_in = [sb(f"carry_in{j}", [6, 2, GW], BF16) for j in range(US)]
        psum = root.enter_context(nc.psum_tensor("psum", [P, US, 1024], F32))

        def edge_rows(ap, g):
            return ap[bass.ds(g * GW, GW), :].rearrange("(k p) d -> p k d", p=P)

        with ExitStack() as ctx:
            sem = phase_semaphores(nc, ctx, "")

            w_in, col_in, ids_in = sem("w_in"), sem("col_in"), sem("ids_in")
            filled, pool_done = sem("filled"), sem("pool_done")
            pe_done, act_done, dve_done = sem("pe_done"), sem("act_done"), sem("dve_done")
            ends_out, ends_in, tb_out = sem("ends_out"), sem("ends_in"), sem("tb_out")
            split, split_out, split_in = sem("split"), sem("split_out"), sem("split_in")
            FULL = ET - 1 - HB
            block = ctx.enter_context(nc.Block())

            @block.sync
            def _(sp):
                sp.wait_ge(filled, 3)
                for a, s in enumerate((src, dst)):
                    sp.dma_start(ids_i[:, a, 0, :], s[0:HB * P].rearrange("(t p) -> t p", p=P)).then_inc(ids_in, 16)
                    sp.dma_start(ids_i[0:FULL, a, 1, :],
                                 s[HB * P:(ET - 1) * P].rearrange("(t p) -> t p", p=P)).then_inc(ids_in, 16)
                    sp.dma_start(ids_i[FULL:HB, a, 1, 0:TAIL],
                                 s[(ET - 1) * P:E].rearrange("(t p) -> t p", t=1)).then_inc(ids_in, 16)
                ew = edge_weight
                sp.dma_start(w_tb[:, 0, :], ew[0:HB * P].rearrange("(t p) -> t p", p=P)).then_inc(ids_in, 16)
                sp.dma_start(w_tb[0:FULL, 1, :],
                             ew[HB * P:(ET - 1) * P].rearrange("(t p) -> t p", p=P)).then_inc(ids_in, 16)
                sp.dma_start(w_tb[FULL:HB, 1, 0:TAIL],
                             ew[(ET - 1) * P:E].rearrange("(t p) -> t p", t=1)).then_inc(ids_in, 16)
                for k, w in enumerate((W_obj, W_rel, W1_self, W1_neigh, W2_self, W2_neigh)):
                    sp.dma_start(w_raw[:, k, :], w).then_inc(w_in, 16)
                sp.dma_start(cols[:, 0:2], ln_gamma.rearrange("l d -> d l")).then_inc(col_in, 16)
                sp.dma_start(cols[:, 2:4], ln_beta.rearrange("l d -> d l")).then_inc(col_in, 16)
                sp.dma_start(cols[:, 4:5], b1.rearrange("(d a) -> d a", a=1)).then_inc(col_in, 16)
                sp.dma_start(cols[:, 5:6], b2.rearrange("(d a) -> d a", a=1)).then_inc(col_in, 16)
                sp.dma_start(bias_row[:, 0, :], b_obj.rearrange("(a d) -> a d", a=1)).then_inc(col_in, 16)
                sp.dma_start(bias_row[:, 1, :], b_rel.rearrange("(a d) -> a d", a=1)).then_inc(col_in, 16)
                sp.wait_ge(dve_done, 4)
                for b in range(2):
                    sp.dma_start(dst_flat[0:1, b * HB * P:(b + 1) * HB * P].rearrange("a (t p) -> (a t) p", p=P),
                                 ids_f[:, 1, b, :]).then_inc(tb_out, 16)
                    for side, at in enumerate((0, P - 1)):
                        lo = side * ET + b * HB
                        sp.dma_start(ends_dram[0:1, lo:lo + HB].rearrange("a (t o) -> (a t) o", o=1),
                                     ids_f[:, 1, b, at:at + 1]).then_inc(ends_out, 16)
                sp.wait_ge(ends_out, 64)
                sp.dma_start(ends_b.rearrange("t s n -> t (s n)"),
                             ends_dram.to_broadcast([HB, 2 * ET])).then_inc(ends_in, 16)
                sp.wait_ge(dve_done, 8)
                for row in range(6):
                    for b in range(2):
                        sp.dma_start(
                            ends_mask[row:row + 1, b * HB * P:(b + 1) * HB * P].rearrange("a (t p) -> (a t) p", p=P),
                            mask_tb[:, row // 3, b, :]).then_inc(tb_out, 16)
                sp.wait_ge(split, 6)
                sp.dma_start(bias_dram.rearrange("k (b d) -> (k b) d", d=P).unsqueeze(0),
                             bias_parts.rearrange("a k b d -> a (k b) d")).then_inc(split_out, 16)
                sp.wait_ge(split_out, 16)
                sp.dma_start(bias3.rearrange("k b d -> k (b d)"), bias_dram).then_inc(split_in, 16)
                sp.wait_ge(split_in, 16)
                sp.wait_ge(tb_out, 32 + 192)

            @block.gpsimd
            def _(pool):
                pool.iota(ids_i[:, :, :, :], [[0, 2 * 2 * P]], base=PAD, channel_multiplier=0).then_inc(filled, 1)
                pool.memset(w_tb[:, :, :], 0.0).then_inc(filled, 1)
                pool.memset(ones3[:, :], 1.0).then_inc(filled, 1)
                pool.memset(ones_sq[:, :], 1.0).then_inc(pool_done, 1)
                pool.memset(ident[:, :], 0.0).then_inc(pool_done, 1)
                pool.wait_ge(pool_done, 2)
                pool.affine_select(out=ident[:, :], in_=ident[:, :], compare_op=ALU.not_equal, fill=1.0, base=0,
                                   pattern=[[-1, P]], channel_multiplier=1).then_inc(pool_done, 1)
                pool.affine_select(out=upper[:, :], in_=ones_sq[:, :], compare_op=ALU.is_gt, fill=0.0, base=0,
                                   pattern=[[1, P]], channel_multiplier=-1).then_inc(pool_done, 1)
                pool.iota(iota_i[:, :], [[1, HI]], base=0, channel_multiplier=0).then_inc(pool_done, 1)
                pool.iota(edge_no_i[:, :], [[P, ET]], base=0, channel_multiplier=1).then_inc(pool_done, 1)
                pool.memset(eps_t[:, 0:1], EPS).then_inc(pool_done, 1)
                pool.memset(eps_t[:, 1:2], EPS * EPS).then_inc(pool_done, 1)
                pool.wait_ge(dve_done, 12)
                for b in range(2):
                    pool.affine_select(out=reach[:, 0, b, :], in_=reach[:, 0, b, :], compare_op=ALU.is_gt, fill=0.0,
                                       base=-b * HB, pattern=[[1, ET]], channel_multiplier=-1).then_inc(pool_done, 1)
                    pool.affine_select(out=reach[:, 1, b, :], in_=reach[:, 1, b, :], compare_op=ALU.is_gt, fill=0.0,
                                       base=b * HB, pattern=[[-1, ET]], channel_multiplier=1).then_inc(pool_done, 1)

            @block.tensor
            def _(pe):
                pe.wait_ge(pool_done, 3)
                pe.wait_ge(w_in, 96)
                for k in range(4):
                    pe.transpose(psum[:, 0, k * P:(k + 1) * P], w_raw[:, k, :], ident[:, :])
                pe.wait_ge(dve_done, 5)
                for k in range(4, 6):
                    pe.matmul(psum[:, 0, k * P:(k + 1) * P], w_raw[:, k, :], center[:, :], start=True, stop=True)
                pe.wait_ge(col_in, 96)
                pe.matmul(psum[0:1, 1, 0:P], cols[:, 5:6], center[:, :], start=True, stop=True).then_inc(pe_done, 1)
                for b in range(2):
                    pe.transpose(psum[:, 2, b * HB:(b + 1) * HB], ids_f[:, 0, b, :], ident[0:HB, 0:HB])
                for b in range(2):
                    pe.transpose(psum[:, 2, 512 + b * HB:512 + (b + 1) * HB], ids_f[:, 1, b, :], ident[0:HB, 0:HB])
                for b in range(2):
                    mm = pe.transpose(psum[:, 3, b * HB:(b + 1) * HB], w_tb[:, b, :], ident[0:HB, 0:HB])
                mm.then_inc(pe_done, 1)

            @block.scalar
            def _(act):
                act.wait_ge(pe_done, 1)
                act.copy(w_use.rearrange("p k d -> p (k d)"), psum[:, 0, 0:6 * P]).then_inc(act_done, 1)
                act.copy(bias_f[:, 1, :], psum[0:1, 1, 0:P]).then_inc(act_done, 1)

            @block.vector
            def _(dve):
                dve.wait_ge(ids_in, 144)
                for a in range(2):
                    for b in range(2):
                        dve.tensor_copy(ids_f[:, a, b, :], ids_i[:, a, b, :]).then_inc(dve_done, 1)
                dve.wait_ge(pool_done, 3)
                dve.tensor_scalar(center[:, :], ident[:, :], 1.0 / P, None, ALU.subtract).then_inc(dve_done, 1)
                dve.wait_ge(dve_done, 4)
                for b in range(2):
                    for side, at in enumerate((0, P - 1)):
                        ins = dve.tensor_scalar(mask_tb[:, side, b, :], ids_f[:, 1, b, :],
                                                ids_f[:, 1, b, at:at + 1], None, ALU.is_equal)
                        if (b, side) != (0, 0):
                            ins.then_inc(dve_done, 1)
                dve.wait_ge(ends_in, 16)
                for b in range(2):
                    for side, at in enumerate((P - 1, 0)):
                        dve.tensor_scalar(reach[:, side, b, :], ends_b[:, side, :], ids_f[:, 1, b, at:at + 1],
                                          None, ALU.is_equal).then_inc(dve_done, 1)
                dve.wait_ge(pool_done, 8)
                dve.tensor_copy(iota_h[:, :], iota_i[:, :]).then_inc(dve_done, 1)
                dve.tensor_copy(edge_no[:, :], edge_no_i[:, :]).then_inc(dve_done, 1)
                dve.wait_ge(col_in, 96)
                dve.scalar_tensor_tensor(out=bias_f[:, 0, :], in0=bias_row[:, 0, :], scalar=2.0, in1=bias_row[:, 1, :],
                                         op0=ALU.mult, op1=ALU.add).then_inc(dve_done, 1)
                dve.wait_ge(pe_done, 2)
                dve.tensor_copy(srcP[:, :], psum[:, 2, 0:ET]).then_inc(dve_done, 1)
                dve.tensor_copy(dstP[:, :], psum[:, 2, 512:512 + ET]).then_inc(dve_done, 1)
                dve.tensor_copy(wP[:, :], psum[:, 3, 0:ET]).then_inc(dve_done, 1)
                dve.wait_ge(dve_done, 18)
                dve.tensor_copy(idx_srcn, srcP[:, :]).then_inc(dve_done, 1)
                dve.tensor_copy(idx_dstn, dstP[:, :]).then_inc(dve_done, 1)
                dve.tensor_scalar(idx_src[:, :], srcP[:, :], float(N - 1), None, ALU.min).then_inc(dve_done, 1)
                dve.tensor_scalar(idx_dst[:, :], dstP[:, :], float(N - 1), None, ALU.min).then_inc(dve_done, 1)
                dve.wait_ge(dve_done, 20)
                for a, ids in enumerate((idx_srcn, idx_dstn)):
                    dve.tensor_scalar(hilo_i[:, 2 * a, :], ids, LO.bit_length() - 1, None,
                                      ALU.logical_shift_right).then_inc(dve_done, 1)
                    dve.tensor_scalar(hilo_i[:, 2 * a + 1, :], ids, LO - 1, None,
                                      ALU.bitwise_and).then_inc(dve_done, 1)
                dve.wait_ge(dve_done, 26)
                dve.tensor_copy(hilo.rearrange("p a t -> p (a t)"),
                                hilo_i.rearrange("p a t -> p (a t)")).then_inc(dve_done, 1)
                dve.wait_ge(act_done, 2)
                dve.wait_ge(dve_done, 15)
                for k in range(3):
                    if k:
                        dve.wait_ge(split, 2 * k)
                    dve.tensor_copy(bias_parts[:, k, :, :], bias_f[:, :, :]).then_inc(split, 1)
                    dve.wait_ge(split, 2 * k + 1)
                    dve.tensor_tensor(bias_f[:, :, :], bias_f[:, :, :], bias_parts[:, k, :, :], ALU.subtract
                                      ).then_inc(split, 1)

        DENSE = -(-N // GW)
        DENSE_IT = 13
        SRC_IT = EP // ROWS
        assert SRC_IT * ROWS == EP
        assert DENSE_IT * US + len(BESIDE) * BESIDE_IT * BESIDE_SLOTS == DENSE and 2 * NG == (DENSE_IT + 1) * US

        def node_rows(ap, q):
            lo = min(q * GW, N - GW) if isinstance(q, int) else q * GW
            return ap[bass.ds(lo, GW), :].rearrange("(p k) d -> p (k d)", p=P)

        with ExitStack() as ctx:
            sem = phase_semaphores(nc, ctx, "")

            HR = 14
            onehot = ctx.enter_context(nc.sbuf_tensor("onehot", [P, HR, HI + LO], F16))
            flat3 = buf[3].rearrange("p b w -> p (b w)")
            node = flat3[0:HP, 0:16 * LO].rearrange("p (b l f) -> p b l f", b=4, f=4)
            incl = flat3[0:HP, 16 * LO:20 * LO].rearrange("p (b l) -> p b l", b=4)
            tot = ctx.enter_context(nc.sbuf_tensor("tot", [HP, 8], F32))
            ring_info = ctx.enter_context(nc.sbuf_tensor("ring_info", [P, US, G, 4], F32))
            hot_ready, hot_used = sem("hot_ready"), sem("hot_used")
            counted, tab_dve, tab_pe, node_out = sem("counted"), sem("tab_dve"), sem("tab_pe"), sem("node_out")
            dstrow_in, match_ready = [sem(f"dstrow_in{p}") for p in range(2)], sem("match_ready")
            match_out = [sem(f"match_out{p}") for p in range(2)]
            idx_copied, ring_free = sem("idx_copied"), sem("ring_free")
            rows_in = [sem(f"rows_in{p}") for p in range(2)]
            rows_out = [sem(f"rows_out{p}") for p in range(2)]
            info_in = [sem(f"info_in{p}") for p in range(US)]
            info_copied = sem("info_copied")

            D_PLAN = Plan("keep 394 ask0 546 ask1 833 ask2 1030 turn_x 8 copy_x 217 centre1 235 square1 237 "
                          "sum1 246 root1 343 norm1 373 turn1 388 exp1 439 affine1 443 shifted_elu1 456 "
                          "centre2 460 square2 478 sum2 485 root2 486 norm2 491 turn2 562 exp2 586 affine2 630 "
                          "elu2 636 join 695 centre3 705 square3 725 sum3 731 root3 734 norm3 740 turn3 759 "
                          "copy3 811 hidden 866 relu 888 sage 926 add 981 square4 985 sum4 1025 root4 1172 "
                          "norm4 1179")
            S_PLAN = Plan("match 103 turn_x 24 copy_x 81 centre1 129 square1 135 sum1 197 root1 223 norm1 257 "
                          "turn1 271 exp1 273 affine1 309 fold1 275 elu1 311 turn_y 345 rows_y 367 centre2 415 "
                          "square2 434 sum2 439 root2 468 norm2 477 turn2 491 exp2 492 affine2 493 elu2 514 "
                          "join 532 centre3 581 square3 590 sum3 623 root3 633 norm_x1 649 norm3 671 turn3 685 "
                          "copy3 699 hidden 730 relu 736 turn_h 743 rows_h 743 sage 810 add 815 square4 923 "
                          "sum4 979 root4 1025 norm4 1066", shift=90)
            dense_chain = Chain(locals(), sem, "d")
            source_chain = Chain(locals(), sem, "s", source=True, after=(dense_chain, DENSE_IT))
            block = ctx.enter_context(nc.Block())

            def B(j, k):
                return buf[j][:, k, :]

            def wide(ap):
                return ap.rearrange("p (k d) -> p k d", d=P)

            def flat_rows(ap, lo):
                return ap[bass.ds(lo, GW), :].rearrange("(p k) d -> p (k d)", p=P)

            def dense_then_source(engine, dense, source):
                staggered(engine, DENSE_IT, D_PLAN, dense, drain=False)
                staggered(engine, SRC_IT, S_PLAN, source, before=(DENSE_IT, D_PLAN, dense))

            @block.sync
            def _(sp):
                def load_dst(g, p):
                    sp.dma_start(extra[:, p, :], dst_flat[0:1, bass.ds(g * GW, GW)].to_broadcast([P, GW])
                                 ).then_inc(dstrow_in[p], 16)

                def store_match(g, p):
                    sp.dma_start(match_dram[bass.ds(g, 1)].rearrange("a p w -> (a p) w"), extra[:, 2 + p, :]
                                 ).then_inc(match_out[p], 16)

                for p in range(2):
                    load_dst(p, p)
                sp.wait_ge(tab_dve, 17)
                sp.dma_start(node_dram.rearrange("(b p l) f -> p b (l f)", p=HP, l=LO),
                             node.rearrange("p b l f -> p b (l f)")).then_inc(node_out, 16)

                dense_load, dense_store = node_traffic(sp, dense_chain, x, out, node_rows, DENSE_IT, US, 0)
                for j in range(US):
                    if j == 3:
                        sp.wait_ge(node_out, 16)
                    dense_load(0, j)

                def dense(stage, it, j):
                    if stage == "copy_x":
                        if is_last(it, DENSE_IT):
                            sp.wait_ge(dense_chain.pe_s[j], dense_chain.PE.at(it, "turn_x"))
                            load_s(0, j)
                        else:
                            dense_load(it + 1, j)
                    if stage == "norm4":
                        dense_store(it, j)

                for p in range(2):
                    sp.wait_ge(rows_out[p], 8 * NG)

                c = source_chain

                def load_s(it, j):
                    sp.dma_start(B(j, 0), flat_rows(src_x, it * ROWS + j * GW)).then_inc(c.arrived[j], 16)

                def store_s(l, it, j, k, name):
                    sp.dma_start(flat_rows(level_rows[l], EP + (it * ROWS + j * GW)), B(j, k)
                                 ).then_inc(c.stored[name][j], 16)

                def source(name, it, j):
                    if name == "match":
                        sp.wait_ge(match_ready, US * it + (j + 1))
                        store_match(US * it + j, j % 2)
                        if not (is_last(it, SRC_IT) and j >= US - 2):
                            load_dst(US * it + (j + 2), j % 2)
                    if name == "copy_x" and not is_last(it, SRC_IT):
                        sp.wait_ge(c.pe_s[j], c.PE.at(it, "turn_x"))
                        load_s(it + 1, j)
                    if name == "rows_y":
                        sp.wait_ge(c.act_s[j], c.ACT.at(it, "rows_y"))
                        store_s(1, it, j, 5, "y1")
                    if name == "norm3":
                        sp.wait_ge(c.dve_s[j], c.DVE.at(it, "norm3"))
                        store_s(2, it, j, 2, "x1")
                        store_s(3, it, j, 3, "x2")
                    if name == "rows_h":
                        sp.wait_ge(c.act_s[j], c.ACT.at(it, "rows_h"))
                        store_s(4, it, j, 5, "h1")
                    if name == "norm4":
                        sp.wait_ge(c.dve_s[j], c.DVE.at(it, "norm4"))
                        store_s(5, it, j, 4, "x3")

                dense_then_source(sp, dense, source)
                for j in range(US):
                    sp.wait_ge(dense_chain.stored["out"][j], 16 * DENSE_IT)
                    for s in c.stored.values():
                        sp.wait_ge(s[j], 16 * SRC_IT)
                for p in range(2):
                    sp.wait_ge(match_out[p], 8 * NG)

            @block.gpsimd
            def _(pool):
                def ask_rows(ids, g, p, count):
                    pool.tensor_copy(ring_idx[:, p, :], ids[:, bass.ds(g * G, G)]).then_inc(idx_copied, 1)
                    pool.wait_ge(idx_copied, count)
                    pool.sem_inc(ring_free, 1)
                    for k in range(G):
                        pool.indirect_dma_start(
                            out=extra[:, 4 + p, k * P:(k + 1) * P], out_offset=None, in_=x,
                            in_offset=bass.IndirectOffsetOnAxis(ap=ring_idx[:, p, k:k + 1], axis=0),
                        ).then_inc(rows_in[p], 16)

                def pair(i):
                    for p in range(2):
                        wait(pool, rows_out[p], 16 * i)
                        ask_rows(idx_src, 2 * i + p, p, 2 * i + (p + 1))
                pair(0)
                with pool.Fori(1, NG // 2) as i:
                    pair(i)
                for p in range(2):
                    pool.wait_ge(rows_out[p], 8 * NG)

                pool.wait_ge(node_out, 16)

                def ask_info(it, j, tiles):
                    for k in tiles:
                        pool.indirect_dma_start(
                            out=ring_info[:, j, k, :], out_offset=None, in_=node_dram,
                            in_offset=bass.IndirectOffsetOnAxis(ap=ring_idx[:, j, k:k + 1], axis=0),
                        ).then_inc(info_in[j], 16)

                def take_ids(group, j):
                    pool.tensor_copy(ring_idx[:, j, :], idx_node[:, bass.ds(group * G, G)]).then_inc(idx_copied, 1)

                def keep_info(it, j):
                    pool.wait_ge(info_in[j], 16 * G * it + 16 * G)
                    pool.sem_inc(ring_free, 1)
                    pool.tensor_copy(info_flat[:, bass.ds((US * it + j) * G, G), :], ring_info[:, j, :, :]
                                     ).then_inc(info_copied, 1)

                for j in range(US):
                    take_ids(j, j)
                for j in range(US):
                    pool.wait_ge(idx_copied, NG + j + 1)
                    ask_info(0, j, range(G))

                def dense(stage, it, j):
                    if stage == "keep":
                        keep_info(it, j)
                        take_ids(US * it + (US + j), j)
                    if stage == "ask0":
                        pool.wait_ge(idx_copied, it * US + (NG + US + j + 1))
                        pool.wait_ge(info_copied, it * US + (j + 1))
                        pool.sem_inc(ring_free, 1)
                        ask_info(it, j, (0, 1))
                    if stage == "ask1":
                        ask_info(it, j, (2, 3))
                    if stage == "ask2":
                        ask_info(it, j, (4, 5, 6))
                    dense_chain.pool(pool, stage, it, j, ring_free)

                def source(stage, it, j):
                    if stage == "join" and first(it):
                        keep_info(DENSE_IT, j)
                    source_chain.pool(pool, stage, it, j, ring_free)

                dense_then_source(pool, dense, source)

            @block.tensor
            def _(pe):
                def bank(a, b):
                    return psum[0:HP, 2 * a + b // 2, (b % 2) * 512:(b % 2) * 512 + LO]

                for a in range(2):
                    def count(i, q, first):
                        pe.wait_ge(hot_ready, i * HR + (a * ET + q + 1))
                        for b in range(4):
                            mm = pe.matmul(bank(a, b), onehot[:, q, b * HP:(b + 1) * HP], onehot[:, q, HI:HI + LO],
                                           start=first, stop=False)
                        mm.then_inc(hot_used, 1)
                    for q in range(HR):
                        count(0, q, q == 0)
                    with pe.Fori(1, ET // HR) as i:
                        for q in range(HR):
                            count(i, q, False)
                pe.wait_ge(tab_dve, 1)
                for a in range(2):
                    for b in range(4):
                        mm = pe.matmul(bank(a, b), onehot[:, 0, b * HP:(b + 1) * HP], onehot[:, 1, HI:HI + LO],
                                       start=False, stop=True)
                mm.then_inc(counted, 1)
                pe.wait_ge(tab_dve, 12)
                pe.matmul(psum[0:HP, 0, 0:4], upper[0:HP, 0:HP], tot[:, 0:4], start=True, stop=False)
                pe.matmul(psum[0:HP, 0, 0:4], ones_sq[0:HP, 0:HP], tot[:, 4:8], start=False,
                          stop=True).then_inc(tab_pe, 1)
                pe.wait_ge(tab_dve, 17)

                dense_then_source(pe, lambda stage, it, j: dense_chain.pe(pe, stage, it, j),
                                  lambda stage, it, j: source_chain.pe(pe, stage, it, j))

            @block.scalar
            def _(act):
                act.preload_act_table_set("natural_log_exp_and_others")
                with act.Fori(0, NG // 2) as i:
                    for p in range(2):
                        act.wait_ge(rows_in[p], i * (16 * G) + 16 * G)
                        act.dma_start(edge_rows(src_x, 2 * i + p), wide(extra[:, 4 + p, :])).then_inc(rows_out[p], 16)

                dense_then_source(act, lambda stage, it, j: dense_chain.act(act, stage, it, j),
                                  lambda stage, it, j: source_chain.act(act, stage, it, j))

            @block.vector
            def _(dve):
                for a in range(2):
                    def hot(i, q, wait):
                        t = i * HR + q
                        if wait:
                            dve.wait_ge(hot_used, a * ET + t - HR + 1)
                        dve.tensor_scalar(onehot[:, q, 0:HI], iota_h[:, :], hilo[:, 2 * a, bass.ds(t, 1)], None,
                                          ALU.is_equal)
                        dve.tensor_scalar(onehot[:, q, HI:HI + LO], iota_h[:, 0:LO],
                                          hilo[:, 2 * a + 1, bass.ds(t, 1)], None, ALU.is_equal
                                          ).then_inc(hot_ready, 1)
                    for q in range(HR):
                        hot(0, q, a > 0)
                    with dve.Fori(1, ET // HR) as i:
                        for q in range(HR):
                            hot(i, q, True)
                dve.wait_ge(hot_used, 2 * ET)
                dve.memset(onehot[:, 1, HI:HI + LO], 0.0).then_inc(tab_dve, 1)

                dve.wait_ge(counted, 1)
                for a, f in enumerate((2, 1)):
                    for h in range(2):
                        dve.tensor_copy(node[:, 2 * h:2 * h + 2, :, f],
                                        psum[0:HP, 2 * a + h, :].rearrange("p (b w) -> p b w", b=2)[:, :, 0:LO]
                                        ).then_inc(tab_dve, 1)
                dve.memset(node[:, :, :, 3], 0.0).then_inc(tab_dve, 1)
                dve.wait_ge(tab_dve, 6)
                for b in range(4):
                    dve.tensor_tensor_scan(incl[:, b, :], node[:, b, :, 1], node[:, b, :, 3], 0.0, ALU.add, ALU.add
                                           ).then_inc(tab_dve, 1)
                dve.wait_ge(tab_dve, 10)
                dve.tensor_copy(tot[:, 0:4], incl[:, :, LO - 1])
                dve.memset(tot[:, 4:5], 0.0)
                dve.tensor_copy(tot[:, 5:6], incl[:, 0, LO - 1:LO])
                dve.tensor_tensor(tot[:, 6:7], incl[:, 0, LO - 1:LO], incl[:, 1, LO - 1:LO], ALU.add
                                  ).then_inc(tab_dve, 1)
                dve.wait_ge(tab_dve, 11)
                dve.tensor_tensor(tot[:, 7:8], tot[:, 6:7], incl[:, 2, LO - 1:LO], ALU.add
                                  ).then_inc(tab_dve, 1)
                dve.wait_ge(tab_pe, 1)
                dve.tensor_copy(tot[:, 0:4], psum[0:HP, 0, 0:4]).then_inc(tab_dve, 1)
                dve.wait_ge(tab_dve, 13)
                for b in range(4):
                    dve.scalar_tensor_tensor(out=node[:, b, :, 0], in0=incl[:, b, :], scalar=tot[:, b:b + 1],
                                             in1=node[:, b, :, 1], op0=ALU.add, op1=ALU.subtract
                                             ).then_inc(tab_dve, 1)

                def source(stage, it, j):
                    if stage == "match":
                        p, n = j % 2, US * it + j
                        dve.wait_ge(dstrow_in[p], it * (US * 8) + (j // 2 * 16 + 16))
                        wait(dve, match_out[p], it * (US * 8) + j // 2 * 16)
                        dve.tensor_tensor(wide(extra[:, 2 + p, :]), wide(extra[:, p, :]),
                                          dstP[:, bass.ds(n * G, G)].unsqueeze(2).to_broadcast([P, G, P]),
                                          ALU.is_equal).then_inc(match_ready, 1)
                    source_chain.dve(dve, stage, it, j)

                dense_then_source(dve, lambda stage, it, j: dense_chain.dve(dve, stage, it, j), source)

        with ExitStack() as ctx:
            sem = phase_semaphores(nc, ctx, "")

            v, a = sem("wt_dve"), sem("wt_act")
            block = ctx.enter_context(nc.Block())
            out_src, out_dst, in_dst = info[:, 0, :, 2], info[:, 1, :, 2], info[:, 1, :, 1]
            in_src, first_src, first_dst = info[:, 0, :, 1], info[:, 0, :, 0], info[:, 1, :, 0]

            @block.vector
            def _(dve):
                dve.tensor_tensor(tmp[:, 0, :], out_src, in_dst, ALU.mult).then_inc(v, 1)
                dve.tensor_scalar(w_light[:, :], out_dst, 1.0, None, ALU.max).then_inc(v, 1)
                dve.wait_ge(v, 2)
                dve.tensor_tensor(tmp[:, 1, :], out_src, w_light[:, :], ALU.mult).then_inc(v, 1)
                dve.reciprocal(w_mean[:, :], in_dst).then_inc(v, 1)
                dve.tensor_scalar(tmp[:, 2, :], in_src, 0.5, None, ALU.is_gt).then_inc(v, 1)
                dve.tensor_scalar(edge_no[:, :], edge_no[:, :], float(EP), None, ALU.add).then_inc(v, 1)
                dve.wait_ge(v, 6)
                dve.tensor_tensor(first_src, first_src, edge_no[:, :], ALU.subtract).then_inc(v, 1)
                dve.wait_ge(v, 7)
                dve.tensor_tensor(first_src, first_src, tmp[:, 2, :], ALU.mult).then_inc(v, 1)
                dve.wait_ge(v, 8)
                dve.tensor_tensor(first_src, first_src, edge_no[:, :], ALU.add).then_inc(v, 1)
                dve.wait_ge(v, 9)
                dve.tensor_copy(idx_lvl[:, :], first_src).then_inc(v, 1)
                dve.tensor_scalar(edge_no[:, :], edge_no[:, :], -float(EP), None, ALU.add).then_inc(v, 1)
                dve.wait_ge(v, 11)
                dve.tensor_tensor(tmp[:, 2, :], first_dst, edge_no[:, :], ALU.not_equal).then_inc(v, 1)
                dve.wait_ge(v, 12)
                dve.scalar_tensor_tensor(out=tmp[:, 2, :], in0=tmp[:, 2, :], scalar=float(4 * HI * LO), in1=dstP[:, :],
                                         op0=ALU.mult, op1=ALU.add).then_inc(v, 1)
                dve.wait_ge(v, 13)
                dve.tensor_copy(idx_out[:, :], tmp[:, 2, :]).then_inc(v, 1)
                dve.wait_ge(a, 4)
                dve.tensor_tensor(w_gcn[:, :], tmp[:, 0, :], wP[:, :], ALU.mult).then_inc(v, 1)

            @block.scalar
            def _(act):
                act.wait_ge(v, 3)
                act.activation(tmp[:, 0, :], tmp[:, 0, :], ACT.Ln).then_inc(a, 1)
                act.activation(tmp[:, 1, :], tmp[:, 1, :], ACT.Ln).then_inc(a, 1)
                act.wait_ge(a, 2)
                act.activation(tmp[:, 0, :], tmp[:, 0, :], ACT.Exp, scale=-0.5).then_inc(a, 1)
                act.activation(w_light[:, :], tmp[:, 1, :], ACT.Exp, scale=-0.5).then_inc(a, 1)

        weights = [w_gcn, w_gcn, None, w_mean, w_mean, w_light]
        tables = [src_x] + level_rows[1:6]
        dst_tables = [dst_x] + level_rows[1:6]
        for level in range(6):
            if level in BESIDE:
                gather_beside_dense(nc, locals(), level, weights[level], tables[level])
            else:
                sum_relational(nc, locals(), level, tables[level], dst_tables[level])
            carry_sums(nc, locals(), level)
            update_rows(nc, locals(), level, dst_tables)


def gather_beside_dense(nc, env, level, weight, table):
    buf, extra, psum, ring_idx, idx_lvl, ends = (
        env[k] for k in ("buf", "extra", "psum", "ring_idx", "idx_lvl", "ends"))
    match_dram, sums_dram, node_rows, NG = (env[k] for k in ("match_dram", "sums_dram", "node_rows", "NG"))
    edge_rows = env["edge_rows"]
    N_IT, SLOTS, EDGES = BESIDE_IT, BESIDE_SLOTS, BESIDE_EDGES
    assert EDGES == 7 and NG == N_IT * EDGES
    edge_stages = dict.fromkeys(("gask", "weigh", "gsum", "gcopy", "ends", "keep"), EDGES)
    if level == 0:
        PLAN = Plan("gask 115 weigh 231 gsum 461 gcopy 515 ends 671 keep 351 turn_x 150 copy_x 211 centre1 272 "
                    "square1 278 sum1 300 root1 319 norm1 331 turn1 369 exp1 399 affine1 430 shifted_elu1 436 "
                    "centre2 467 square2 541 sum2 545 root2 550 norm2 562 turn2 624 exp2 648 affine2 653 "
                    "elu2 694 join 737 centre3 761 square3 813 sum3 849 root3 882 norm3 893 turn3 943 "
                    "copy3 974 hidden 981 relu 988 sage 1070 add 1095 square4 1109 sum4 1137 root4 1150 "
                    "norm4 1207",
                    copies=SLOTS, others=edge_stages)
    else:
        PLAN = Plan("gask 270 weigh 621 gsum 665 gcopy 698 ends 861 turn_x 41 copy_x 51 centre1 106 "
                    "square1 157 sum1 186 root1 191 norm1 245 turn1 302 exp1 315 affine1 322 shifted_elu1 380 "
                    "centre2 385 square2 409 sum2 440 root2 463 norm2 469 turn2 513 exp2 537 affine2 544 "
                    "elu2 626 join 664 centre3 683 square3 699 sum3 735 root3 745 norm3 781 turn3 831 "
                    "copy3 848 hidden 849 relu 884 sage 984 add 997 square4 1005 sum4 1048 root4 1048 "
                    "norm4 1097",
                    copies=SLOTS, others=edge_stages)
    base = env["DENSE_IT"] * US + BESIDE.index(level) * N_IT * SLOTS
    rows = [buf[3][:, k, :] for k in range(4)]
    match = [buf[3][:, 4, :], buf[3][:, 5, :], extra[:, 0, :], extra[:, 1, :]]
    sums = [extra[:, 2 + k, :] for k in range(3)]
    psum_sum = psum[:, US - 1, 0:GW]
    IN = [0, 1, 2, 0, 1, 2, 3]
    IN_BACK = [4, 4, 4, 3, 3, 3, 7]
    IN_USES = [2, 2, 2, 1]
    OUT = [0, 1, 0, 1, 0, 1, 2]
    OUT_BACK = [3, 3, 2, 2, 2, 2, 7]
    OUT_USES = [3, 3, 1]

    def in_use(it, p):
        return it * IN_USES[IN[p]] + IN[:p + 1].count(IN[p])

    def out_use(it, p):
        return it * OUT_USES[OUT[p]] + OUT[:p + 1].count(OUT[p])

    def wide(ap):
        return ap.rearrange("p (k d) -> p k d", d=P)

    with ExitStack() as ctx:
        sem = phase_semaphores(nc, ctx, f"_{level}")
        chain = Chain(env, sem, "b", dve_joins=True, slots=SLOTS)
        gathered, match_in = ([sem(f"{n}{b}") for b in range(4)] for n in ("gathered", "b_match_in"))
        sums_out = [sem(f"b_sums_out{b}") for b in range(3)]
        weighed, summed, copied, taken = (sem(n) for n in ("weighed", "summed", "copied", "ends_taken"))
        idx_copied, passed = sem("b_idx"), sem("b_passed")
        if level == 0:
            fetch = ctx.enter_context(nc.sbuf_tensor("fetch", [P, 3, GW], F32))
            fetched, fetched_out = ([sem(f"{n}{b}") for b in range(3)] for n in ("fetched", "fetched_out"))
        block = ctx.enter_context(nc.Block())

        @block.sync
        def _(sp):
            load, store = node_traffic(sp, chain, env["x"], env["out"], node_rows, N_IT, SLOTS, base)
            for j in range(SLOTS):
                load(0, j)

            def body(stage, it, j):
                n = EDGES * it + j
                if stage == "gask":
                    wait(sp, summed, n + (1 - IN_BACK[j]))
                    sp.dma_start(match[IN[j]], match_dram[bass.ds(n, 1)].rearrange("a p w -> (a p) w")
                                 ).then_inc(match_in[IN[j]], 16)
                    if level == 0:
                        sp.dma_start(wide(rows[IN[j]]), edge_rows(table, n)).then_inc(gathered[IN[j]], 16)
                elif stage == "keep":
                    sp.wait_ge(fetched[OUT[j]], 16 * G * out_use(it, j))
                    sp.dma_start(edge_rows(env["dst_x"], n), wide(fetch[:, OUT[j], :])
                                 ).then_inc(fetched_out[OUT[j]], 16)
                elif stage == "ends":
                    sp.wait_ge(copied, n + 1)
                    sp.dma_start(sums_dram[bass.ds(n, 1)].rearrange("a p w -> (a p) w"), sums[OUT[j]]
                                 ).then_inc(sums_out[OUT[j]], 16)
                elif stage == "copy_x" and not is_last(it, N_IT):
                    load(it + 1, j)
                elif stage == "norm4":
                    store(it, j)

            staggered(sp, N_IT, PLAN, body)
            for b in range(3):
                sp.wait_ge(sums_out[b], 16 * OUT_USES[b] * N_IT)
                if level == 0:
                    sp.wait_ge(fetched_out[b], 16 * OUT_USES[b] * N_IT)
            for j in range(SLOTS):
                sp.wait_ge(chain.stored["out"][j], 16 * N_IT)

        @block.gpsimd
        def _(pool):
            def body(stage, it, j):
                if stage == "gask":
                    n = EDGES * it + j
                    if level == 0:
                        b, ids, source, to, arrived = OUT[j], env["idx_dst"], env["x"], fetch[:, OUT[j], :], fetched
                        wait(pool, fetched_out[b], 16 * (out_use(it, j) - 1))
                    else:
                        b, ids, source, to, arrived = IN[j], idx_lvl, table, rows[IN[j]], gathered
                        wait(pool, summed, n + (1 - IN_BACK[j]))
                    pool.sem_inc(passed, 1)
                    pool.tensor_copy(ring_idx[:, b, :], ids[:, bass.ds(n * G, G)]).then_inc(idx_copied, 1)
                    pool.wait_ge(idx_copied, n + 1)
                    pool.sem_inc(passed, 1)
                    for k in range(G):
                        pool.indirect_dma_start(
                            out=to[:, k * P:(k + 1) * P], out_offset=None, in_=source,
                            in_offset=bass.IndirectOffsetOnAxis(ap=ring_idx[:, b, k:k + 1], axis=0),
                        ).then_inc(arrived[b], 16)

            staggered(pool, N_IT, PLAN, body)

        @block.tensor
        def _(pe):
            def body(stage, it, j):
                if stage == "gsum":
                    n, b = EDGES * it + j, IN[j]
                    pe.wait_ge(weighed, n + 1)
                    pe.wait_ge(match_in[b], 16 * in_use(it, j))
                    wait(pe, copied, n)
                    for k in range(G):
                        at = slice(k * P, (k + 1) * P)
                        mm = pe.matmul(psum_sum[:, at], rows[b][:, at], match[b][:, at], start=True, stop=True)
                    mm.then_inc(summed, 1)
                else:
                    chain.pe(pe, stage, it, j)

            staggered(pe, N_IT, PLAN, body)

        @block.vector
        def _(dve):
            def body(stage, it, j):
                n = EDGES * it + j
                if stage == "weigh":
                    b = IN[j]
                    dve.wait_ge(gathered[b], (16 if level == 0 else 16 * G) * in_use(it, j))
                    w = weight[:, bass.ds(n * G, G)].unsqueeze(2).to_broadcast([P, G, P])
                    dve.tensor_tensor(wide(rows[b]), wide(rows[b]), w, ALU.mult).then_inc(weighed, 1)
                elif stage == "ends":
                    dve.wait_ge(copied, n + 1)
                    dve.tensor_copy(ends[:, bass.ds(n * G, G), :], wide(sums[OUT[j]])[:, :, 0:P:P - 1]
                                    ).then_inc(taken, 1)
                else:
                    chain.dve(dve, stage, it, j)

            staggered(dve, N_IT, PLAN, body)

        @block.scalar
        def _(act):
            def body(stage, it, j):
                if stage == "gcopy":
                    n = EDGES * it + j
                    act.wait_ge(summed, n + 1)
                    wait(act, taken, n + (1 - OUT_BACK[j]))
                    wait(act, sums_out[OUT[j]], 16 * (out_use(it, j) - 1))
                    act.copy(sums[OUT[j]], psum_sum).then_inc(copied, 1)
                else:
                    chain.act(act, stage, it, j)

            staggered(act, N_IT, PLAN, body)


def sum_relational(nc, env, level, table, dst_table):
    buf, extra, psum, ident, w_use = (env[k] for k in ("buf", "extra", "psum", "ident", "w_use"))
    match_dram, sums_dram, edge_attr, ends = (env[k] for k in ("match_dram", "sums_dram", "edge_attr", "ends"))
    ring_idx, idx_lvl, ones3, bias3 = env["ring_idx"], env["idx_lvl"], env["ones3"], env["bias3"]
    edge_rows, NG, E, TAIL, EP = env["edge_rows"], env["NG"], env["E"], env["TAIL"], env["EP"]
    IT = NG // US
    PLAN = Plan("join 222 turn_z 287 copy_z 297 turn_a 374 copy_a 431 message 537 relu 579 sum 656 copy 708 "
                "ends 790")
    PE_, ACT_, DVE_ = Steps("turn_z turn_a message sum"), Steps("copy_z relu copy"), Steps("join copy_a ends")

    def wide(ap):
        return ap.rearrange("p (k d) -> p k d", d=P)

    def B(j, k):
        return buf[j][:, k, :]

    def ps(j):
        return psum[:, j, 0:GW]

    with ExitStack() as ctx:
        sem = phase_semaphores(nc, ctx, f"_{level}")

        def slots(name):
            return [sem(f"{name}{j}") for j in range(US)]

        match_in, rows_in, more_in, sums_out = (slots(n) for n in ("match_in", "edge_rows_in", "more_in", "sums_out"))
        pe_s, act_s, dve_s = (slots(n) for n in ("g_pe", "g_act", "g_dve"))
        idx_copied, ring_free = sem("lvl_idx"), sem("lvl_ring_free")
        block = ctx.enter_context(nc.Block())

        @block.sync
        def _(sp):
            def loads(it, j):
                g = US * it + j
                last = isinstance(it, int) and it == IT - 1 and j == US - 1
                sp.dma_start(B(j, 0), match_dram[bass.ds(g, 1)].rearrange("a p w -> (a p) w")).then_inc(match_in[j], 16)
                sp.dma_start(wide(B(j, 3)), edge_rows(dst_table, g)).then_inc(more_in[j], 16)
                sp.dma_start(wide(B(j, 4))[:, 0:G - 1, :],
                             edge_attr[bass.ds(g * GW, GW - P), :].rearrange("(k p) d -> p k d", p=P)
                             ).then_inc(more_in[j], 16)
                rows = TAIL if last else P
                sp.dma_start(B(j, 4)[0:rows, (G - 1) * P:GW],
                             edge_attr[bass.ds(g * GW + GW - P, rows), :]).then_inc(more_in[j], 16)

            for j in range(US):
                loads(0, j)

            def body(name, it, j):
                if name == "copy" and not (isinstance(it, int) and it == IT - 1):
                    sp.wait_ge(pe_s[j], PE_.at(it, "sum"))
                    loads(it + 1, j)
                if name == "ends":
                    sp.wait_ge(act_s[j], ACT_.at(it, "copy"))
                    sp.dma_start(sums_dram[bass.ds(US * it + j, 1)].rearrange("a p w -> (a p) w"), B(j, 2)
                                 ).then_inc(sums_out[j], 16)

            staggered(sp, IT, PLAN, body)
            for j in range(US):
                sp.wait_ge(sums_out[j], 16 * IT)

        @block.gpsimd
        def _(pool):
            def body(it):
                for j in range(US):
                    if not (isinstance(it, int) and it == 0):
                        pool.wait_ge(pe_s[j], PE_.at(it - 1, "turn_z"))
                        pool.sem_inc(ring_free, 1)
                    pool.tensor_copy(ring_idx[:, j, :], idx_lvl[:, bass.ds((US * it + j) * G, G)]
                                     ).then_inc(idx_copied, 1)
                    pool.wait_ge(idx_copied, US * it + j + 1)
                    pool.sem_inc(ring_free, 1)
                    for k in range(G):
                        pool.indirect_dma_start(
                            out=B(j, 1)[:, k * P:(k + 1) * P], out_offset=None, in_=table,
                            in_offset=bass.IndirectOffsetOnAxis(ap=ring_idx[:, j, k:k + 1], axis=0),
                        ).then_inc(rows_in[j], 16)

            body(0)
            with pool.Fori(1, IT) as it:
                body(it)

        @block.tensor
        def _(pe):
            def body(name, it, j):
                mm = None
                if name == "turn_z":
                    pe.wait_ge(dve_s[j], DVE_.at(it, "join"))
                    wait(pe, act_s[j], it * ACT_.n)
                    for k in range(G):
                        mm = pe.transpose(ps(j)[:, k * P:(k + 1) * P], B(j, 1)[:, k * P:(k + 1) * P], ident[:, :])
                elif name == "turn_a":
                    pe.wait_ge(act_s[j], ACT_.at(it, "copy_z"))
                    for k in range(G):
                        mm = pe.transpose(ps(j)[:, k * P:(k + 1) * P], B(j, 4)[:, k * P:(k + 1) * P], ident[:, :])
                elif name == "message":
                    pe.wait_ge(dve_s[j], DVE_.at(it, "copy_a"))
                    for k in range(G):
                        o, at = ps(j)[:, k * P:(k + 1) * P], slice(k * P, (k + 1) * P)
                        pe.matmul(o, B(j, 5)[:, at], w_use[:, 0, :], start=True, stop=False)
                        pe.matmul(o, extra[:, j, at], w_use[:, 1, :], start=False, stop=False)
                        mm = pe.matmul(o, ones3[:, :], bias3[:, 0, :], start=False, stop=True)
                elif name == "sum":
                    pe.wait_ge(match_in[j], 16 * it + 16)
                    pe.wait_ge(act_s[j], ACT_.at(it, "relu"))
                    for k in range(G):
                        at = slice(k * P, (k + 1) * P)
                        mm = pe.matmul(ps(j)[:, at], B(j, 5)[:, at], B(j, 0)[:, at], start=True, stop=True)
                if mm is not None:
                    mm.then_inc(pe_s[j], 1)

            staggered(pe, IT, PLAN, body)

        @block.vector
        def _(dve):
            def body(name, it, j):
                if name == "join":
                    dve.wait_ge(rows_in[j], 16 * G * it + 16 * G)
                    dve.wait_ge(more_in[j], 48 * it + 48)
                    dve.tensor_tensor(B(j, 1), B(j, 1), B(j, 3), ALU.add).then_inc(dve_s[j], 1)
                elif name == "copy_a":
                    dve.wait_ge(pe_s[j], PE_.at(it, "turn_a"))
                    dve.tensor_copy(extra[:, j, :], ps(j)).then_inc(dve_s[j], 1)
                elif name == "ends":
                    dve.wait_ge(act_s[j], ACT_.at(it, "copy"))
                    dve.tensor_copy(ends[:, bass.ds((US * it + j) * G, G), :], wide(B(j, 2))[:, :, 0:P:P - 1]
                                    ).then_inc(dve_s[j], 1)

            staggered(dve, IT, PLAN, body)

        @block.scalar
        def _(act):
            def body(name, it, j):
                if name == "copy_z":
                    act.wait_ge(pe_s[j], PE_.at(it, "turn_z"))
                    act.copy(B(j, 5), ps(j)).then_inc(act_s[j], 1)
                elif name == "relu":
                    act.wait_ge(pe_s[j], PE_.at(it, "message"))
                    act.activation(B(j, 5), ps(j), ACT.Relu).then_inc(act_s[j], 1)
                elif name == "copy":
                    act.wait_ge(pe_s[j], PE_.at(it, "sum"))
                    wait(act, sums_out[j], 16 * it)
                    wait(act, dve_s[j], it * DVE_.n)
                    act.copy(B(j, 2), ps(j)).then_inc(act_s[j], 1)

            staggered(act, IT, PLAN, body)


def carry_sums(nc, env, level):
    extra, psum, reach, ends, ident, center = (env[k] for k in ("extra", "psum", "reach", "ends", "ident", "center"))
    carry_dram, HB, ET = env["carry_dram"], env["HB"], env["ET"]
    with ExitStack() as ctx:
        sem = phase_semaphores(nc, ctx, f"_{level}")
        by_tile, turned, carried, split, carry_out = (
            sem(n) for n in ("by_tile", "ends_turned", "carried", "carry_split", "carry_out"))
        parts = ctx.enter_context(nc.sbuf_tensor(f"parts_{level}", [HB, 3, 4 * P], BF16))
        block = ctx.enter_context(nc.Block())
        rows = extra[0:HB, 0, 0:4 * P]
        rest = extra[0:HB, 1, 0:4 * P]

        @block.sync
        def _(sp):
            sp.wait_ge(split, 6)
            for k in range(3):
                for s in range(2):
                    sp.dma_start(carry_dram[3 * s + k:3 * s + k + 1, :].rearrange("a (b t d) -> (a t) b d", b=2, d=P),
                                 parts[:, k, s * 2 * P:(s + 1) * 2 * P].rearrange("t (b d) -> t b d", b=2)
                                 ).then_inc(carry_out, 16)
            sp.wait_ge(carry_out, 96)

        @block.tensor
        def _(pe):
            for s in range(2):
                for b in range(2):
                    mm = pe.matmul(psum[0:HB, 0, (2 * s + b) * P:(2 * s + b + 1) * P],
                                   ends[:, b * HB:(b + 1) * HB, 1 - s], center[:, :] if level in JOINED else ident[:, :],
                                   start=True, stop=True)
            mm.then_inc(turned, 1)
            pe.wait_ge(by_tile, 1)
            for s in range(2):
                for tb in range(2):
                    for b in range(2):
                        mm = pe.matmul(psum[0:HB, 1, (2 * s + tb) * P:(2 * s + tb + 1) * P],
                                       reach[:, s, b, tb * HB:(tb + 1) * HB],
                                       rows[:, (2 * s + b) * P:(2 * s + b + 1) * P], start=(b == 0), stop=(b == 1))
            mm.then_inc(carried, 1)

        @block.vector
        def _(dve):
            dve.wait_ge(turned, 1)
            dve.tensor_copy(rows, psum[0:HB, 0, 0:4 * P]).then_inc(by_tile, 1)
            dve.wait_ge(carried, 1)
            for k in range(3):
                left = psum[0:HB, 1, 0:4 * P] if k == 0 else rest
                if k:
                    dve.wait_ge(split, 2 * k)
                dve.tensor_copy(parts[:, k, :], left).then_inc(split, 1)
                dve.wait_ge(split, 2 * k + 1)
                dve.tensor_tensor(rest, left, parts[:, k, :], ALU.subtract).then_inc(split, 1)


def update_rows(nc, env, level, dst_tables):
    buf, carry_in, psum, small, cols = (env[k] for k in ("buf", "carry_in", "psum", "small", "cols"))
    ident, center, w_use, eps_t, extra = (env[k] for k in ("ident", "center", "w_use", "eps_t", "extra"))
    ones3, bias3, sums_dram, carry_dram = (env[k] for k in ("ones3", "bias3", "sums_dram", "carry_dram"))
    ends_mask, edge_rows, NG, N = env["ends_mask"], env["edge_rows"], env["NG"], env["N"]
    idx_out, ring_out, out = env["idx_out"], env["ring_idx"], env["out"]
    IT = NG // US
    LNA = lambda k: f"square{k} log{k} root{k}"
    PLAN, PE_, ACT_, DVE_, RESULT, RESULT_AT = [
        ("turn_r 0 gather 50 centre1 208 square1 285 sum1 338 root1 428 norm1 479 turn1 544 exp1 557 "
         "affine1 618 fold1 702 elu1 758 turn_y 909 rows_y 960",
         "turn_r centre1 turn1 turn_y", f"{LNA(1)} exp1 affine1 rows_y", "gather sum1 norm1 fold1", 5, "rows_y"),
        ("turn_r 33 gather 104 turn_x 147 copy_x 169 centre1 259 square1 297 sum1 342 root1 385 norm1 390 "
         "turn1 416 exp1 430 affine1 560 elu1 675 join 781 centre3 856 square3 904 sum3 936 root3 947 "
         "norm3 1032",
         "turn_r turn_x centre1 turn1 centre3", f"copy_x {LNA(1)} exp1 affine1 {LNA(3)}",
         "gather sum1 norm1 elu1 sum3 norm3", 3, "norm1"),
        ("carry 51 gather 108 turn_x 325 join 411 centre1 709 square1 750 sum1 791 root1 874 norm1 941",
         "carry turn_x centre1", LNA(1), "gather join sum1 norm1", 3, "norm1"),
        ("carry 9 gather 83 turn_x 128 copy_x 251 hidden 335 relu 527 turn_h 656 rows_h 838",
         "carry turn_x hidden turn_h", "copy_x relu rows_h", "gather", 5, "rows_h"),
        ("carry 11 gather 120 turn_x 289 copy_x 443 sage 589 add 706 square4 875 sum4 913 root4 920 norm4 936",
         "carry turn_x sage", f"copy_x {LNA(4)}", "gather add sum4 norm4", 5, "norm4"),
        ("turn_r 0 gather 28 centre1 63 square1 126 sum1 155 root1 191 norm1 208",
         "turn_r centre1", LNA(1), "gather sum1 norm1", 3, "norm1"),
    ][level]
    PLAN, PE_, ACT_, DVE_ = Plan(PLAN), Steps(PE_), Steps(ACT_), Steps(DVE_)
    POOL_ = Steps("join" if level == 1 else "elu1")
    joined = level in JOINED
    by_act = level in (0, 3)
    last_step = PLAN.names[-1]

    def B(j, k):
        return buf[j][:, k, :]

    def sums_in(j):
        return extra[:, j, :]

    def ps(j):
        return psum[:, j, 0:GW]

    def wide(ap):
        return ap.rearrange("p (k d) -> p k d", d=P)

    with ExitStack() as ctx:
        sem = phase_semaphores(nc, ctx, f"_{level}")

        def slots(name):
            return [sem(f"{name}{j}") for j in range(US)]

        sums_got, rows_got, second_got, stored = (slots(n) for n in ("sums_got", "rows_got", "second_got", "stored"))
        pe_s, act_s, dve_s = (slots(n) for n in ("u_pe", "u_act", "u_dve"))
        pool_s, carry_got, carry_used = slots("u_pool"), slots("carry_got"), sem("carry_used")
        idx_ready, rows_final = sem("idx_ready"), sem("rows_final")
        STORES = 16 * G if level == 5 else 16
        second = [ctx.enter_context(nc.sbuf_tensor(f"second{level}_{j}", [P, GW], F32)) for j in range(US)] \
            if level in (1, 4) else None
        block = ctx.enter_context(nc.Block())

        @block.sync
        def _(sp):
            def load_sums(it, j):
                g = US * it + j
                sp.dma_start(sums_in(j), sums_dram[bass.ds(g, 1)].rearrange("a p w -> (a p) w")).then_inc(sums_got[j], 16)

            def load_carry(it, j):
                g = US * it + j
                sp.dma_start(carry_in[j][:, 0, :], carry_dram[:, bass.ds(g * GW, GW)]).then_inc(carry_got[j], 16)
                sp.dma_start(carry_in[j][:, 1, :], ends_mask[:, bass.ds(g * GW, GW)]).then_inc(carry_got[j], 16)

            def load_rows(it, j):
                sp.dma_start(wide(B(j, 0)), edge_rows(dst_tables[3 if level == 4 else level], US * it + j)
                             ).then_inc(rows_got[j], 16)

            def load_second(it, j):
                if second:
                    sp.dma_start(wide(second[j][:, :]), edge_rows(dst_tables[0 if level == 1 else 4], US * it + j)
                                 ).then_inc(second_got[j], 16)

            for j in range(US):
                load_sums(0, j)
                load_carry(0, j)
                load_rows(0, j)
                load_second(0, j)

            def body(name, it, j):
                last = isinstance(it, int) and it == IT - 1
                if not last:
                    if name == "gather":
                        sp.wait_ge(dve_s[j], DVE_.at(it, "gather"))
                        load_sums(it + 1, j)
                        if joined:
                            load_rows(it + 1, j)
                    if name == ("centre1" if joined else "carry"):
                        sp.wait_ge(pe_s[j], PE_.at(it, name))
                        sp.sem_inc(carry_used, 1)
                        load_carry(it + 1, j)
                    if name == "join" and level == 2:
                        sp.wait_ge(dve_s[j], DVE_.at(it, "join"))
                        load_rows(it + 1, j)
                    if name == "copy_x":
                        sp.wait_ge(act_s[j], ACT_.at(it, "copy_x"))
                        load_second(it + 1, j)
                        if level == 3:
                            load_rows(it + 1, j)
                    if name == "add":
                        sp.wait_ge(dve_s[j], DVE_.at(it, "add"))
                        load_rows(it + 1, j)
                if level < 5 and name == last_step:
                    if by_act:
                        sp.wait_ge(act_s[j], it * ACT_.n + ACT_.n)
                    else:
                        sp.wait_ge(dve_s[j], it * DVE_.n + DVE_.n)
                    sp.dma_start(edge_rows(dst_tables[level + 1], US * it + j), wide(B(j, RESULT))
                                 ).then_inc(stored[j], 16)

            staggered(sp, IT, PLAN, body)
            if level < 5:
                for j in range(US):
                    sp.wait_ge(stored[j], 16 * IT)

        if level < 2:
            @block.gpsimd
            def _(pool):
                def body(name, it, j):
                    if name == "elu1" and level == 0:
                        pool.wait_ge(act_s[j], ACT_.at(it, "affine1"))
                        pool.wait_ge(dve_s[j], DVE_.at(it, "fold1"))
                        pool.sem_inc(idx_ready, 1)
                        pool.tensor_tensor(B(j, 4), B(j, 2), B(j, 3), ALU.add).then_inc(pool_s[j], 1)
                    elif name == "join":
                        pool.wait_ge(dve_s[j], DVE_.at(it, "elu1"))
                        pool.sem_inc(idx_ready, 1)
                        pool.tensor_tensor(B(j, 4), B(j, 4), B(j, 5), ALU.add).then_inc(pool_s[j], 1)

                staggered(pool, IT, PLAN, body)

        if level == 5:
            @block.gpsimd
            def _(pool):
                def body(it):
                    for j in range(US):
                        if not (isinstance(it, int) and it == 0):
                            pool.wait_ge(stored[j], STORES * it)
                            pool.sem_inc(rows_final, 1)
                        pool.tensor_copy(ring_out[:, j, :], idx_out[:, bass.ds((US * it + j) * G, G)]
                                         ).then_inc(idx_ready, 1)
                        pool.wait_ge(idx_ready, US * it + j + 1)
                        pool.wait_ge(dve_s[j], it * DVE_.n + DVE_.n)
                        pool.sem_inc(rows_final, 1)
                        for k in range(G):
                            pool.indirect_dma_start(
                                out=out, out_offset=bass.IndirectOffsetOnAxis(ap=ring_out[:, j, k:k + 1], axis=0),
                                in_=B(j, 3)[:, k * P:(k + 1) * P], in_offset=None,
                                bounds_check=N - 1, oob_is_err=False).then_inc(stored[j], 16)

                body(0)
                with pool.Fori(1, IT) as it:
                    body(it)
                for j in range(US):
                    pool.wait_ge(stored[j], STORES * IT)

        @block.tensor
        def _(pe):
            I, C = ident[:, :], center[:, :]

            def each_tile(j, terms, bias=False):
                for t in range(G):
                    at = slice(t * P, (t + 1) * P)
                    for n, (a, b) in enumerate(terms):
                        mm = pe.matmul(ps(j)[:, at], a[:, at], b if b.shape[-1] == P else b[:, at], start=(n == 0),
                                       stop=(n == len(terms) - 1 and not bias))
                    if bias:
                        mm = pe.matmul(ps(j)[:, at], ones3[:, :], bias3[:, 1, :], start=False, stop=True)
                return mm

            def turn(j, rows):
                for t in range(G):
                    at = slice(t * P, (t + 1) * P)
                    mm = pe.transpose(ps(j)[:, at], rows[:, at], I)
                return mm

            def body(name, it, j):
                mm = None
                if name in ("carry", "turn_r"):
                    if by_act:
                        wait(pe, act_s[j], it * ACT_.n)
                    else:
                        wait(pe, dve_s[j], it * DVE_.n)
                    if joined:
                        pe.wait_ge(rows_got[j], 16 * it + 16)
                        mm = turn(j, B(j, 0))
                    else:
                        pe.wait_ge(carry_got[j], 32 * it + 32)
                        mm = each_tile(j, [(carry_in[j][:, 0, :], carry_in[j][:, 1, :])])
                elif name == "turn_x":
                    pe.wait_ge(dve_s[j], DVE_.at(it, "gather"))
                    pe.wait_ge((second_got if second else rows_got)[j], 16 * it + 16)
                    mm = turn(j, second[j][:, :] if second else B(j, 0))
                elif name == "centre1":
                    if level == 1:
                        pe.wait_ge(act_s[j], ACT_.at(it, "copy_x"))
                    else:
                        pe.wait_ge(dve_s[j], DVE_.at(it, "join" if level == 2 else "gather"))
                    if joined:
                        pe.wait_ge(carry_got[j], 32 * it + 32)
                    mm = each_tile(j, [(B(j, 1), C)] + [(carry_in[j][:, 1, :], carry_in[j][:, 0, :])] * joined)
                elif name == "turn1":
                    pe.wait_ge(dve_s[j], DVE_.at(it, "norm1"))
                    mm = turn(j, B(j, 3))
                elif name == "turn_y":
                    pe.wait_ge(pool_s[j], POOL_.at(it, "elu1"))
                    mm = turn(j, B(j, 4))
                elif name == "centre3":
                    pe.wait_ge(pool_s[j], POOL_.at(it, "join"))
                    mm = each_tile(j, [(B(j, 4), C)])
                elif name == "hidden":
                    pe.wait_ge(act_s[j], ACT_.at(it, "copy_x"))
                    for lo, hi in ((0, 512), (512, GW)):
                        pe.matmul(ps(j)[:, lo:hi], w_use[:, 2, :], B(j, 1)[:, lo:hi], start=True, stop=False)
                        mm = pe.matmul(ps(j)[:, lo:hi], w_use[:, 3, :], B(j, 4)[:, lo:hi], start=False, stop=True)
                elif name == "turn_h":
                    pe.wait_ge(act_s[j], ACT_.at(it, "relu"))
                    mm = turn(j, B(j, 3))
                elif name == "sage":
                    pe.wait_ge(act_s[j], ACT_.at(it, "copy_x"))
                    mm = each_tile(j, [(B(j, 1), w_use[:, 4, :]), (B(j, 4), w_use[:, 5, :])], bias=True)
                if mm is not None:
                    mm.then_inc(pe_s[j], 1)

            staggered(pe, IT, PLAN, body)

        @block.scalar
        def _(act):
            affine = dict(bias=cols[:, 2 + level:3 + level], scale=cols[:, level:level + 1])

            def body(name, it, j):
                k = name[-1]

                def step(ins):
                    ins.then_inc(act_s[j], 1)

                if name == "copy_x":
                    act.wait_ge(pe_s[j], PE_.at(it, "turn_x"))
                    step(act.copy(B(j, 5 if level == 1 else 1), ps(j)))
                elif name in ("square1", "square3"):
                    act.wait_ge(pe_s[j], PE_.at(it, "centre" + k))
                    step(act.activation(B(j, 2), ps(j), ACT.Square))
                elif name == "square4":
                    act.wait_ge(dve_s[j], DVE_.at(it, "add"))
                    step(act.activation(B(j, 2), B(j, 4), ACT.Square))
                elif name.startswith("root"):
                    act.wait_ge(dve_s[j], DVE_.at(it, "sum" + k))
                    step(act.activation(small[:, j, 1, :], small[:, j, 0, :], ACT.Ln, bias=eps_t[:, 0:1],
                                        scale=1.0 / P))
                    act.wait_ge(act_s[j], ACT_.at(it, "log" + k))
                    step(act.activation(small[:, j, 2, :], small[:, j, 1, :], ACT.Exp, scale=-0.5))
                elif name == "exp1":
                    act.wait_ge(pe_s[j], PE_.at(it, "turn1"))
                    step(act.activation(B(j, 2), ps(j), ACT.Exp, **affine))
                elif name == "affine1":
                    step(act.activation(B(j, 3), ps(j), ACT.Relu, **affine))
                elif name == "relu":
                    act.wait_ge(pe_s[j], PE_.at(it, "hidden"))
                    step(act.activation(B(j, 3), ps(j), ACT.Relu, bias=cols[:, 4:5]))
                elif name in ("rows_y", "rows_h"):
                    act.wait_ge(pe_s[j], PE_.at(it, "turn_" + name[-1]))
                    wait(act, stored[j], STORES * it)
                    step(act.copy(B(j, 5), ps(j)))

            staggered(act, IT, PLAN, body)

        @block.vector
        def _(dve):
            def body(name, it, j):
                k = name[-1]

                def step(ins):
                    ins.then_inc(dve_s[j], 1)

                if name == RESULT_AT:
                    wait(dve, stored[j], STORES * it)
                if name == "gather":
                    dve.wait_ge(sums_got[j], 16 * it + 16)
                    dve.wait_ge(pe_s[j], PE_.at(it, "turn_r" if joined else "carry"))
                    step(dve.tensor_tensor(B(j, 1 if joined else 4), ps(j), sums_in(j), ALU.add))
                elif name == "join" and level == 2:
                    dve.wait_ge(pe_s[j], PE_.at(it, "turn_x"))
                    step(dve.scalar_tensor_tensor(out=B(j, 1), in0=B(j, 4), scalar=0.0, in1=ps(j), op0=ALU.max,
                                                  op1=ALU.add))
                elif name.startswith("sum"):
                    dve.wait_ge(act_s[j], ACT_.at(it, "square" + k))
                    step(dve.tensor_reduce(small[:, j, 0, :], wide(B(j, 2)), AX_X, ALU.add))
                elif name.startswith("norm"):
                    dve.wait_ge(act_s[j], ACT_.at(it, "root" + k))
                    rows, o = (B(j, 4), 5) if k == "4" else (ps(j), 3)
                    step(dve.tensor_tensor(wide(B(j, o)), wide(rows),
                                           small[:, j, 2, :].unsqueeze(2).to_broadcast([P, G, P]), ALU.mult))
                elif name == "fold1":
                    dve.wait_ge(act_s[j], ACT_.at(it, "exp1"))
                    step(dve.tensor_scalar(B(j, 2), B(j, 2), -1.0, 0.0, ALU.add, ALU.min))
                elif name == "elu1" and level == 1:
                    dve.wait_ge(act_s[j], ACT_.at(it, "affine1"))
                    step(dve.scalar_tensor_tensor(out=B(j, 4), in0=B(j, 2), scalar=1.0, in1=B(j, 3), op0=ALU.min,
                                                  op1=ALU.add))
                elif name == "add":
                    dve.wait_ge(pe_s[j], PE_.at(it, "sage"))
                    dve.wait_ge(rows_got[j], 16 * it + 16)
                    step(dve.tensor_tensor(B(j, 4), ps(j), B(j, 0), ALU.add))

            staggered(dve, IT, PLAN, body)


_INS = ["x", "src", "dst", "edge_attr_128", "edge_weight", "L0_gnn_ln_gamma", "L0_gnn_ln_beta", "L1_gnn_W_obj",
        "L1_gnn_b_obj", "L1_gnn_W_rel", "L1_gnn_b_rel", "L2_gnn_W1_self", "L2_gnn_W1_neigh", "L2_gnn_b1",
        "L2_gnn_W2_self", "L2_gnn_W2_neigh", "L2_gnn_b2"]


def build(nc, shapes):
    args = [nc.dram_tensor(f"in_{n}_dram", s, d, kind="ExternalInput").ap() for n, s, d in shapes]
    out = nc.dram_tensor("out_0_dram", shapes[0][1], F32, kind="ExternalOutput").ap()
    gnn_kernel(nc, *args, out)


def kernel(**inputs):
    import numpy as _np
    import concourse.bacc as _bacc
    from concourse.bass_utils import run_bass_kernel_spmd as _run

    nc = _bacc.Bacc("TRN2", target_bir_lowering=False, num_devices=1)
    arrays, shapes = {}, []
    for name in _INS:
        a = _np.ascontiguousarray(inputs[name])
        arrays[f"in_{name}_dram"] = a
        shapes.append((name, a.shape, mybir.dt.from_np(a.dtype)))
    build(nc, shapes)
    r = _run(nc, [arrays], core_ids=[0])
    return r.results[0]["out_0_dram"]
```
